# Optimizing a Trainium2 kernel written in Bass

```python
import numpy as np
import jax
import jax.numpy as jnp

def _softmax(x, axis=-1):
    return jax.nn.softmax(x, axis=axis)

def _gelu(x):
    return jax.nn.gelu(x, approximate=True)

def _silu(x):
    return jax.nn.silu(x)

def _sigmoid(x):
    return jax.nn.sigmoid(x)

def _layernorm(x, axis=-1, eps=1e-05):
    m = jnp.mean(x, axis=axis, keepdims=True)
    v = jnp.var(x, axis=axis, keepdims=True)
    return (x - m) / jnp.sqrt(v + eps)

def _scatter_add(tgt, idx, src, axis=0):
    return tgt.at[idx].add(src)

def _segment_sum(src, seg, n):
    return jax.ops.segment_sum(src, seg, n)
kernel_name = 'mk_gnn_preln_d2_gnn_r8_3e6b62'

def setup_inputs(seed: int=0):
    np.random.seed(seed)
    _w = jnp.asarray

    def _rec_inputs():
        import jax
        import jax.numpy as jnp
        _gk = jax.random.key(seed)
        x = -0.000202 + 1 * jax.random.normal(jax.random.fold_in(_gk, 1), (6250, 128), jnp.float32)
        _s = jax.random.randint(jax.random.fold_in(_gk, 2), (50000,), 0, 6250, jnp.int32)
        _d = jax.random.randint(jax.random.fold_in(_gk, 3), (50000,), 0, 6250, jnp.int32)
        _loop = jnp.arange(6250, dtype=jnp.int32)
        src = jnp.concatenate([_s, _d, _loop])
        dst = jnp.concatenate([_d, _s, _loop])
        _o = jnp.argsort(dst, stable=True)
        src = src[_o]
        dst = dst[_o]
        edge_attr_128 = -4.21973e-05 + 0.999841 * jax.random.normal(jax.random.fold_in(_gk, 11), (106250, 128), jnp.float32)
        return (x, src, dst, edge_attr_128)
    x, src, dst, edge_attr_128 = _rec_inputs()

    def _L0_gnn_setup():
        import jax, jax.numpy as jnp
        import numpy as np
        HIDDEN = 128
        N_NODES = 6250
        N_EDGES = 75000
        EPS = 1e-05

        def _linear_params(key, fan_in, fan_out):
            kw, kb = jax.random.split(key)
            bound = 1.0 / np.sqrt(fan_in)
            W = jax.random.uniform(kw, (fan_in, fan_out), jnp.float32, -bound, bound)
            b = jax.random.uniform(kb, (fan_out,), jnp.float32, -bound, bound)
            return (W, b)

        def _mlp2(x, W1, b1, W2, b2):
            h = jax.nn.silu(x @ W1 + b1)
            return h @ W2 + b2

        def _layernorm(x, gamma, beta):
            mu = jnp.mean(x, axis=-1, keepdims=True)
            var = jnp.mean(jnp.square(x - mu), axis=-1, keepdims=True)
            return (x - mu) * jax.lax.rsqrt(var + EPS) * gamma + beta
        key = jax.random.key(seed)
        ks = jax.random.split(key, 8)
        h_node = jax.random.normal(ks[0], (N_NODES, HIDDEN), jnp.float32)
        h_edge = jax.random.normal(ks[1], (N_EDGES, HIDDEN), jnp.float32)
        edge_index = jax.random.randint(ks[2], (2, N_EDGES), 0, N_NODES, jnp.int64 if jax.config.jax_enable_x64 else jnp.int32)
        msg_W1, msg_b1 = _linear_params(ks[3], 3 * HIDDEN, HIDDEN)
        msg_W2, msg_b2 = _linear_params(ks[4], HIDDEN, HIDDEN)
        upd_W1, upd_b1 = _linear_params(ks[5], 2 * HIDDEN, HIDDEN)
        upd_W2, upd_b2 = _linear_params(ks[6], HIDDEN, HIDDEN)
        ln_gamma = jnp.ones((HIDDEN,), jnp.float32)
        ln_beta = jnp.zeros((HIDDEN,), jnp.float32)
        return {'h_node': h_node, 'h_edge': h_edge, 'edge_index': edge_index, 'msg_W1': msg_W1, 'msg_b1': msg_b1, 'msg_W2': msg_W2, 'msg_b2': msg_b2, 'upd_W1': upd_W1, 'upd_b1': upd_b1, 'upd_W2': upd_W2, 'upd_b2': upd_b2, 'ln_gamma': ln_gamma, 'ln_beta': ln_beta}
    _L0_gnn_all = _L0_gnn_setup()
    _L0_gnn_in = {k: v for k, v in _L0_gnn_all.items() if k in ('msg_W1', 'msg_b1', 'msg_W2', 'msg_b2', 'upd_W1', 'upd_b1', 'upd_W2', 'upd_b2', 'ln_gamma', 'ln_beta')}
    del _L0_gnn_all

    def _L1_gnn_setup():
        import jax, jax.numpy as jnp
        import numpy as np
        N, E, F_IN, F_OUT = (6250, 200000, 128, 128)
        ALPHA = 0.2
        key = jax.random.key(seed)
        k1, k2, k3, k4 = jax.random.split(key, 4)
        h = jax.random.normal(k1, (N, F_IN), dtype=jnp.float32)
        edge_index = jax.random.randint(k2, (2, E), 0, N, dtype=jnp.int32)
        gain = 1.414
        std_W = gain * np.sqrt(2.0 / (F_IN + F_OUT))
        std_a = gain * np.sqrt(2.0 / (1 + 2 * F_OUT))
        W = std_W * jax.random.normal(k3, (F_IN, F_OUT), dtype=jnp.float32)
        a = std_a * jax.random.normal(k4, (1, 2 * F_OUT), dtype=jnp.float32)
        return {'h': h, 'edge_index': edge_index, 'W': W, 'a': a}
    _L1_gnn_all = _L1_gnn_setup()
    _L1_gnn_in = {k: v for k, v in _L1_gnn_all.items() if k in ('W', 'a')}
    del _L1_gnn_all
    return {'x': x, 'src': src, 'dst': dst, 'edge_attr_128': edge_attr_128, 'L0_gnn_msg_W1': _L0_gnn_in['msg_W1'], 'L0_gnn_msg_b1': _L0_gnn_in['msg_b1'], 'L0_gnn_msg_W2': _L0_gnn_in['msg_W2'], 'L0_gnn_msg_b2': _L0_gnn_in['msg_b2'], 'L0_gnn_upd_W1': _L0_gnn_in['upd_W1'], 'L0_gnn_upd_b1': _L0_gnn_in['upd_b1'], 'L0_gnn_upd_W2': _L0_gnn_in['upd_W2'], 'L0_gnn_upd_b2': _L0_gnn_in['upd_b2'], 'L0_gnn_ln_gamma': _L0_gnn_in['ln_gamma'], 'L0_gnn_ln_beta': _L0_gnn_in['ln_beta'], 'L1_gnn_W': _L1_gnn_in['W'], 'L1_gnn_a': _L1_gnn_in['a']}

def reference(x, src, dst, edge_attr_128, L0_gnn_msg_W1, L0_gnn_msg_b1, L0_gnn_msg_W2, L0_gnn_msg_b2, L0_gnn_upd_W1, L0_gnn_upd_b1, L0_gnn_upd_W2, L0_gnn_upd_b2, L0_gnn_ln_gamma, L0_gnn_ln_beta, L1_gnn_W, L1_gnn_a):
    import jax
    import jax.numpy as jnp

    def _L0_gnn_ref(h_node, h_edge, edge_index, msg_W1, msg_b1, msg_W2, msg_b2, upd_W1, upd_b1, upd_W2, upd_b2, ln_gamma, ln_beta):
        import jax, jax.numpy as jnp
        import numpy as np
        HIDDEN = 128
        N_NODES = 6250
        N_EDGES = 75000
        EPS = 1e-05

        def _linear_params(key, fan_in, fan_out):
            kw, kb = jax.random.split(key)
            bound = 1.0 / np.sqrt(fan_in)
            W = jax.random.uniform(kw, (fan_in, fan_out), jnp.float32, -bound, bound)
            b = jax.random.uniform(kb, (fan_out,), jnp.float32, -bound, bound)
            return (W, b)

        def _mlp2(x, W1, b1, W2, b2):
            h = jax.nn.silu(x @ W1 + b1)
            return h @ W2 + b2

        def _layernorm(x, gamma, beta):
            mu = jnp.mean(x, axis=-1, keepdims=True)
            var = jnp.mean(jnp.square(x - mu), axis=-1, keepdims=True)
            return (x - mu) * jax.lax.rsqrt(var + EPS) * gamma + beta
        src, dst = (edge_index[0], edge_index[1])
        m_in = jnp.concatenate([h_node[src], h_node[dst], h_edge], axis=-1)
        m = _mlp2(m_in, msg_W1, msg_b1, msg_W2, msg_b2)
        agg = jax.ops.segment_sum(m, dst, num_segments=h_node.shape[0])
        h_new = _mlp2(jnp.concatenate([h_node, agg], axis=-1), upd_W1, upd_b1, upd_W2, upd_b2)
        return _layernorm(h_node + h_new, ln_gamma, ln_beta)

    def _L1_gnn_ref(h, edge_index, W, a):
        import jax, jax.numpy as jnp
        import numpy as np
        N, E, F_IN, F_OUT = (6250, 200000, 128, 128)
        ALPHA = 0.2
        n = h.shape[0]
        row, col = (edge_index[0], edge_index[1])
        Wh = h @ W
        a_src, a_dst = (a[0, :F_OUT], a[0, F_OUT:])
        score = Wh[row] @ a_src + Wh[col] @ a_dst
        edge_e = jnp.exp(-jax.nn.leaky_relu(score, negative_slope=ALPHA))
        e_rowsum = jax.ops.segment_sum(edge_e, row, num_segments=n)
        h_prime = jax.ops.segment_sum(edge_e[:, None] * Wh[col], row, num_segments=n)
        h_prime = h_prime / e_rowsum[:, None]
        return jax.nn.elu(h_prime)
    edge_index = jnp.stack([src, dst])
    h = jnp.maximum(_layernorm(x, axis=-1), 0.0)
    x = x + _L0_gnn_ref(h, edge_attr_128, edge_index, L0_gnn_msg_W1, L0_gnn_msg_b1, L0_gnn_msg_W2, L0_gnn_msg_b2, L0_gnn_upd_W1, L0_gnn_upd_b1, L0_gnn_upd_W2, L0_gnn_upd_b2, L0_gnn_ln_gamma, L0_gnn_ln_beta)
    h = jnp.maximum(_layernorm(x, axis=-1), 0.0)
    x = x + _L1_gnn_ref(h, edge_index, L1_gnn_W, L1_gnn_a)
    return x

_drawn_inputs = setup_inputs


def setup_inputs(seed=0):
    import zlib

    import numpy as np

    out = dict(_drawn_inputs(seed))
    spreads = {'L0_gnn_ln_gamma': (1.0, 0.2), 'L0_gnn_ln_beta': (0.0, 0.1)}
    factors = {'L0_gnn_msg_b1': 2.981, 'L0_gnn_upd_b1': 5.09}
    for name, (base, spread) in spreads.items():
        noise = np.random.default_rng([zlib.crc32(name.encode()), seed]).standard_normal(out[name].shape)
        drawn = base * np.exp(spread * noise) if base else spread * noise
        out[name] = jnp.asarray(drawn.astype(out[name].dtype))
    for name, factor in factors.items():
        out[name] = (out[name] * factor).astype(out[name].dtype)
    return out
```

```python
import concourse.bass as bass
from concourse import mybir
from concourse.alu_op_type import AluOpType as ALU
from contextlib import ExitStack
from collections import namedtuple

N, E, H = 6250, 106250, 128
P = 128
GROUP = 1024
G = -(-E // GROUP)
SUB = GROUP // P
HALF = GROUP // 2
HS = SUB // 2
NH = 2 * G
NT = 50
ROWS = NT * P
CT = 5
CW = CT * P
NC = NT // CT
DUMP = N + 1
NACC = 4
AW = H + 1
WW = H + 2
EPS = 1e-5
ALPHA = 0.2

F32, BF16, I32 = mybir.dt.float32, mybir.dt.bfloat16, mybir.dt.int32
ACT = mybir.ActivationFunctionType
X = mybir.AxisListType.X


def wait(eng, sem, value):
    if isinstance(value, int) and value <= 0:
        return
    eng.wait_ge(sem, value)


def passed(eng, sem):
    eng.sem_inc(sem, 1)


def cols(tensor, start, size):
    if isinstance(start, int):
        return tensor[:, start:start + size]
    return tensor[:, bass.ds(start, size)]


def rows(table, start, size):
    if isinstance(start, int):
        return table[start:start + size]
    return table[bass.ds(start, size)]


def wide(column, shape):
    return column.unsqueeze(2).broadcast_to(shape)


def over_tiles(row, shape):
    return row.unsqueeze(1).broadcast_to(shape)


class Chain:

    def __init__(self, eng, sem, start=0):
        self.eng, self.sem, self.start, self.n = eng, sem, start, 0

    def did(self, instruction):
        self.n += 1
        instruction.then_inc(self.sem, 1)
        return self.n

    def after(self, n=None):
        wait(self.eng, self.sem, self.start + (self.n if n is None else n))

    def then(self, instruction):
        self.did(instruction)
        self.after()


def turns(eng, count, body):
    body(0)
    with eng.Fori(1, count - 1) as i:
        body(i)
    body(count - 1)


def named(kind, things):
    return namedtuple(kind, list(things))(**things)


def signals(nc, ctx, phase, names):
    found, free = {}, []

    def clear(*_):
        nc.clear_and_free_semaphores(free)
        nc.all_engine_barrier(sem_only=True)
    ctx.callback(clear)
    for name in names.split():
        name, _, n = name.partition("*")
        if n:
            found[name] = [nc.alloc_semaphore(f"{phase}_{name}{k}") for k in range(int(n))]
        else:
            found[name] = nc.alloc_semaphore(f"{phase}_{name}")
        free += found[name] if n else [found[name]]
    return named("Signals", found)


def buffers(nc, ctx, phase, **shapes):
    found = {}
    for name, (shape, dtype, *n) in shapes.items():
        made = [ctx.enter_context(nc.sbuf_tensor(f"{phase}_{name}{k}", shape, dtype)) for k in range(n[0] if n else 1)]
        found[name] = made if n else made[0]
    return named("Buffers", found)


def tiles(ap, width=H):
    return ap.rearrange("p (t f) -> p t f", f=width)


def prepare(nc, d, m, ps):
    with ExitStack() as ctx:
        s = signals(nc, ctx, "prep", "ids_in weights_in vectors_in iotas consts own rows_ready rows_out tr_ps tr_evac bc_ps bc_used"
                    " span_ps flag_ready zeros_ready acc_zeroed l1wT_ps l1wT wa_ps")
        b = buffers(nc, ctx, "prep", dst_g=([G, GROUP], I32), src_g=([G, GROUP], I32), hi_i=([G, GROUP], I32),
                    lo_i=([G, GROUP], I32), dst_f=([G, GROUP], F32), src_f=([G, GROUP], F32), hi_f=([G, GROUP], F32),
                    rel_f=([G, GROUP], F32), rows3=([G, 3 * GROUP], BF16), first=([G, 1], F32), last=([G, 1], F32),
                    span=([G, 1], F32), iota_n_i=([P, P], I32), iota_p_i=([P, 1], I32), iota_node=([P, NT], I32), node_f=([P, NT], F32), span_row=([1, G], F32),
                    vec=([1, 8 * H], F32), l1w=([P, H], F32), l1wT=([P, H], F32), acol=([P, 2], F32), widest=([1, 1], F32),
                    zeros=([P, ROWS * AW // P // 2], F32))
        VEC = ["b1", "b2", "ub1", "ub2", "gamma", "beta"]
        block = ctx.enter_context(nc.Block())

        @block.sync
        def _(sp):
            sp.dma_start(b.dst_g[:, :], d.dst.rearrange("(g e) -> g e", e=GROUP)).then_inc(s.ids_in, 16)
            sp.dma_start(b.src_g[:, :], d.src.rearrange("(g e) -> g e", e=GROUP)).then_inc(s.ids_in, 16)
            for t in range(3):
                sp.dma_start(m.w1[:, t * H:(t + 1) * H], d.w1[t * H:(t + 1) * H, :]).then_inc(s.weights_in, 16)
            for t in range(2):
                sp.dma_start(m.u1[:, t * H:(t + 1) * H], d.u1[t * H:(t + 1) * H, :]).then_inc(s.weights_in, 16)
            sp.dma_start(m.w2[:, :], d.w2).then_inc(s.weights_in, 16)
            sp.dma_start(m.u2[:, :], d.u2).then_inc(s.weights_in, 16)
            sp.dma_start(b.l1w[:, :], d.l1w).then_inc(s.weights_in, 16)
            for n, name in enumerate(VEC):
                v = {"b1": d.b1, "b2": d.b2, "ub1": d.ub1, "ub2": d.ub2, "gamma": d.gamma, "beta": d.beta}[name]
                sp.dma_start(b.vec[:, n * H:(n + 1) * H], v.rearrange("(o f) -> o f", o=1)).then_inc(s.vectors_in, 16)
            sp.dma_start(b.vec[:, 6 * H:8 * H], d.a).then_inc(s.vectors_in, 16)
            sp.wait_ge(s.zeros_ready, 1)
            for acc in d.acc:
                halves = acc.rearrange("(p r) c -> p (r c)", p=P)
                half = ROWS * AW // P // 2
                for n in range(2):
                    sp.dma_start(halves[:, n * half:(n + 1) * half], b.zeros[:, :]).then_inc(s.acc_zeroed, 16)
            sp.wait_ge(s.rows_ready, 3)
            sp.dma_start(d.edge_rows.rearrange("g r e -> g (r e)"), b.rows3[:, :]).then_inc(s.rows_out, 16)
            sp.wait_ge(s.rows_out, 16)
            sp.wait_ge(s.weights_in, 16 * 8)
            sp.wait_ge(s.acc_zeroed, 16 * 2 * len(d.acc))

        @block.gpsimd
        def _(pool):
            pool.iota(b.iota_n_i[:, :], [[1, P]], base=0, channel_multiplier=0).then_inc(s.iotas, 1)
            pool.iota(b.iota_p_i[:, :], [[0, 1]], base=0, channel_multiplier=1).then_inc(s.iotas, 1)
            pool.iota(b.iota_node[:, :], [[P, NT]], base=0, channel_multiplier=1).then_inc(s.iotas, 1)
            pool.memset(b.zeros[:, :], 0.0).then_inc(s.zeros_ready, 1)

        @block.vector
        def _(dve):
            own = Chain(dve, s.own)
            own.did(dve.memset(m.aggT[:, :], 0.0))
            own.did(dve.memset(m.degree[:, :], 0.0))
            own.did(dve.memset(m.ones_row[:, :], 1.0))
            own.did(dve.memset(m.ones_bf[:, :], 1.0))
            dve.wait_ge(s.iotas, 3)
            own.then(dve.tensor_copy(b.node_f[:, :], b.iota_node[:, :]))
            own.did(dve.tensor_scalar(m.no_node[:, :], b.node_f[:, :], float(N), None, ALU.is_ge))
            own.then(dve.tensor_copy(m.iota_n[:, :], b.iota_n_i[:, :]))
            own.then(dve.tensor_copy(m.iota_p[:, :], b.iota_p_i[:, :]))
            own.did(dve.tensor_scalar(m.before[:, :], m.iota_n[:, :], m.iota_p[:, :], None, ALU.is_lt))
            own.did(dve.tensor_scalar(m.ident[:, :], m.iota_n[:, :], m.iota_p[:, :], None, ALU.is_equal))
            for n in range(3):
                own.did(dve.tensor_scalar(m.pick[0:3, n * P:(n + 1) * P], m.iota_p[0:3, :].broadcast_to([3, P]), float(n), None, ALU.is_equal))
            own.after()
            own.then(dve.scalar_tensor_tensor(m.pick[0:3, 3 * P:4 * P], m.pick[0:3, 0:P], float(P), m.pick[0:3, P:2 * P], ALU.mult, ALU.add))
            dve.tensor_scalar(m.dump[:, :], m.iota_p[:, :], float(DUMP), None, ALU.add).then_inc(s.consts, 1)
            dve.wait_ge(s.ids_in, 32)
            own.did(dve.tensor_copy(b.dst_f[:, :], b.dst_g[:, :]))
            own.did(dve.tensor_copy(b.src_f[:, :], b.src_g[:, :]))
            own.did(dve.tensor_single_scalar(b.hi_i[:, :], b.src_g[:, :], 7, ALU.logical_shift_right))
            own.then(dve.tensor_single_scalar(b.lo_i[:, :], b.src_g[:, :], P - 1, ALU.bitwise_and))
            own.did(dve.tensor_copy(b.hi_f[:, :], b.hi_i[:, :]))
            own.did(dve.tensor_reduce(b.first[:, :], b.dst_f[:, :], X, ALU.min))
            own.then(dve.tensor_reduce(b.last[:, :], b.dst_f[:, :], X, ALU.max))
            own.did(dve.tensor_tensor(b.span[:, :], b.last[:, :], b.first[:, :], ALU.subtract))
            own.then(dve.tensor_scalar(b.rel_f[:, :], b.dst_f[:, :], b.first[:, :], None, ALU.subtract))
            dve.tensor_copy(b.rows3[:, 0:GROUP], b.hi_i[:, :]).then_inc(s.rows_ready, 1)
            dve.tensor_copy(b.rows3[:, GROUP:2 * GROUP], b.lo_i[:, :]).then_inc(s.rows_ready, 1)
            dve.tensor_copy(b.rows3[:, 2 * GROUP:], b.rel_f[:, :]).then_inc(s.rows_ready, 1)
            for q, col in enumerate((m.src_c, m.hi_c, m.dst_c, m.rel_c)):
                dve.wait_ge(s.tr_ps, 2 * q + 2)
                for half in range(2):
                    got = ps[:, 2 * q + half, 0:HS * G].rearrange("p (j g) -> p j g", g=G)
                    ins = dve.tensor_copy(col[:, :].rearrange("p (g j) -> p j g", j=SUB)[:, half * HS:(half + 1) * HS, :], got)
                    ins.then_inc(s.tr_evac, 1)
            dve.wait_ge(s.tr_evac, 8)
            own.did(dve.tensor_copy(m.src_i[:, :], m.src_c[:, :]))
            own.did(dve.tensor_copy(m.dst_i[:, :], m.dst_c[:, :]))
            dve.wait_ge(s.bc_ps, 1)
            own.did(dve.tensor_copy(m.b1_all[:, :], ps[:, 0, 0:H]))
            own.did(dve.tensor_copy(m.gamma_all[:, :], ps[:, 0, H:2 * H]))
            own.did(dve.tensor_copy(m.beta_all[:, :], ps[:, 0, 2 * H:3 * H]))
            own.did(dve.tensor_copy(m.ub1_col[:, :], ps[:, 1, 0:1]))
            own.did(dve.tensor_copy(b.acol[:, :], ps[:, 1, 1:3]))
            own.did(dve.tensor_copy(m.b2_row[:, :], b.vec[:, H:2 * H]))
            own.did(dve.tensor_copy(m.ub2_row[:, :], b.vec[:, 3 * H:4 * H]))
            own.did(dve.tensor_copy(b.l1wT[:, :], ps[:, 2, 0:H]))
            own.did(dve.tensor_copy(m.first_row[:, :], ps[0:1, 3, 0:G]))
            own.after()
            dve.tensor_copy(b.span_row[:, :], ps[0:1, 3, G:2 * G]).then_inc(s.bc_used, 1)
            dve.wait_ge(s.bc_used, 1)
            own.then(dve.tensor_reduce(b.widest[:, :], b.span_row[:, :], X, ALU.max))
            own.did(dve.tensor_scalar(m.fits[:, :], b.widest[:, :], float(P), None, ALU.is_lt))
            own.did(dve.tensor_copy(m.l1wx[:, 0:H], b.l1w[:, :]))
            dve.wait_ge(s.wa_ps, 1)
            own.did(dve.tensor_copy(m.l1wx[:, H:H + 1], ps[:, 4, 1:2]))
            own.did(dve.tensor_copy(m.l1wx[:, H + 1:H + 2], ps[:, 4, 0:1]))
            own.after()

        @block.tensor
        def _(pe):
            pe.wait_ge(s.consts, 1)
            pe.wait_ge(s.rows_ready, 3)
            for q, f in enumerate((b.src_f, b.hi_f, b.dst_f, b.rel_f)):
                for j in range(SUB):
                    out = ps[:, 2 * q + j // HS, (j % HS) * G:(j % HS + 1) * G]
                    ins = pe.transpose(out, f[:, j * P:(j + 1) * P], m.ident[0:G, 0:G])
                    if j % HS == HS - 1:
                        ins.then_inc(s.tr_ps, 1)
            pe.wait_ge(s.tr_evac, 8)
            pe.wait_ge(s.vectors_in, 16 * 7)
            pe.wait_ge(s.weights_in, 16 * 8)
            for n, v in enumerate((0, 4, 5)):
                pe.matmul(ps[:, 0, n * H:(n + 1) * H], m.ones_row[:, :], b.vec[:, v * H:(v + 1) * H], start=True, stop=True)
            for n, v in enumerate((2, 6, 7)):
                pe.matmul(ps[:, 1, n:n + 1], b.vec[:, v * H:(v + 1) * H], m.ones_row[:, 0:1], start=True, stop=True)
            pe.transpose(ps[:, 2, 0:H], b.l1w[:, :], m.ident[:, :])
            pe.transpose(ps[0:1, 3, 0:G], b.first[:, :], m.ident[0:G, 0:G])
            pe.transpose(ps[0:1, 3, G:2 * G], b.span[:, :], m.ident[0:G, 0:G]).then_inc(s.bc_ps, 1)
            pe.wait_ge(s.bc_used, 1)
            pe.matmul(ps[:, 4, 0:2], b.l1wT[:, :], b.acol[:, :], start=True, stop=True).then_inc(s.wa_ps, 1)


NORM = "summed meaned centred squared spread deviated rooted inverted scaled"


def norm_buffers(nc, ctx, phase):
    return buffers(nc, ctx, phase, total=([P, CT], F32, 2), mean=([P, CT], F32, 2), sq_total=([P, CT], F32, 2),
                   var=([P, CT], F32, 2), dev=([P, CT], F32, 2), inv=([P, CT], F32, 2), xc=([P, CW], F32, 2),
                   xn=([P, CW], F32, 2))


def norm_centre(dve, s, b, k, u, x):
    dve.tensor_reduce(b.total[u][:, :], tiles(x), X, ALU.add).then_inc(s.summed, 1)
    wait(dve, s.summed, k + 1)
    dve.tensor_scalar(b.mean[u][:, :], b.total[u][:, :], 1.0 / H, None, ALU.mult).then_inc(s.meaned, 1)
    wait(dve, s.meaned, k + 1)
    wait(dve, s.scaled, k - 1)
    dve.tensor_tensor(tiles(b.xc[u][:, :]), tiles(x), wide(b.mean[u][:, :], [P, CT, H]), ALU.subtract).then_inc(s.centred, 1)


def norm_square(act, s, b, k, u, used):
    wait(act, s.centred, k + 1)
    wait(act, used, k - 1)
    act.activation(b.xn[u][:, :], b.xc[u][:, :], ACT.Square).then_inc(s.squared, 1)


def norm_variance(dve, s, b, k, u):
    wait(dve, s.squared, k + 1)
    dve.tensor_reduce(b.sq_total[u][:, :], tiles(b.xn[u][:, :]), X, ALU.add).then_inc(s.spread, 1)
    wait(dve, s.spread, k + 1)
    dve.tensor_scalar(b.var[u][:, :], b.sq_total[u][:, :], 1.0 / H, EPS, ALU.mult, ALU.add).then_inc(s.deviated, 1)


def norm_root(act, s, b, k, u):
    wait(act, s.deviated, k + 1)
    act.activation(b.dev[u][:, :], b.var[u][:, :], ACT.Sqrt).then_inc(s.rooted, 1)


def norm_scale(dve, s, b, k, u):
    wait(dve, s.rooted, k + 1)
    dve.reciprocal(b.inv[u][:, :], b.dev[u][:, :]).then_inc(s.inverted, 1)
    wait(dve, s.inverted, k + 1)
    dve.tensor_tensor(tiles(b.xn[u][:, :]), tiles(b.xc[u][:, :]), wide(b.inv[u][:, :], [P, CT, H]), ALU.mult).then_inc(s.scaled, 1)


def split_three(dve, s, k, x, high, mid, low, rest):
    dve.tensor_copy(high, x).then_inc(s.high, 1)
    wait(dve, s.high, k + 1)
    dve.tensor_tensor(rest, x, high, ALU.subtract).then_inc(s.rest, 1)
    wait(dve, s.rest, k + 1)
    dve.tensor_copy(mid, rest).then_inc(s.mid, 1)
    wait(dve, s.mid, k + 1)
    dve.tensor_tensor(low, rest, mid, ALU.subtract).then_inc(s.low, 1)


def chunk_rows(table, k):
    return rows(table, k * CW, CW).rearrange("(t p) f -> p t f", p=P)


def turn_pairs(eng, body):
    turns(eng, NC // 2, body)


def node_pass_one(nc, d, m, ps):
    with ExitStack() as ctx:
        s = signals(nc, ctx, "n1", NORM + " x_in*2 relued h_kept hT_ps hT_moved hT_kept pq_ps p_moved q_made high rest mid low p_out*2 q_out*2 qs_out*2")
        nb = norm_buffers(nc, ctx, "n1")
        b = buffers(nc, ctx, "n1", x=([P, CW], F32, 2), h=([P, CW], F32, 2), hT=([P, CW], F32, 2), p=([P, CW], F32, 2),
                    q=([P, CW], F32, 2), rest=([P, CW], F32, 2), qs=([P, 3 * CW], BF16, 2))
        hT_ps = [ps[:, 0:2, :].rearrange("p b c -> p (b c)"), ps[:, 2:4, :].rearrange("p b c -> p (b c)")]
        pq_ps = ps[:, 4:7, :].rearrange("p b c -> p (b c)")
        block = ctx.enter_context(nc.Block())

        @block.sync
        def _(sp):
            def turn(i):
                for u in range(2):
                    k = 2 * i + u
                    wait(sp, s.centred, k - 1)
                    sp.dma_start(tiles(b.x[u][:, :]), chunk_rows(d.x, k)).then_inc(s.x_in[u], 16)
                for u in range(2):
                    k = 2 * i + u
                    wait(sp, s.p_moved, k + 1)
                    sp.dma_start(chunk_rows(d.p_table, k), tiles(b.p[u][:, :])).then_inc(s.p_out[u], 16)
                    wait(sp, s.q_made, k + 1)
                    sp.dma_start(chunk_rows(d.q_table, k), tiles(b.q[u][:, :])).then_inc(s.q_out[u], 16)
                    wait(sp, s.low, k + 1)
                    sp.dma_start(chunk_rows(d.q_split, k), tiles(b.qs[u][:, :], 3 * H)).then_inc(s.qs_out[u], 16)
            turn_pairs(sp, turn)
            for u in range(2):
                sp.wait_ge(s.p_out[u], 16 * NC // 2)
                sp.wait_ge(s.q_out[u], 16 * NC // 2)
                sp.wait_ge(s.qs_out[u], 16 * NC // 2)

        @block.vector
        def _(dve):
            def turn(i):
                for u in range(2):
                    wait(dve, s.x_in[u], 16 * (i + 1))
                    norm_centre(dve, s, nb, 2 * i + u, u, b.x[u][:, :])
                for u in range(2):
                    norm_variance(dve, s, nb, 2 * i + u, u)
                for u in range(2):
                    norm_scale(dve, s, nb, 2 * i + u, u)
                for u in range(2):
                    k = 2 * i + u
                    wait(dve, s.pq_ps, k + 1)
                    wait(dve, s.q_out[u], 16 * i)
                    wait(dve, s.low, k - 1)
                    dve.tensor_tensor(tiles(b.q[u][:, :]), tiles(pq_ps[:, 0:2 * CW], 2 * H)[:, :, H:],
                                      over_tiles(m.b1_all[:, :], [P, CT, H]), ALU.add).then_inc(s.q_made, 1)
                    wait(dve, s.q_made, k + 1)
                    wait(dve, s.qs_out[u], 16 * i)
                    parts = tiles(b.qs[u][:, :], 3 * H)
                    split_three(dve, s, k, tiles(b.q[u][:, :]), parts[:, :, 0:H], parts[:, :, H:2 * H], parts[:, :, 2 * H:], tiles(b.rest[u][:, :]))
            turn_pairs(dve, turn)

        @block.scalar
        def _(act):
            def turn(i):
                for u in range(2):
                    norm_square(act, s, nb, 2 * i + u, u, s.relued)
                for u in range(2):
                    norm_root(act, s, nb, 2 * i + u, u)
                for u in range(2):
                    k = 2 * i + u
                    wait(act, s.scaled, k + 1)
                    wait(act, s.hT_ps, k - 1)
                    wait(act, s.h_kept, k - 1)
                    act.activation(b.h[u][:, :], nb.xn[u][:, :], ACT.Relu).then_inc(s.relued, 1)
                for u in range(2):
                    k = 2 * i + u
                    wait(act, s.hT_ps, k + 1)
                    wait(act, s.pq_ps, k - 1)
                    wait(act, s.hT_kept, k - 1)
                    act.activation(b.hT[u][:, :], hT_ps[u][:, 0:CW], ACT.Copy).then_inc(s.hT_moved, 1)
                for u in range(2):
                    k = 2 * i + u
                    wait(act, s.q_made, k + 1)
                    wait(act, s.p_out[u], 16 * i)
                    act.activation(tiles(b.p[u][:, :]), tiles(pq_ps[:, 0:2 * CW], 2 * H)[:, :, 0:H], ACT.Copy).then_inc(s.p_moved, 1)
            turn_pairs(act, turn)

        @block.gpsimd
        def _(pool):
            def turn(i):
                for u in range(2):
                    k = 2 * i + u
                    wait(pool, s.relued, k + 1)
                    pool.tensor_copy(cols(m.h, k * CW, CW), b.h[u][:, :]).then_inc(s.h_kept, 1)
                for u in range(2):
                    k = 2 * i + u
                    wait(pool, s.hT_moved, k + 1)
                    pool.tensor_copy(cols(m.hT, k * CW, CW), b.hT[u][:, :]).then_inc(s.hT_kept, 1)
            turn_pairs(pool, turn)

        @block.tensor
        def _(pe):
            def turn(i):
                for u in range(2):
                    k = 2 * i + u
                    wait(pe, s.relued, k + 1)
                    wait(pe, s.hT_moved, k - 1)
                    for t in range(CT):
                        ins = pe.transpose(hT_ps[u][:, t * P:(t + 1) * P], b.h[u][:, t * H:(t + 1) * H], m.ident[:, :])
                    ins.then_inc(s.hT_ps, 1)
                for u in range(2):
                    k = 2 * i + u
                    wait(pe, s.hT_moved, k + 1)
                    wait(pe, s.p_moved, k)
                    for t in range(CT):
                        ins = pe.matmul(pq_ps[:, t * 2 * H:(t + 1) * 2 * H], b.hT[u][:, t * P:(t + 1) * P], m.w1[:, 0:2 * H], start=True, stop=True)
                    ins.then_inc(s.pq_ps, 1)
            turn_pairs(pe, turn)


def edges_one_fast(nc, d, m, ps, s, b):
    rel_ps = ps[:, 0, :]
    z_ps = [ps[:, 2, :], ps[:, 3, :]]
    src_ps = ps[:, 4, :]
    agg_ps = [ps[:, 5, 0:P], ps[:, 6, 0:P]]
    deg_ps = [ps[0:1, 1, 0:P], ps[0:1, 7, 0:P]]

    def sync(sp):
        def turn(i):
            for u in range(2):
                g = 2 * i + u
                wait(sp, s.z_ps, 2 * (g - 1))
                wait(sp, s.src_ps, 2 * (g - 1))
                sp.dma_start(b.rows3[u][:, :], rows(d.edge_rows, g, 1).rearrange("o r e -> (o r) e")).then_inc(s.rows_in[u], 16)
                sp.dma_start(b.attr[u][:, :], rows(d.attrT, g, 1).rearrange("o f e -> (o f) e")).then_inc(s.attr_in[u], 16)
                first = sp.value_load(cols(m.first_row, g, 1), min_val=0, max_val=N)
                sp.dma_start(b.window[u][:, :], rows(d.q_split, first, P)).then_inc(s.window_in[u], 16)
        turns(sp, G // 2, turn)

    def gpsimd(pool):
        pool.tensor_copy(b.idx[0][:, :], m.src_i[:, 0:SUB]).then_inc(s.idx_ready, 1)

        def group(g, u, i, last):
            pool.wait_ge(s.idx_ready, g + 1)
            wait(pool, s.z_ready, 2 * (g - 1))
            passed(pool, s.passed)
            for j in range(SUB):
                pool.indirect_dma_start(b.gathered[u][:, j * H:(j + 1) * H], None, d.p_table[:, :],
                                        bass.IndirectOffsetOnAxis(ap=b.idx[u][:, j:j + 1], axis=0)).then_inc(s.gathered[u], 16)
                if j == SUB - 2 and not last:
                    wait(pool, s.gathered[1 - u], 16 * SUB * (i + u))
                    pool.tensor_copy(b.idx[1 - u][:, :], cols(m.src_i, (g + 1) * SUB, SUB)).then_inc(s.idx_ready, 1)

        def turn(i):
            for u in range(2):
                group(2 * i + u, u, i, isinstance(i, int) and 2 * i + u == G - 1)
        turns(pool, G // 2, turn)

    def tensor(pe):
        def broadcast(h, u, w, i):
            if w == 0:
                wait(pe, s.rows_in[u], 16 * (i + 1))
            wait(pe, s.oneT_ready, h)
            pe.matmul(rel_ps, m.pick[0:3, 2 * P:3 * P], b.rows3[u][:, w * HALF:(w + 1) * HALF], start=True, stop=True).then_inc(s.rel_ps, 1)
            wait(pe, s.counted, HS * h)
            pe.matmul(src_ps, m.pick[0:3, 3 * P:4 * P], b.rows3[u][:, w * HALF:(w + 1) * HALF], start=True, stop=True).then_inc(s.src_ps, 1)

        def sums(h, v, u, w, g):
            wait(pe, s.silu_ready, h + 1)
            wait(pe, s.one_ready, h + 1)
            if w == 0:
                wait(pe, s.agg_added, g - 1)
            for j in range(HS):
                pe.matmul(agg_ps[u], b.silu[v][:, j * H:(j + 1) * H], b.one[v][:, j * P:(j + 1) * P],
                          start=(w == 0 and j == 0), stop=(w == 1 and j == HS - 1))
            for j in range(HS):
                upper = b.one[v][:, j * P:(j + 1) * P].bitcast(BF16)[:, 1::2]
                ins = pe.matmul(deg_ps[u], m.ones_bf[:, :], upper, start=(w == 0 and j == 0), stop=(w == 1 and j == HS - 1))
            ins.then_inc(s.agg_ps, 1)

        def turn(i):
            for q in range(4):
                h, u, w, v = 4 * i + q, q // 2, q % 2, q % 2
                if not (isinstance(i, int) and h == NH - 1):
                    broadcast(h + 1, (q + 1) // 2 % 2, 1 - w, i + (q + 1) // 4)
                if w == 0:
                    wait(pe, s.attr_in[u], 16 * (i + 1))
                    wait(pe, s.window_in[u], 16 * (i + 1))
                wait(pe, s.oneT_ready, h + 1)
                wait(pe, s.z_ready, h - 1)
                for j in range(HS):
                    e = (w * HS + j) * P
                    z = z_ps[v][:, j * H:(j + 1) * H]
                    pe.matmul(z, b.attr[u][:, e:e + P], m.w1[:, 2 * H:3 * H], start=True, stop=False)
                    for part in range(3):
                        ins = pe.matmul(z, b.oneT[v][:, j * P:(j + 1) * P], b.window[u][:, part * H:(part + 1) * H], start=False, stop=(part == 2))
                ins.then_inc(s.z_ps, 1)
                if not (isinstance(i, int) and h == 0):
                    sums(h - 1, 1 - v, (q - 1) // 2 % 2, 1 - w, 2 * i + (q - 1) // 2)
        broadcast(0, 0, 0, 0)
        turns(pe, G // 2, turn)
        sums(NH - 1, 1, 1, 1, G - 1)

    def scalar(act):
        def turn(i):
            for q in range(4):
                h, v = 4 * i + q, q % 2
                wait(act, s.z_ready, h + 1)
                wait(act, s.agg_ps, h - 1)
                act.activation(b.silu[v][:, :], b.z[v][:, :], ACT.Silu).then_inc(s.silu_ready, 1)
        turns(act, G // 2, turn)

    def vector(dve):
        def add_rows(h, v, u, w, i):
            wait(dve, s.z_ps, h + 1)
            if w == 0:
                wait(dve, s.gathered[u], 16 * SUB * (i + 1))
            wait(dve, s.silu_ready, h - 1)
            dve.tensor_tensor(b.z[v][:, :], z_ps[v], b.gathered[u][:, w * HS * H:(w + 1) * HS * H], ALU.add).then_inc(s.z_ready, 1)

        def add_sums(g, u):
            wait(dve, s.agg_ps, 2 * (g + 1))
            wait(dve, s.agg_added, g)
            wait(dve, s.deg_added, g)
            first = dve.value_load(cols(m.first_row, g, 1), min_val=0, max_val=N)
            dve.tensor_tensor(cols(m.degree, first, P), deg_ps[u], cols(m.degree, first, P), ALU.add).then_inc(s.deg_added, 1)
            wait(dve, s.deg_added, g + 1)
            dve.tensor_tensor(cols(m.aggT, first, P), agg_ps[u], cols(m.aggT, first, P), ALU.add).then_inc(s.agg_added, 1)

        def turn(i):
            for q in range(4):
                h, u, w, v = 4 * i + q, q // 2, q % 2, q % 2
                c = (2 * i + u) * SUB + w * HS
                wait(dve, s.rel_ps, h + 1)
                wait(dve, s.z_ps, h - 1)
                dve.tensor_scalar(b.oneT[v][:, :], rel_ps, m.iota_p[:, :], None, ALU.is_equal).then_inc(s.oneT_ready, 1)
                wait(dve, s.src_ps, h + 1)
                wait(dve, s.counted, HS * h)
                for j in range(HS):
                    dve.scalar_tensor_tensor(b.junk[:, j * P:(j + 1) * P], src_ps[:, j * P:(j + 1) * P], cols(m.src_c, c + j, 1),
                                             m.before[:, :], ALU.is_equal, ALU.mult, accum_out=cols(m.repeats, c + j, 1)).then_inc(s.counted, 1)
                wait(dve, s.agg_ps, h - 1)
                dve.tensor_tensor(tiles(b.one[v][:, :]), wide(cols(m.rel_c, c, HS), [P, HS, P]),
                                  over_tiles(m.iota_n[:, :], [P, HS, P]), ALU.is_equal).then_inc(s.one_ready, 1)
                if not (isinstance(i, int) and h == 0):
                    add_rows(h - 1, 1 - v, (q - 1) // 2 % 2, 1 - w, i + (q - 1) // 4)
                if w == 1 and not (isinstance(i, int) and h == 1):
                    add_sums(2 * i + u - 1, 1 - u)
        turns(dve, G // 2, turn)
        add_rows(NH - 1, 1, 1, 1, G // 2 - 1)
        add_sums(G - 1, 1)
        again, away = m.rel_c[:, :], m.dst_c[:, :]
        step = Chain(dve, s.rows_chosen)
        dve.wait_ge(s.counted, HS * NH)
        dve.wait_ge(s.one_ready, NH)
        step.did(dve.tensor_scalar(again, m.repeats[:, :], 0.0, None, ALU.is_gt))
        step.then(dve.tensor_scalar(away, m.src_c[:, :], -1.0, m.dump[:, :], ALU.mult, ALU.add))
        step.then(dve.tensor_tensor(away, away, again, ALU.mult))
        step.then(dve.tensor_tensor(again, away, m.src_c[:, :], ALU.add))
        step.then(dve.tensor_copy(m.to_i[:, :], again))
    return sync, gpsimd, tensor, scalar, vector


TAIL = 9


def each_tile(eng, body):
    with eng.Fori(0, G) as g:
        with eng.Fori(0, SUB) as j:
            body(g * SUB + j, g, j)


def combine_indices(dve, m, s, b, own, t, key_c):
    dve.wait_ge(s.key_in, 16 * (t + 1))
    own.then(dve.tensor_copy(b.key_f[:, :], b.key_i[:, :]))
    own.then(dve.tensor_scalar(b.same[:, :], b.key_f[:, :], cols(key_c, t, 1), None, ALU.is_equal))
    own.then(dve.tensor_tensor(b.earlier[:, :], b.same[:, :], m.before[:, :], ALU.mult))
    own.then(dve.tensor_reduce(b.repeat[:, :], b.earlier[:, :], X, ALU.add))
    own.then(dve.tensor_scalar(b.again[:, :], b.repeat[:, :], 0.0, None, ALU.is_gt))
    own.then(dve.tensor_tensor(b.away[:, :], m.dump[:, :], cols(key_c, t, 1), ALU.subtract))
    own.then(dve.tensor_tensor(b.away[:, :], b.away[:, :], b.again[:, :], ALU.mult))
    own.then(dve.tensor_tensor(b.to_f[:, :], b.away[:, :], cols(key_c, t, 1), ALU.add))
    own.then(dve.tensor_copy(b.to_i[:, :], b.to_f[:, :]))


def scatter_tile(pool, s, b, t, acc):
    pool.wait_ge(s.sums_moved, t + 1)
    passed(pool, s.passed)
    pool.indirect_dma_start(acc[:, :], bass.IndirectOffsetOnAxis(ap=b.to_i[:, 0:1], axis=0), b.sums[:, :], None,
                            compute_op=ALU.add).then_inc(s.added, 16)
    pool.wait_ge(s.added, 16 * (t + 1))


def general_buffers(nc, ctx, phase):
    return buffers(nc, ctx, phase, src_x=([P, 1], I32), dst_x=([P, 1], I32), key_i=([P, P], I32), key_f=([P, P], F32),
                   same=([P, P], F32), earlier=([P, P], F32), repeat=([P, 1], F32), again=([P, 1], F32), away=([P, 1], F32),
                   to_f=([P, 1], F32), to_i=([P, 1], I32), vals=([P, AW], F32), sums=([P, AW], F32), at_src=([P, WW], F32),
                   at_dst=([P, WW], F32), attr=([P, P], F32), z=([P, P], F32), score=([P, 1], F32), leaky=([P, 1], F32),
                   node_sums=([P, AW], F32))


GENERAL = "idx_ready rows_in key_in attr_in z_ps z_ready vals_ready own sums_ps sums_moved added node_in node_ps node_moved passed sp_passed"


def edges_one_general(nc, d, m, ps, s, b):
    acc = d.acc[NACC]
    STEPS = TAIL + 3

    def sync(sp):
        def tile(t, g, j):
            sp.dma_start(b.attr[:, :], d.attrT[bass.ds(g, 1), :, bass.ds(j * P, P)].rearrange("o f e -> (o f) e")).then_inc(s.attr_in, 16)
            sp.dma_start(b.key_i[:, :], rows(d.dst, t * P, P).partition_broadcast(P)).then_inc(s.key_in, 16)
            sp.wait_ge(s.added, 16 * (t + 1))
            passed(sp, s.sp_passed)
        each_tile(sp, tile)
        with sp.Fori(0, NT) as t:
            sp.dma_start(b.node_sums[:, :], rows(acc, t * P, P)).then_inc(s.node_in, 16)
            sp.wait_ge(s.node_moved, 2 * (t + 1))
            passed(sp, s.sp_passed)

    def gpsimd(pool):
        def tile(t, g, j):
            pool.tensor_copy(b.src_x[:, :], cols(m.src_i, t, 1)).then_inc(s.idx_ready, 1)
            pool.tensor_copy(b.dst_x[:, :], cols(m.dst_i, t, 1)).then_inc(s.idx_ready, 1)
            pool.wait_ge(s.idx_ready, 2 * (t + 1))
            passed(pool, s.passed)
            pool.indirect_dma_start(b.at_src[:, 0:H], None, d.p_table[:, :], bass.IndirectOffsetOnAxis(ap=b.src_x[:, 0:1], axis=0)).then_inc(s.rows_in, 16)
            pool.indirect_dma_start(b.at_dst[:, 0:H], None, d.q_table[:, :], bass.IndirectOffsetOnAxis(ap=b.dst_x[:, 0:1], axis=0)).then_inc(s.rows_in, 16)
            scatter_tile(pool, s, b, t, acc)
        each_tile(pool, tile)

    def tensor(pe):
        def tile(t, g, j):
            pe.wait_ge(s.attr_in, 16 * (t + 1))
            pe.matmul(ps[:, 0, 0:H], b.attr[:, :], m.w1[:, 2 * H:3 * H], start=True, stop=True).then_inc(s.z_ps, 1)
            pe.wait_ge(s.vals_ready, t + 1)
            pe.wait_ge(s.own, STEPS * (t + 1))
            pe.matmul(ps[:, 1, 0:AW], b.same[:, :], b.vals[:, :], start=True, stop=True).then_inc(s.sums_ps, 1)
            pe.wait_ge(s.added, 16 * (t + 1))
        each_tile(pe, tile)
        with pe.Fori(0, NT) as t:
            pe.wait_ge(s.node_in, 16 * (t + 1))
            pe.transpose(ps[:, 2, 0:P], b.node_sums[:, 0:H], m.ident[:, :])
            pe.transpose(ps[0:1, 3, 0:P], b.node_sums[:, H:AW], m.ident[:, :]).then_inc(s.node_ps, 1)
            pe.wait_ge(s.node_moved, 2 * (t + 1))

    def scalar(act):
        def tile(t, g, j):
            act.wait_ge(s.z_ready, t + 1)
            act.activation(b.vals[:, 0:H], b.z[:, :], ACT.Silu).then_inc(s.vals_ready, 1)
            act.wait_ge(s.added, 16 * (t + 1))
        each_tile(act, tile)

    def vector(dve):
        def tile(t, g, j):
            own = Chain(dve, s.own, STEPS * t)
            own.did(dve.memset(b.vals[:, H:AW], 1.0))
            dve.wait_ge(s.rows_in, 32 * (t + 1))
            own.then(dve.tensor_tensor(b.z[:, :], b.at_src[:, 0:H], b.at_dst[:, 0:H], ALU.add))
            dve.wait_ge(s.z_ps, t + 1)
            dve.tensor_tensor(b.z[:, :], b.z[:, :], ps[:, 0, 0:H], ALU.add).then_inc(s.z_ready, 1)
            combine_indices(dve, m, s, b, own, t, m.dst_c)
            own.then(dve.memset(b.away[:, :], 0.0))
            dve.wait_ge(s.sums_ps, t + 1)
            dve.tensor_copy(b.sums[:, :], ps[:, 1, 0:AW]).then_inc(s.sums_moved, 1)
            dve.wait_ge(s.added, 16 * (t + 1))
        each_tile(dve, tile)
        with dve.Fori(0, NT) as t:
            dve.wait_ge(s.node_ps, t + 1)
            dve.tensor_copy(cols(m.aggT, t * P, P), ps[:, 2, 0:P]).then_inc(s.node_moved, 1)
            dve.tensor_copy(cols(m.degree, t * P, P), ps[0:1, 3, 0:P]).then_inc(s.node_moved, 1)
            dve.wait_ge(s.node_moved, 2 * (t + 1))
    return sync, gpsimd, tensor, scalar, vector


def edges_two_general(nc, d, m, ps, s, b):
    acc = d.acc[0]
    STEPS = TAIL + 2

    def sync(sp):
        def tile(t, g, j):
            sp.dma_start(b.key_i[:, :], rows(d.src, t * P, P).partition_broadcast(P)).then_inc(s.key_in, 16)
            sp.wait_ge(s.added, 16 * (t + 1))
            passed(sp, s.sp_passed)
        each_tile(sp, tile)

    def gpsimd(pool):
        def tile(t, g, j):
            pool.tensor_copy(b.src_x[:, :], cols(m.src_i, t, 1)).then_inc(s.idx_ready, 1)
            pool.tensor_copy(b.dst_x[:, :], cols(m.dst_i, t, 1)).then_inc(s.idx_ready, 1)
            pool.wait_ge(s.idx_ready, 2 * (t + 1))
            passed(pool, s.passed)
            pool.indirect_dma_start(b.at_src[:, :], None, d.wh_table[:, :], bass.IndirectOffsetOnAxis(ap=b.src_x[:, 0:1], axis=0)).then_inc(s.rows_in, 16)
            pool.indirect_dma_start(b.at_dst[:, :], None, d.wh_table[:, :], bass.IndirectOffsetOnAxis(ap=b.dst_x[:, 0:1], axis=0)).then_inc(s.rows_in, 16)
            scatter_tile(pool, s, b, t, acc)
        each_tile(pool, tile)

    def tensor(pe):
        def tile(t, g, j):
            pe.wait_ge(s.z_ready, t + 1)
            pe.matmul(ps[:, 1, 0:AW], b.same[:, :], b.vals[:, :], start=True, stop=True).then_inc(s.sums_ps, 1)
            pe.wait_ge(s.added, 16 * (t + 1))
        each_tile(pe, tile)

    def scalar(act):
        def tile(t, g, j):
            act.wait_ge(s.own, STEPS * t + 2)
            act.activation(b.vals[:, H:AW], b.leaky[:, :], ACT.Exp, scale=-1.0).then_inc(s.vals_ready, 1)
            act.wait_ge(s.added, 16 * (t + 1))
        each_tile(act, tile)

    def vector(dve):
        def tile(t, g, j):
            own = Chain(dve, s.own, STEPS * t)
            dve.wait_ge(s.rows_in, 32 * (t + 1))
            own.then(dve.tensor_tensor(b.score[:, :], b.at_dst[:, H:H + 1], b.at_src[:, H + 1:H + 2], ALU.add))
            own.then(dve.scalar_tensor_tensor(b.leaky[:, :], b.score[:, :], ALPHA, b.score[:, :], ALU.mult, ALU.max))
            combine_indices(dve, m, s, b, own, t, m.src_c)
            dve.wait_ge(s.vals_ready, t + 1)
            dve.tensor_scalar(b.vals[:, 0:H], b.at_dst[:, 0:H], b.vals[:, H:AW], None, ALU.mult).then_inc(s.z_ready, 1)
            dve.wait_ge(s.sums_ps, t + 1)
            dve.tensor_copy(b.sums[:, :], ps[:, 1, 0:AW]).then_inc(s.sums_moved, 1)
            dve.wait_ge(s.added, 16 * (t + 1))
        each_tile(dve, tile)
    return sync, gpsimd, tensor, scalar, vector


def branch(nc, m, fast, general):
    with nc.Block() as block:
        def both(n):
            def program(eng):
                fits = eng.value_load(m.fits[0:1, 0:1], min_val=0, max_val=1)
                with eng.If(fits == 1):
                    fast[n](eng)
                with eng.Else():
                    general[n](eng)
            return program
        block.sync(both(0))
        block.gpsimd(both(1))
        block.tensor(both(2))
        block.scalar(both(3))
        block.vector(both(4))


def edges_one(nc, d, m, ps):
    with ExitStack() as ctx:
        s = signals(nc, ctx, "e1", "rows_in*2 attr_in*2 window_in*2 idx_ready gathered*2 rel_ps src_ps z_ps agg_ps oneT_ready counted"
                    " one_ready z_ready silu_ready deg_added agg_added rows_chosen passed")
        b = buffers(nc, ctx, "e1", rows3=([3, GROUP], BF16, 2), attr=([P, GROUP], F32, 2), window=([P, 3 * H], BF16, 2),
                    gathered=([P, SUB * H], F32, 2), idx=([P, SUB], I32, 2), oneT=([P, HALF], BF16, 2), one=([P, HALF], F32, 2),
                    z=([P, HALF], F32, 2), silu=([P, HALF], F32, 2), junk=([P, HALF], F32))
        sg = signals(nc, ctx, "e1g", GENERAL)
        bg = general_buffers(nc, ctx, "e1g")
        branch(nc, m, edges_one_fast(nc, d, m, ps, s, b), edges_one_general(nc, d, m, ps, sg, bg))


def node_pass_two(nc, d, m, ps):
    with ExitStack() as ctx:
        s = signals(nc, ctx, "n2", "x_in*2 agg_ps agg_moved pre_ps mid_ready new_ps y_ready gammaed betaed x1_ready x1_kept relued hT_ps hT_moved wh_ps"
                    " wh_moved high rest mid low score_kept wh_out*2 ws_out*2 own")
        sa, sb = signals(nc, ctx, "n2a", NORM), signals(nc, ctx, "n2b", NORM)
        na, nb = norm_buffers(nc, ctx, "n2a"), norm_buffers(nc, ctx, "n2b")
        b = buffers(nc, ctx, "n2", x=([P, CW], F32, 2), msg=([P, CW], F32, 2), mid=([P, CW], F32, 2), y=([P, CW], F32, 2), x1=([P, CW], F32, 2),
                    h=([P, CW], F32, 2), wh=([P, CT * WW], F32, 2), rest=([P, CT * AW], F32, 2),
                    ws=([P, 3 * CT * AW], BF16, 2))
        bank2 = [ps[:, 2 * n:2 * n + 2, :].rearrange("p b c -> p (b c)") for n in range(4)]
        one_ps, two_ps = bank2[0:2], bank2[2:4]
        slices = [(0, 512), (512, CW - 512)]
        where = [(t // 3) * 512 + (t % 3) * WW for t in range(CT)]
        block = ctx.enter_context(nc.Block())

        @block.sync
        def _(sp):
            def turn(i):
                for u in range(2):
                    k = 2 * i + u
                    wait(sp, s.x1_ready, k - 1)
                    sp.dma_start(tiles(b.x[u][:, :]), chunk_rows(d.x, k)).then_inc(s.x_in[u], 16)
                for u in range(2):
                    k = 2 * i + u
                    wait(sp, s.wh_moved, k + 1)
                    sp.dma_start(chunk_rows(d.wh_table, k), tiles(b.wh[u][:, :], WW)).then_inc(s.wh_out[u], 16)
                    wait(sp, s.low, k + 1)
                    sp.dma_start(chunk_rows(d.w_split, k), tiles(b.ws[u][:, :], 3 * AW)).then_inc(s.ws_out[u], 16)
            turn_pairs(sp, turn)
            for u in range(2):
                sp.wait_ge(s.wh_out[u], 16 * NC // 2)
                sp.wait_ge(s.ws_out[u], 16 * NC // 2)

        @block.tensor
        def _(pe):
            def turn(i):
                for u in range(2):
                    k = 2 * i + u
                    wait(pe, s.hT_moved, k - 1)
                    for c, n in slices:
                        pe.matmul(one_ps[u][:, c:c + n], m.w2[:, :], cols(m.aggT, k * CW + c, n), start=True, stop=False)
                        ins = pe.matmul(one_ps[u][:, c:c + n], m.b2_row[:, :], cols(m.degree, k * CW + c, n), start=False, stop=True)
                    ins.then_inc(s.agg_ps, 1)
                for u in range(2):
                    k = 2 * i + u
                    wait(pe, s.agg_moved, k + 1)
                    wait(pe, s.wh_moved, k - 1)
                    for c, n in slices:
                        pe.matmul(two_ps[u][:, c:c + n], m.u1[:, 0:H], cols(m.hT, k * CW + c, n), start=True, stop=False)
                        ins = pe.matmul(two_ps[u][:, c:c + n], m.u1[:, H:2 * H], b.msg[u][:, c:c + n], start=False, stop=True)
                    ins.then_inc(s.pre_ps, 1)
                for u in range(2):
                    k = 2 * i + u
                    wait(pe, s.mid_ready, k + 1)
                    for t in range(CT):
                        out = one_ps[u][:, t * H:(t + 1) * H]
                        pe.matmul(out, b.mid[u][:, t * P:(t + 1) * P], m.u2[:, :], start=True, stop=False)
                        ins = pe.matmul(out, m.ones_row[:, :], m.ub2_row[:, :], start=False, stop=True)
                    ins.then_inc(s.new_ps, 1)
                for u in range(2):
                    k = 2 * i + u
                    wait(pe, s.relued, k + 1)
                    for t in range(CT):
                        ins = pe.transpose(one_ps[u][:, t * P:(t + 1) * P], b.h[u][:, t * H:(t + 1) * H], m.ident[:, :])
                    ins.then_inc(s.hT_ps, 1)
                for u in range(2):
                    k = 2 * i + u
                    wait(pe, s.hT_moved, k + 1)
                    for t in range(CT):
                        ins = pe.matmul(two_ps[u][:, where[t]:where[t] + WW], b.mid[u][:, t * P:(t + 1) * P], m.l1wx[:, :], start=True, stop=True)
                    ins.then_inc(s.wh_ps, 1)
            turn_pairs(pe, turn)

        @block.scalar
        def _(act):
            def turn(i):
                for u in range(2):
                    k = 2 * i + u
                    wait(act, s.agg_ps, k + 1)
                    wait(act, s.pre_ps, k - 1)
                    act.activation(b.msg[u][:, :], one_ps[u][:, 0:CW], ACT.Copy).then_inc(s.agg_moved, 1)
                for u in range(2):
                    k = 2 * i + u
                    wait(act, s.pre_ps, k + 1)
                    wait(act, s.wh_ps, k - 1)
                    act.activation(b.mid[u][:, :], two_ps[u][:, 0:CW], ACT.Silu, bias=m.ub1_col[:, :]).then_inc(s.mid_ready, 1)
                for sn, bn, used in ((sa, na, s.x1_ready), (sb, nb, s.relued)):
                    for u in range(2):
                        norm_square(act, sn, bn, 2 * i + u, u, used)
                    for u in range(2):
                        norm_root(act, sn, bn, 2 * i + u, u)
                for u in range(2):
                    k = 2 * i + u
                    wait(act, sb.scaled, k + 1)
                    wait(act, s.hT_ps, k - 1)
                    act.activation(b.h[u][:, :], nb.xn[u][:, :], ACT.Relu).then_inc(s.relued, 1)
                for u in range(2):
                    k = 2 * i + u
                    wait(act, s.hT_ps, k + 1)
                    act.activation(b.mid[u][:, :], one_ps[u][:, 0:CW], ACT.Copy).then_inc(s.hT_moved, 1)
                for u in range(2):
                    k = 2 * i + u
                    wait(act, s.wh_ps, k + 1)
                    wait(act, s.wh_out[u], 16 * i)
                    wait(act, s.low, k - 1)
                    wait(act, s.score_kept, k - 1)
                    act.activation(tiles(b.wh[u][:, 0:3 * WW], WW), tiles(two_ps[u][:, 0:3 * WW], WW), ACT.Copy).then_inc(s.own, 1)
                    act.activation(tiles(b.wh[u][:, 3 * WW:], WW), tiles(two_ps[u][:, 512:512 + 2 * WW], WW), ACT.Copy).then_inc(s.own, 1)
                    wait(act, s.own, 2 * (k + 1))
                    act.nop().then_inc(s.wh_moved, 1)
            turn_pairs(act, turn)

        @block.gpsimd
        def _(pool):
            def turn(i):
                for u in range(2):
                    k = 2 * i + u
                    wait(pool, s.x1_ready, k + 1)
                    wait(pool, s.agg_ps, k + 1)
                    pool.tensor_copy(cols(m.aggT, k * CW, CW), b.x1[u][:, :]).then_inc(s.x1_kept, 1)
            turn_pairs(pool, turn)

        @block.vector
        def _(dve):
            def turn(i):
                for u in range(2):
                    k = 2 * i + u
                    wait(dve, s.new_ps, k + 1)
                    wait(dve, sa.centred, k - 1)
                    dve.tensor_tensor(b.y[u][:, :], one_ps[u][:, 0:CW], cols(m.h, k * CW, CW), ALU.add).then_inc(s.y_ready, 1)
                    wait(dve, s.y_ready, k + 1)
                    norm_centre(dve, sa, na, k, u, b.y[u][:, :])
                for u in range(2):
                    norm_variance(dve, sa, na, 2 * i + u, u)
                for u in range(2):
                    k = 2 * i + u
                    norm_scale(dve, sa, na, k, u)
                    wait(dve, sa.scaled, k + 1)
                    xn = na.xn[u][:, :]
                    dve.tensor_tensor(tiles(xn), tiles(xn), over_tiles(m.gamma_all[:, :], [P, CT, H]), ALU.mult).then_inc(s.gammaed, 1)
                    wait(dve, s.gammaed, k + 1)
                    dve.tensor_tensor(tiles(xn), tiles(xn), over_tiles(m.beta_all[:, :], [P, CT, H]), ALU.add).then_inc(s.betaed, 1)
                    wait(dve, s.betaed, k + 1)
                    wait(dve, s.x_in[u], 16 * (i + 1))
                    wait(dve, s.x1_kept, k - 1)
                    wait(dve, sb.centred, k - 1)
                    dve.tensor_tensor(b.x1[u][:, :], xn, b.x[u][:, :], ALU.add).then_inc(s.x1_ready, 1)
                    wait(dve, s.x1_ready, k + 1)
                    norm_centre(dve, sb, nb, k, u, b.x1[u][:, :])
                for u in range(2):
                    norm_variance(dve, sb, nb, 2 * i + u, u)
                for u in range(2):
                    norm_scale(dve, sb, nb, 2 * i + u, u)
                for u in range(2):
                    k = 2 * i + u
                    wait(dve, s.wh_moved, k + 1)
                    whole = tiles(b.wh[u][:, :], WW)
                    dve.tensor_copy(cols(m.s_src, k * CT, CT), whole[:, :, WW - 1]).then_inc(s.score_kept, 1)
                    wait(dve, s.ws_out[u], 16 * i)
                    parts = tiles(b.ws[u][:, :], 3 * AW)
                    split_three(dve, s, k, whole[:, :, 0:AW], parts[:, :, 0:AW], parts[:, :, AW:2 * AW], parts[:, :, 2 * AW:], tiles(b.rest[u][:, :], AW))
            turn_pairs(dve, turn)


def edges_two_fast(nc, d, m, ps, s, b):
    rel_ps, lo_ps, src_ps, score_ps = ps[:, 0, :], ps[:, 1, :], ps[:, 2, :], ps[:, 3, 0:HS * NT]
    wh_ps = [ps[:, 4, :], ps[:, 5, :]]
    sums_ps = ps[:, 6:8, 0:2 * AW]

    def sync(sp):
        def turn(i):
            for u in range(2):
                g = 2 * i + u
                wait(sp, s.wh_ps, 2 * (g - 1))
                wait(sp, s.src_ps, 2 * (g - 1))
                sp.dma_start(b.rows3[u][:, :], rows(d.edge_rows, g, 1).rearrange("o r e -> (o r) e")).then_inc(s.rows_in[u], 16)
                first = sp.value_load(cols(m.first_row, g, 1), min_val=0, max_val=N)
                sp.dma_start(b.window[u][:, :], rows(d.w_split, first, P)).then_inc(s.window_in[u], 16)
        turns(sp, G // 2, turn)

    def gpsimd(pool):
        pool.tensor_copy(b.idx[0][:, :], m.to_i[:, 0:SUB]).then_inc(s.idx_ready, 1)

        def turn(i):
            for u in range(2):
                g = 2 * i + u
                last = isinstance(i, int) and g == G - 1
                pool.wait_ge(s.idx_ready, g + 1)
                for j in range(SUB):
                    w, a = j // HS, j % HS
                    h = 2 * g + w
                    if a == 0:
                        pool.wait_ge(s.sums_moved, h + 1)
                    wait(pool, s.added[a], 16 * h)
                    passed(pool, s.passed)
                    pool.indirect_dma_start(d.acc[a][:, :], bass.IndirectOffsetOnAxis(ap=b.idx[u][:, j:j + 1], axis=0),
                                            b.sums[w][:, a * AW:(a + 1) * AW], None, compute_op=ALU.add).then_inc(s.added[a], 16)
                    if j == SUB - 2 and not last:
                        pool.tensor_copy(b.idx[1 - u][:, :], cols(m.to_i, (g + 1) * SUB, SUB)).then_inc(s.idx_ready, 1)
        turns(pool, G // 2, turn)
        for a in range(NACC):
            pool.wait_ge(s.added[a], 16 * NH)

    def tensor(pe):
        def broadcast(h, u, w, i):
            if w == 0:
                wait(pe, s.rows_in[u], 16 * (i + 1))
            half = b.rows3[u][:, w * HALF:(w + 1) * HALF]
            wait(pe, s.oneT_ready, h)
            pe.matmul(rel_ps, m.pick[0:3, 2 * P:3 * P], half, start=True, stop=True).then_inc(s.rel_ps, 1)
            wait(pe, s.loT_ready, h)
            pe.matmul(lo_ps, m.pick[0:3, P:2 * P], half, start=True, stop=True).then_inc(s.lo_ps, 1)
            wait(pe, s.same_ready, h)
            pe.matmul(src_ps, m.pick[0:3, 3 * P:4 * P], half, start=True, stop=True).then_inc(s.src_ps, 1)

        def combine(h, v):
            wait(pe, s.same_ready, h + 1)
            wait(pe, s.vals_ready, h + 1)
            wait(pe, s.sums_moved, h)
            for j in range(HS):
                ins = pe.matmul(sums_ps[:, j // 2, (j % 2) * AW:(j % 2 + 1) * AW], b.same[v][:, j * P:(j + 1) * P],
                                b.vals[v][:, j * AW:(j + 1) * AW], start=True, stop=True)
            ins.then_inc(s.sums_ps, 1)

        def turn(i):
            for q in range(4):
                h, u, w, v = 4 * i + q, q // 2, q % 2, q % 2
                if w == 0:
                    wait(pe, s.window_in[u], 16 * (i + 1))
                wait(pe, s.oneT_ready, h + 1)
                wait(pe, s.loT_ready, h + 1)
                wait(pe, s.scored, h)
                for j in range(HS):
                    out = score_ps[:, j * NT:(j + 1) * NT]
                    pe.matmul(out, b.loT[v][:, j * P:(j + 1) * P], m.s_src[:, :], start=True, stop=False)
                    for part in range(3):
                        s_dst = b.window[u][:, part * AW + H:part * AW + AW].broadcast_to([P, NT])
                        ins = pe.matmul(out, b.oneT[v][:, j * P:(j + 1) * P], s_dst, start=False, stop=(part == 2))
                ins.then_inc(s.score_ps, 1)
                wait(pe, s.vals_ready, h - 1)
                for j in range(HS):
                    for part in range(3):
                        ins = pe.matmul(wh_ps[v][:, j * H:(j + 1) * H], b.oneT[v][:, j * P:(j + 1) * P],
                                        b.window[u][:, part * AW:part * AW + H], start=(part == 0), stop=(part == 2))
                ins.then_inc(s.wh_ps, 1)
                if not (isinstance(i, int) and h == NH - 1):
                    broadcast(h + 1, (q + 1) // 2 % 2, 1 - w, i + (q + 1) // 4)
                if not (isinstance(i, int) and h == 0):
                    combine(h - 1, 1 - v)
        broadcast(0, 0, 0, 0)
        turns(pe, G // 2, turn)
        combine(NH - 1, 1)

    def scalar(act):
        def move_sums(h, v):
            wait(act, s.sums_ps, h + 1)
            for a in range(NACC):
                wait(act, s.added[a], 16 * (h - 1))
            act.activation(b.sums[v][:, :].rearrange("p (b c) -> p b c", b=2), sums_ps, ACT.Copy).then_inc(s.sums_moved, 1)

        def turn(i):
            for q in range(4):
                h, v = 4 * i + q, q % 2
                wait(act, s.scored, h + 1)
                wait(act, s.vals_ready, h - 1)
                act.activation(b.weight[v][:, :], b.leaky[v][:, :], ACT.Exp, scale=-1.0).then_inc(s.weighed, 1)
                wait(act, s.weighed, h + 1)
                wait(act, s.wh_ps, h + 1)
                wait(act, s.sums_ps, h - 1)
                for j in range(HS):
                    act.activation(b.vals[v][:, j * AW:j * AW + H], wh_ps[v][:, j * H:(j + 1) * H], ACT.Copy,
                                   scale=b.weight[v][:, j:j + 1]).then_inc(s.val_parts, 1)
                act.activation(tiles(b.vals[v][:, :], AW)[:, :, H], b.weight[v][:, :], ACT.Copy).then_inc(s.val_parts, 1)
                wait(act, s.val_parts, (HS + 1) * (h + 1))
                act.nop().then_inc(s.vals_ready, 1)
                if not (isinstance(i, int) and h == 0):
                    move_sums(h - 1, 1 - v)
        turns(act, G // 2, turn)
        move_sums(NH - 1, 1)

    def vector(dve):
        def turn(i):
            for q in range(4):
                h, u, w, v = 4 * i + q, q // 2, q % 2, q % 2
                c = (2 * i + u) * SUB + w * HS
                wait(dve, s.rel_ps, h + 1)
                wait(dve, s.wh_ps, h - 1)
                dve.tensor_scalar(b.oneT[v][:, :], rel_ps, m.iota_p[:, :], None, ALU.is_equal).then_inc(s.oneT_ready, 1)
                wait(dve, s.lo_ps, h + 1)
                dve.tensor_scalar(b.loT[v][:, :], lo_ps, m.iota_p[:, :], None, ALU.is_equal).then_inc(s.loT_ready, 1)
                wait(dve, s.src_ps, h + 1)
                wait(dve, s.sums_ps, h - 1)
                dve.tensor_tensor(tiles(b.same[v][:, :]), tiles(src_ps), wide(cols(m.src_c, c, HS), [P, HS, P]),
                                  ALU.is_equal).then_inc(s.same_ready, 1)
                wait(dve, s.score_ps, h + 1)
                wait(dve, s.picked, HS * h)
                wait(dve, s.scored, h - 1)
                for j in range(HS):
                    dve.scalar_tensor_tensor(b.junk[:, j * NT:(j + 1) * NT], m.iota_n[:, 0:NT], cols(m.hi_c, c + j, 1),
                                             score_ps[:, j * NT:(j + 1) * NT], ALU.is_equal, ALU.mult,
                                             accum_out=b.score[v][:, j:j + 1]).then_inc(s.picked, 1)
                wait(dve, s.picked, HS * (h + 1))
                wait(dve, s.weighed, h - 1)
                dve.scalar_tensor_tensor(b.leaky[v][:, :], b.score[v][:, :], ALPHA, b.score[v][:, :], ALU.mult, ALU.max).then_inc(s.scored, 1)
        turns(dve, G // 2, turn)
    return sync, gpsimd, tensor, scalar, vector


def edges_two(nc, d, m, ps):
    with ExitStack() as ctx:
        s = signals(nc, ctx, "e2", "rows_in*2 window_in*2 idx_ready added*4 rel_ps lo_ps src_ps score_ps wh_ps sums_ps oneT_ready loT_ready"
                    " same_ready picked scored weighed val_parts vals_ready sums_moved passed")
        b = buffers(nc, ctx, "e2", rows3=([3, GROUP], BF16, 2), window=([P, 3 * AW], BF16, 2), idx=([P, SUB], I32, 2),
                    oneT=([P, HALF], BF16, 2), loT=([P, HALF], F32, 2), same=([P, HALF], F32, 2), junk=([P, HS * NT], F32),
                    score=([P, HS], F32, 2), leaky=([P, HS], F32, 2), weight=([P, HS], F32, 2), vals=([P, HS * AW], F32, 2),
                    sums=([P, HS * AW], F32, 2))
        sg = signals(nc, ctx, "e2g", GENERAL)
        bg = general_buffers(nc, ctx, "e2g")
        branch(nc, m, edges_two_fast(nc, d, m, ps, s, b), edges_two_general(nc, d, m, ps, sg, bg))


def node_pass_three(nc, d, m):
    with ExitStack() as ctx:
        s = signals(nc, ctx, "n3", "acc_in*2 added01 added23 summed totalled inverted divided below powered above elued out_ready out_done*2")
        b = buffers(nc, ctx, "n3", acc=([P, NACC * CT * AW], F32, 2), one=([P, CT * AW], F32, 2), two=([P, CT * AW], F32, 2),
                    sums=([P, CT * AW], F32, 2), inv=([P, CT], F32, 2), total=([P, CT], F32, 2), mean=([P, CW], F32, 2), below=([P, CW], F32, 2),
                    power=([P, CW], F32, 2), out=([P, CW], F32, 2))
        block = ctx.enter_context(nc.Block())
        W = CT * AW

        @block.sync
        def _(sp):
            def turn(i):
                for u in range(2):
                    k = 2 * i + u
                    wait(sp, s.added01, k - 1)
                    wait(sp, s.added23, k - 1)
                    for a in range(NACC):
                        sp.dma_start(tiles(b.acc[u][:, a * W:(a + 1) * W], AW), chunk_rows(d.acc[a], k)).then_inc(s.acc_in[u], 16)
                for u in range(2):
                    k = 2 * i + u
                    wait(sp, s.out_ready, k + 1)
                    if isinstance(i, int) and k == NC - 1:
                        full, left = divmod(N - k * CW, P)
                        sp.dma_start(d.out[k * CW:k * CW + full * P].rearrange("(t p) f -> p t f", p=P),
                                     tiles(b.out[u][:, 0:full * H])).then_inc(s.out_done[u], 16)
                        sp.dma_start(d.out[k * CW + full * P:N], b.out[u][0:left, full * H:(full + 1) * H]).then_inc(s.out_done[u], 16)
                    else:
                        sp.dma_start(chunk_rows(d.out, k), tiles(b.out[u][:, :])).then_inc(s.out_done[u], 16)
            turn_pairs(sp, turn)
            sp.wait_ge(s.out_done[0], 16 * (NC // 2))
            sp.wait_ge(s.out_done[1], 16 * (NC // 2 + 1))

        @block.gpsimd
        def _(pool):
            def turn(i):
                for u in range(2):
                    k = 2 * i + u
                    wait(pool, s.acc_in[u], 16 * NACC * (i + 1))
                    wait(pool, s.summed, k - 1)
                    pool.tensor_tensor(b.two[u][:, :], b.acc[u][:, 2 * W:3 * W], b.acc[u][:, 3 * W:], ALU.add).then_inc(s.added23, 1)
            turn_pairs(pool, turn)

        @block.vector
        def _(dve):
            def turn(i):
                for u in range(2):
                    k = 2 * i + u
                    wait(dve, s.acc_in[u], 16 * NACC * (i + 1))
                    wait(dve, s.summed, k - 1)
                    dve.tensor_tensor(b.one[u][:, :], b.acc[u][:, 0:W], b.acc[u][:, W:2 * W], ALU.add).then_inc(s.added01, 1)
                    wait(dve, s.added01, k + 1)
                    wait(dve, s.added23, k + 1)
                    wait(dve, s.divided, k - 1)
                    dve.tensor_tensor(b.sums[u][:, :], b.one[u][:, :], b.two[u][:, :], ALU.add).then_inc(s.summed, 1)
                    wait(dve, s.summed, k + 1)
                    wait(dve, s.inverted, k - 1)
                    dve.tensor_tensor(b.total[u][:, :], tiles(b.sums[u][:, :], AW)[:, :, H], cols(m.no_node, k * CT, CT), ALU.add).then_inc(s.totalled, 1)
                    wait(dve, s.totalled, k + 1)
                    dve.reciprocal(b.inv[u][:, :], b.total[u][:, :]).then_inc(s.inverted, 1)
                    wait(dve, s.inverted, k + 1)
                    wait(dve, s.above, k - 1)
                    dve.tensor_tensor(tiles(b.mean[u][:, :]), tiles(b.sums[u][:, :], AW)[:, :, 0:H],
                                      wide(b.inv[u][:, :], [P, CT, H]), ALU.mult).then_inc(s.divided, 1)
                    wait(dve, s.divided, k + 1)
                    wait(dve, s.powered, k - 1)
                    dve.tensor_scalar(b.below[u][:, :], b.mean[u][:, :], 0.0, None, ALU.min).then_inc(s.below, 1)
                for u in range(2):
                    k = 2 * i + u
                    wait(dve, s.powered, k + 1)
                    wait(dve, s.out_done[u], 16 * i)
                    dve.scalar_tensor_tensor(b.out[u][:, :], b.mean[u][:, :], 0.0, b.power[u][:, :], ALU.max, ALU.add).then_inc(s.above, 1)
                    wait(dve, s.above, k + 1)
                    dve.scalar_tensor_tensor(b.out[u][:, :], b.out[u][:, :], -1.0, cols(m.aggT, k * CW, CW), ALU.add, ALU.add).then_inc(s.out_ready, 1)
            turn_pairs(dve, turn)

        @block.scalar
        def _(act):
            def turn(i):
                for u in range(2):
                    k = 2 * i + u
                    wait(act, s.below, k + 1)
                    wait(act, s.above, k - 1)
                    act.activation(b.power[u][:, :], b.below[u][:, :], ACT.Exp).then_inc(s.powered, 1)
            turn_pairs(act, turn)


def program(nc, given):
    tables = {}
    for name, shape, dtype in (("p_table", [ROWS, H], F32), ("q_table", [ROWS, H], F32), ("q_split", [ROWS, 3 * H], BF16),
                               ("wh_table", [ROWS, WW], F32), ("w_split", [ROWS, 3 * AW], BF16), ("edge_rows", [G, 3, GROUP], BF16)):
        tables[name] = nc.dram_tensor(name, shape, dtype, kind="Internal").ap()
    tables["acc"] = [nc.dram_tensor(f"acc{a}", [ROWS, AW], F32, kind="Internal").ap() for a in range(NACC + 1)]
    d = named("Dram", {**given, **tables})
    with ExitStack() as ctx:
        ps = ctx.enter_context(nc.psum_tensor("ps", [P, 8, 512], F32))
        m = buffers(nc, ctx, "all", h=([P, ROWS], F32), hT=([P, ROWS], F32), aggT=([P, ROWS], F32), degree=([1, ROWS], F32),
                    w1=([P, 3 * H], F32), w2=([P, H], F32), u1=([P, 2 * H], F32), u2=([P, H], F32), l1wx=([P, WW], F32),
                    b1_all=([P, H], F32), gamma_all=([P, H], F32), beta_all=([P, H], F32), ub1_col=([P, 1], F32),
                    b2_row=([1, H], F32), ub2_row=([1, H], F32), ones_row=([1, P], F32), ones_bf=([P, 1], BF16),
                    iota_n=([P, P], F32), iota_p=([P, 1], F32), before=([P, P], F32), ident=([P, P], F32), dump=([P, 1], F32),
                    pick=([3, 4 * P], BF16), first_row=([1, G], I32), fits=([1, 1], I32), src_c=([P, G * SUB], F32),
                    hi_c=([P, G * SUB], F32), dst_c=([P, G * SUB], F32), rel_c=([P, G * SUB], F32), src_i=([P, G * SUB], I32),
                    dst_i=([P, G * SUB], I32), repeats=([P, G * SUB], F32), to_i=([P, G * SUB], I32), s_src=([P, NT], F32), no_node=([P, NT], F32))
        prepare(nc, d, m, ps)
        node_pass_one(nc, d, m, ps)
        edges_one(nc, d, m, ps)
        node_pass_two(nc, d, m, ps)
        edges_two(nc, d, m, ps)
        node_pass_three(nc, d, m)


def kernel(**inputs):
    import numpy as np
    import concourse.bacc as bacc
    from concourse.bass_utils import run_bass_kernel_spmd

    x = np.zeros((ROWS, H), np.float32)
    x[:N] = inputs["x"]
    attr = np.zeros((G * GROUP, H), np.float32)
    attr[:E] = inputs["edge_attr_128"]
    ends = {}
    for name in ("src", "dst"):
        ends[name] = np.full(G * GROUP, N, np.int32)
        ends[name][:E] = inputs[name]
    arrays = {
        "x": x, "src": ends["src"], "dst": ends["dst"],
        "attrT": np.ascontiguousarray(attr.reshape(G, GROUP, H).transpose(0, 2, 1)),
        "w1": inputs["L0_gnn_msg_W1"], "b1": inputs["L0_gnn_msg_b1"], "w2": inputs["L0_gnn_msg_W2"], "b2": inputs["L0_gnn_msg_b2"],
        "u1": inputs["L0_gnn_upd_W1"], "ub1": inputs["L0_gnn_upd_b1"], "u2": inputs["L0_gnn_upd_W2"], "ub2": inputs["L0_gnn_upd_b2"],
        "gamma": inputs["L0_gnn_ln_gamma"], "beta": inputs["L0_gnn_ln_beta"], "l1w": inputs["L1_gnn_W"], "a": inputs["L1_gnn_a"],
    }
    arrays = {name: np.ascontiguousarray(a) for name, a in arrays.items()}
    nc = bacc.Bacc("TRN2", target_bir_lowering=False, num_devices=1)
    d = {name: nc.dram_tensor(f"in_{name}", a.shape, mybir.dt.from_np(a.dtype), kind="ExternalInput").ap()
         for name, a in arrays.items()}
    d["out"] = nc.dram_tensor("out", (N, H), F32, kind="ExternalOutput").ap()
    program(nc, d)
    return run_bass_kernel_spmd(nc, [{f"in_{name}": a for name, a in arrays.items()}], core_ids=[0]).results[0]["out"]
```

```python
import concourse.bass as bass
from concourse import mybir
from concourse.alu_op_type import AluOpType as ALU
from contextlib import ExitStack
from collections import namedtuple

N, E, H = 6250, 106250, 128
P = 128
GROUP = 1024
G = -(-E // GROUP)
SUB = GROUP // P
HALF = GROUP // 2
HS = SUB // 2
NH = 2 * G
NT = 50
ROWS = NT * P
CT = 5
CW = CT * P
NC = NT // CT
DUMP = N + 1
NACC = 4
AW = H + 1
WW = H + 2
EPS = 1e-5
ALPHA = 0.2

F32, BF16, I32 = mybir.dt.float32, mybir.dt.bfloat16, mybir.dt.int32
ACT = mybir.ActivationFunctionType
X = mybir.AxisListType.X


def wait(eng, sem, value):
    if isinstance(value, int) and value <= 0:
        return
    eng.wait_ge(sem, value)


def passed(eng, sem):
    eng.sem_inc(sem, 1)


def cols(tensor, start, size):
    if isinstance(start, int):
        return tensor[:, start:start + size]
    return tensor[:, bass.ds(start, size)]


def rows(table, start, size):
    if isinstance(start, int):
        return table[start:start + size]
    return table[bass.ds(start, size)]


def wide(column, shape):
    return column.unsqueeze(2).broadcast_to(shape)


def over_tiles(row, shape):
    return row.unsqueeze(1).broadcast_to(shape)


class Chain:

    def __init__(self, eng, sem, start=0):
        self.eng, self.sem, self.start, self.n = eng, sem, start, 0

    def did(self, instruction):
        self.n += 1
        instruction.then_inc(self.sem, 1)
        return self.n

    def after(self, n=None):
        wait(self.eng, self.sem, self.start + (self.n if n is None else n))

    def then(self, instruction):
        self.did(instruction)
        self.after()


def turns(eng, count, body):
    body(0)
    with eng.Fori(1, count - 1) as i:
        body(i)
    body(count - 1)


def named(kind, things):
    return namedtuple(kind, list(things))(**things)


def signals(nc, ctx, phase, names):
    found, free = {}, []

    def clear(*_):
        nc.clear_and_free_semaphores(free)
        nc.all_engine_barrier(sem_only=True)
    ctx.callback(clear)
    for name in names.split():
        name, _, n = name.partition("*")
        if n:
            found[name] = [nc.alloc_semaphore(f"{phase}_{name}{k}") for k in range(int(n))]
        else:
            found[name] = nc.alloc_semaphore(f"{phase}_{name}")
        free += found[name] if n else [found[name]]
    return named("Signals", found)


def buffers(nc, ctx, phase, **shapes):
    found = {}
    for name, (shape, dtype, *n) in shapes.items():
        made = [ctx.enter_context(nc.sbuf_tensor(f"{phase}_{name}{k}", shape, dtype)) for k in range(n[0] if n else 1)]
        found[name] = made if n else made[0]
    return named("Buffers", found)


def tiles(ap, width=H):
    return ap.rearrange("p (t f) -> p t f", f=width)


def prepare(nc, d, m, ps):
    with ExitStack() as ctx:
        s = signals(nc, ctx, "prep", "ids_in weights_in vectors_in iotas consts own rows_ready rows_out tr_ps tr_evac bc_ps bc_used"
                    " span_ps flag_ready zeros_ready acc_zeroed l1wT_ps l1wT wa_ps")
        b = buffers(nc, ctx, "prep", dst_g=([G, GROUP], I32), src_g=([G, GROUP], I32), hi_i=([G, GROUP], I32),
                    lo_i=([G, GROUP], I32), dst_f=([G, GROUP], F32), src_f=([G, GROUP], F32), hi_f=([G, GROUP], F32),
                    rel_f=([G, GROUP], F32), rows3=([G, 3 * GROUP], BF16), first=([G, 1], F32), last=([G, 1], F32),
                    span=([G, 1], F32), iota_n_i=([P, P], I32), iota_p_i=([P, 1], I32), iota_node=([P, NT], I32), node_f=([P, NT], F32), span_row=([1, G], F32),
                    vec=([1, 8 * H], F32), l1w=([P, H], F32), l1wT=([P, H], F32), acol=([P, 2], F32), widest=([1, 1], F32),
                    zeros=([P, ROWS * AW // P // 2], F32))
        VEC = ["b1", "b2", "ub1", "ub2", "gamma", "beta"]
        block = ctx.enter_context(nc.Block())

        @block.sync
        def _(sp):
            sp.dma_start(b.dst_g[:, :], d.dst.rearrange("(g e) -> g e", e=GROUP)).then_inc(s.ids_in, 16)
            sp.dma_start(b.src_g[:, :], d.src.rearrange("(g e) -> g e", e=GROUP)).then_inc(s.ids_in, 16)
            for t in range(3):
                sp.dma_start(m.w1[:, t * H:(t + 1) * H], d.w1[t * H:(t + 1) * H, :]).then_inc(s.weights_in, 16)
            for t in range(2):
                sp.dma_start(m.u1[:, t * H:(t + 1) * H], d.u1[t * H:(t + 1) * H, :]).then_inc(s.weights_in, 16)
            sp.dma_start(m.w2[:, :], d.w2).then_inc(s.weights_in, 16)
            sp.dma_start(m.u2[:, :], d.u2).then_inc(s.weights_in, 16)
            sp.dma_start(b.l1w[:, :], d.l1w).then_inc(s.weights_in, 16)
            for n, name in enumerate(VEC):
                v = {"b1": d.b1, "b2": d.b2, "ub1": d.ub1, "ub2": d.ub2, "gamma": d.gamma, "beta": d.beta}[name]
                sp.dma_start(b.vec[:, n * H:(n + 1) * H], v.rearrange("(o f) -> o f", o=1)).then_inc(s.vectors_in, 16)
            sp.dma_start(b.vec[:, 6 * H:8 * H], d.a).then_inc(s.vectors_in, 16)
            sp.wait_ge(s.zeros_ready, 1)
            for acc in d.acc:
                halves = acc.rearrange("(p r) c -> p (r c)", p=P)
                half = ROWS * AW // P // 2
                for n in range(2):
                    sp.dma_start(halves[:, n * half:(n + 1) * half], b.zeros[:, :]).then_inc(s.acc_zeroed, 16)
            sp.wait_ge(s.rows_ready, 3)
            sp.dma_start(d.edge_rows.rearrange("g r e -> g (r e)"), b.rows3[:, :]).then_inc(s.rows_out, 16)
            sp.wait_ge(s.rows_out, 16)
            sp.wait_ge(s.weights_in, 16 * 8)
            sp.wait_ge(s.acc_zeroed, 16 * 2 * len(d.acc))

        @block.gpsimd
        def _(pool):
            pool.iota(b.iota_n_i[:, :], [[1, P]], base=0, channel_multiplier=0).then_inc(s.iotas, 1)
            pool.iota(b.iota_p_i[:, :], [[0, 1]], base=0, channel_multiplier=1).then_inc(s.iotas, 1)
            pool.iota(b.iota_node[:, :], [[P, NT]], base=0, channel_multiplier=1).then_inc(s.iotas, 1)
            pool.memset(b.zeros[:, :], 0.0).then_inc(s.zeros_ready, 1)

        @block.vector
        def _(dve):
            own = Chain(dve, s.own)
            own.did(dve.memset(m.aggT[:, :], 0.0))
            own.did(dve.memset(m.degree[:, :], 0.0))
            own.did(dve.memset(m.ones_row[:, :], 1.0))
            own.did(dve.memset(m.ones_bf[:, :], 1.0))
            own.did(dve.memset(m.minus_half[:, :], -0.5))
            dve.wait_ge(s.iotas, 3)
            own.then(dve.tensor_copy(b.node_f[:, :], b.iota_node[:, :]))
            own.did(dve.tensor_scalar(m.no_node[:, :], b.node_f[:, :], float(N), None, ALU.is_ge))
            own.then(dve.tensor_copy(m.iota_n[:, :], b.iota_n_i[:, :]))
            own.then(dve.tensor_copy(m.iota_p[:, :], b.iota_p_i[:, :]))
            own.did(dve.tensor_scalar(m.before[:, :], m.iota_n[:, :], m.iota_p[:, :], None, ALU.is_lt))
            own.did(dve.tensor_scalar(m.ident[:, :], m.iota_n[:, :], m.iota_p[:, :], None, ALU.is_equal))
            for n in range(3):
                own.did(dve.tensor_scalar(m.pick[0:3, n * P:(n + 1) * P], m.iota_p[0:3, :].broadcast_to([3, P]), float(n), None, ALU.is_equal))
            own.after()
            own.then(dve.scalar_tensor_tensor(m.pick[0:3, 3 * P:4 * P], m.pick[0:3, 0:P], float(P), m.pick[0:3, P:2 * P], ALU.mult, ALU.add))
            dve.tensor_scalar(m.dump[:, :], m.iota_p[:, :], float(DUMP), None, ALU.add).then_inc(s.consts, 1)
            dve.wait_ge(s.ids_in, 32)
            own.did(dve.tensor_copy(b.dst_f[:, :], b.dst_g[:, :]))
            own.did(dve.tensor_copy(b.src_f[:, :], b.src_g[:, :]))
            own.did(dve.tensor_single_scalar(b.hi_i[:, :], b.src_g[:, :], 7, ALU.logical_shift_right))
            own.then(dve.tensor_single_scalar(b.lo_i[:, :], b.src_g[:, :], P - 1, ALU.bitwise_and))
            own.did(dve.tensor_copy(b.hi_f[:, :], b.hi_i[:, :]))
            own.did(dve.tensor_reduce(b.first[:, :], b.dst_f[:, :], X, ALU.min))
            own.then(dve.tensor_reduce(b.last[:, :], b.dst_f[:, :], X, ALU.max))
            own.did(dve.tensor_tensor(b.span[:, :], b.last[:, :], b.first[:, :], ALU.subtract))
            own.then(dve.tensor_scalar(b.rel_f[:, :], b.dst_f[:, :], b.first[:, :], None, ALU.subtract))
            dve.tensor_copy(b.rows3[:, 0:GROUP], b.hi_i[:, :]).then_inc(s.rows_ready, 1)
            dve.tensor_copy(b.rows3[:, GROUP:2 * GROUP], b.lo_i[:, :]).then_inc(s.rows_ready, 1)
            dve.tensor_copy(b.rows3[:, 2 * GROUP:], b.rel_f[:, :]).then_inc(s.rows_ready, 1)
            for q, col in enumerate((m.src_c, m.hi_c, m.dst_c, m.rel_c)):
                dve.wait_ge(s.tr_ps, 2 * q + 2)
                for half in range(2):
                    got = ps[:, 2 * q + half, 0:HS * G].rearrange("p (j g) -> p j g", g=G)
                    ins = dve.tensor_copy(col[:, :].rearrange("p (g j) -> p j g", j=SUB)[:, half * HS:(half + 1) * HS, :], got)
                    ins.then_inc(s.tr_evac, 1)
            dve.wait_ge(s.tr_evac, 8)
            own.did(dve.tensor_copy(m.src_i[:, :], m.src_c[:, :]))
            own.did(dve.tensor_copy(m.dst_i[:, :], m.dst_c[:, :]))
            dve.wait_ge(s.bc_ps, 1)
            own.did(dve.tensor_copy(m.b1_row[:, :], b.vec[:, 0:H]))
            own.did(dve.tensor_copy(m.gamma_all[:, :], ps[:, 0, H:2 * H]))
            own.did(dve.tensor_copy(m.beta_all[:, :], ps[:, 0, 2 * H:3 * H]))
            own.did(dve.tensor_copy(m.ub1_col[:, :], ps[:, 1, 0:1]))
            own.did(dve.tensor_copy(b.acol[:, :], ps[:, 1, 1:3]))
            own.did(dve.tensor_copy(m.b2_row[:, :], b.vec[:, H:2 * H]))
            own.did(dve.tensor_copy(m.ub2_row[:, :], b.vec[:, 3 * H:4 * H]))
            own.did(dve.tensor_copy(b.l1wT[:, :], ps[:, 2, 0:H]))
            own.did(dve.tensor_copy(m.first_row[:, :], ps[0:1, 3, 0:G]))
            own.after()
            dve.tensor_copy(b.span_row[:, :], ps[0:1, 3, G:2 * G]).then_inc(s.bc_used, 1)
            dve.wait_ge(s.bc_used, 1)
            own.then(dve.tensor_reduce(b.widest[:, :], b.span_row[:, :], X, ALU.max))
            own.did(dve.tensor_scalar(m.fits[:, :], b.widest[:, :], float(P), None, ALU.is_lt))
            own.did(dve.tensor_copy(m.l1wx[:, 0:H], b.l1w[:, :]))
            dve.wait_ge(s.wa_ps, 1)
            own.did(dve.tensor_copy(m.l1wx[:, H:H + 1], ps[:, 4, 1:2]))
            own.did(dve.tensor_copy(m.l1wx[:, H + 1:H + 2], ps[:, 4, 0:1]))
            own.after()

        @block.tensor
        def _(pe):
            pe.wait_ge(s.consts, 1)
            pe.wait_ge(s.rows_ready, 3)
            for q, f in enumerate((b.src_f, b.hi_f, b.dst_f, b.rel_f)):
                for j in range(SUB):
                    out = ps[:, 2 * q + j // HS, (j % HS) * G:(j % HS + 1) * G]
                    ins = pe.transpose(out, f[:, j * P:(j + 1) * P], m.ident[0:G, 0:G])
                    if j % HS == HS - 1:
                        ins.then_inc(s.tr_ps, 1)
            pe.wait_ge(s.tr_evac, 8)
            pe.wait_ge(s.vectors_in, 16 * 7)
            pe.wait_ge(s.weights_in, 16 * 8)
            for n, v in ((1, 4), (2, 5)):
                pe.matmul(ps[:, 0, n * H:(n + 1) * H], m.ones_row[:, :], b.vec[:, v * H:(v + 1) * H], start=True, stop=True)
            for n, v in enumerate((2, 6, 7)):
                pe.matmul(ps[:, 1, n:n + 1], b.vec[:, v * H:(v + 1) * H], m.ones_row[:, 0:1], start=True, stop=True)
            pe.transpose(ps[:, 2, 0:H], b.l1w[:, :], m.ident[:, :])
            pe.transpose(ps[0:1, 3, 0:G], b.first[:, :], m.ident[0:G, 0:G])
            pe.transpose(ps[0:1, 3, G:2 * G], b.span[:, :], m.ident[0:G, 0:G]).then_inc(s.bc_ps, 1)
            pe.wait_ge(s.bc_used, 1)
            pe.matmul(ps[:, 4, 0:2], b.l1wT[:, :], b.acol[:, :], start=True, stop=True).then_inc(s.wa_ps, 1)


NORM = "normable measured aggregated spread rooted"


def norm_buffers(nc, ctx, phase):
    return buffers(nc, ctx, phase, stats=([P, CT * 6], F32, 2), mv=([P, CT * 2], F32, 2), var=([P, CT], F32, 2), inv=([P, CT], F32, 2))


def norm_measure(dve, s, b, k, u, x):
    for t in range(CT):
        dve.bn_stats(b.stats[u][:, t * 6:(t + 1) * 6], x[:, t * H:(t + 1) * H]).then_inc(s.measured, 1)
    wait(dve, s.measured, CT * (k + 1))
    passed(dve, s.normable)
    for t in range(CT):
        dve.bn_aggr(b.mv[u][:, t * 2:(t + 1) * 2], b.stats[u][:, t * 6:(t + 1) * 6]).then_inc(s.aggregated, 1)
    wait(dve, s.aggregated, CT * (k + 1))
    dve.tensor_scalar(b.var[u][:, :], tiles(b.mv[u][:, :], 2)[:, :, 1], EPS, None, ALU.add).then_inc(s.spread, 1)


def norm_root(pool, m, s, b, k, u):
    wait(pool, s.spread, k + 1)
    pool.tensor_tensor(b.inv[u][:, :], b.var[u][:, :], m.minus_half[:, :], ALU.pow).then_inc(s.rooted, 1)


def norm_apply(dve, s, b, k, u, x, out, done):
    wait(dve, s.rooted, k + 1)
    for t in range(CT):
        dve.tensor_scalar(out[:, t * H:(t + 1) * H], x[:, t * H:(t + 1) * H], b.mv[u][:, 2 * t:2 * t + 1], b.inv[u][:, t:t + 1],
                          ALU.subtract, ALU.mult).then_inc(done, 1)


def chunk_rows(table, k):
    return rows(table, k * CW, CW).rearrange("(t p) f -> p t f", p=P)


def turn_pairs(eng, body):
    turns(eng, NC // 2, body)


def node_pass_one(nc, d, m, ps):
    with ExitStack() as ctx:
        s = signals(nc, ctx, "n1", NORM + " x_in*2 normed relued h_kept hT_ps hT_moved hT_kept pq_ps p_moved high rest mid low p_out*2 qs_out*2")
        nb = norm_buffers(nc, ctx, "n1")
        b = buffers(nc, ctx, "n1", x=([P, CW], F32, 2), xn=([P, CW], F32, 2), h=([P, CW], F32, 2), hT=([P, CW], F32, 2),
                    p=([P, CW], F32, 2), rest=([P, CW], F32, 2), qs=([P, 3 * CW], BF16, 2))
        hT_ps = ps[:, 0:2, :].rearrange("p b c -> p (b c)")
        pq_ps = [ps[:, n:n + 3, :].rearrange("p b c -> p (b c)") for n in (2, 5)]
        q_ps = [tiles(pq[:, 0:2 * CW], 2 * H)[:, :, H:] for pq in pq_ps]
        parts = [[tiles(b.qs[u][:, :], 3 * H)[:, :, n * H:(n + 1) * H] for n in range(3)] for u in range(2)]
        block = ctx.enter_context(nc.Block())

        @block.sync
        def _(sp):
            def load(k, u):
                wait(sp, s.normed, CT * (k - 1))
                sp.dma_start(tiles(b.x[u][:, :]), chunk_rows(d.x, k)).then_inc(s.x_in[u], 16)

            def turn(i):
                if not (isinstance(i, int) and i == NC // 2 - 1):
                    for u in range(2):
                        load(2 * i + u + 2, u)
                for u in range(2):
                    k = 2 * i + u
                    wait(sp, s.p_moved, k + 1)
                    sp.dma_start(chunk_rows(d.p_table, k), tiles(b.p[u][:, :])).then_inc(s.p_out[u], 16)
                    wait(sp, s.low, k + 1)
                    sp.dma_start(chunk_rows(d.q_split, k), tiles(b.qs[u][:, :], 3 * H)).then_inc(s.qs_out[u], 16)
            load(0, 0)
            load(1, 1)
            turn_pairs(sp, turn)
            for u in range(2):
                sp.wait_ge(s.p_out[u], 16 * NC // 2)
                sp.wait_ge(s.qs_out[u], 16 * NC // 2)

        @block.vector
        def _(dve):
            def measure(k, u, i):
                wait(dve, s.x_in[u], 16 * (i + 1))
                wait(dve, s.normed, CT * (k - 1))
                norm_measure(dve, s, nb, k, u, b.x[u][:, :])

            def turn(i):
                for u in range(2):
                    k = 2 * i + u
                    wait(dve, s.relued, k - 1)
                    norm_apply(dve, s, nb, k, u, b.x[u][:, :], b.xn[u][:, :], s.normed)
                for u in range(2):
                    if not (isinstance(i, int) and i == NC // 2 - 1):
                        measure(2 * i + u + 2, u, i + 1)
                for u in range(2):
                    k = 2 * i + u
                    wait(dve, s.high, k + 1)
                    wait(dve, s.low, k - 1)
                    dve.tensor_tensor(tiles(b.rest[u][:, :]), q_ps[u], parts[u][0], ALU.subtract).then_inc(s.rest, 1)
                for u in range(2):
                    k = 2 * i + u
                    wait(dve, s.mid, k + 1)
                    dve.tensor_tensor(parts[u][2], tiles(b.rest[u][:, :]), parts[u][1], ALU.subtract).then_inc(s.low, 1)
            measure(0, 0, 0)
            measure(1, 1, 0)
            turn_pairs(dve, turn)

        @block.scalar
        def _(act):
            def turn(i):
                for u in range(2):
                    k = 2 * i + u
                    wait(act, s.normed, CT * (k + 1))
                    wait(act, s.hT_ps, k - 1)
                    wait(act, s.h_kept, k - 1)
                    act.activation(b.h[u][:, :], b.xn[u][:, :], ACT.Relu).then_inc(s.relued, 1)
                for u in range(2):
                    k = 2 * i + u
                    wait(act, s.hT_ps, k + 1)
                    wait(act, s.pq_ps, k - 1)
                    wait(act, s.hT_kept, k - 1)
                    act.activation(b.hT[u][:, :], hT_ps[:, 0:CW], ACT.Copy).then_inc(s.hT_moved, 1)
                for u in range(2):
                    k = 2 * i + u
                    wait(act, s.pq_ps, k + 1)
                    wait(act, s.p_out[u], 16 * i)
                    act.activation(tiles(b.p[u][:, :]), tiles(pq_ps[u][:, 0:2 * CW], 2 * H)[:, :, 0:H], ACT.Copy).then_inc(s.p_moved, 1)
                    wait(act, s.qs_out[u], 16 * i)
                    act.activation(parts[u][0], q_ps[u], ACT.Copy).then_inc(s.high, 1)
                for u in range(2):
                    wait(act, s.rest, 2 * i + u + 1)
                    act.activation(parts[u][1], tiles(b.rest[u][:, :]), ACT.Copy).then_inc(s.mid, 1)
            turn_pairs(act, turn)

        @block.gpsimd
        def _(pool):
            def turn(i):
                for u in range(2):
                    if not (isinstance(i, int) and i == NC // 2 - 1):
                        wait(pool, s.normed, CT * (2 * i + u + 1))
                        norm_root(pool, m, s, nb, 2 * i + u + 2, u)
                for u in range(2):
                    k = 2 * i + u
                    wait(pool, s.relued, k + 1)
                    pool.tensor_copy(cols(m.h, k * CW, CW), b.h[u][:, :]).then_inc(s.h_kept, 1)
                for u in range(2):
                    k = 2 * i + u
                    wait(pool, s.hT_moved, k + 1)
                    pool.tensor_copy(cols(m.hT, k * CW, CW), b.hT[u][:, :]).then_inc(s.hT_kept, 1)
            norm_root(pool, m, s, nb, 0, 0)
            norm_root(pool, m, s, nb, 1, 1)
            turn_pairs(pool, turn)

        @block.tensor
        def _(pe):
            def turn(i):
                for u in range(2):
                    k = 2 * i + u
                    wait(pe, s.relued, k + 1)
                    wait(pe, s.hT_moved, k)
                    for t in range(CT):
                        ins = pe.transpose(hT_ps[:, t * P:(t + 1) * P], b.h[u][:, t * H:(t + 1) * H], m.ident[:, :])
                    ins.then_inc(s.hT_ps, 1)
                for u in range(2):
                    k = 2 * i + u
                    wait(pe, s.hT_moved, k + 1)
                    wait(pe, s.p_moved, k - 1)
                    wait(pe, s.rest, k - 1)
                    for t in range(CT):
                        out = pq_ps[u][:, t * 2 * H:(t + 1) * 2 * H]
                        pe.matmul(out, b.hT[u][:, t * P:(t + 1) * P], m.w1[:, 0:2 * H], start=True, stop=False)
                        ins = pe.matmul(out[:, H:], m.ones_row[:, :], m.b1_row[:, :], start=False, stop=True)
                    ins.then_inc(s.pq_ps, 1)
            turn_pairs(pe, turn)


def edges_one_fast(nc, d, m, ps, s, b):
    rel_ps = ps[:, 0, :]
    z_ps = [ps[:, 2, :], ps[:, 3, :]]
    src_ps = ps[:, 4, :]
    agg_ps = [ps[:, 5, 0:P], ps[:, 6, 0:P]]
    deg_ps = [ps[0:1, 1, 0:P], ps[0:1, 7, 0:P]]

    def sync(sp):
        def turn(i):
            for u in range(2):
                g = 2 * i + u
                wait(sp, s.z_ps, 2 * (g - 1))
                wait(sp, s.src_ps, 2 * (g - 1))
                sp.dma_start(b.rows3[u][:, :], rows(d.edge_rows, g, 1).rearrange("o r e -> (o r) e")).then_inc(s.rows_in[u], 16)
                sp.dma_start(b.attr[u][:, :], rows(d.attrT, g, 1).rearrange("o f e -> (o f) e")).then_inc(s.attr_in[u], 16)
                first = sp.value_load(cols(m.first_row, g, 1), min_val=0, max_val=N)
                sp.dma_start(b.window[u][:, :], rows(d.q_split, first, P)).then_inc(s.window_in[u], 16)
        turns(sp, G // 2, turn)

    def gpsimd(pool):
        def turn(i):
            for u in range(2):
                g = 2 * i + u
                pool.wait_ge(s.idx_ready, g + 1)
                wait(pool, s.z_ready, 2 * (g - 1))
                passed(pool, s.passed)
                for j in range(SUB):
                    pool.indirect_dma_start(b.gathered[u][:, j * H:(j + 1) * H], None, d.p_table[:, :],
                                            bass.IndirectOffsetOnAxis(ap=b.idx[u][:, j:j + 1], axis=0)).then_inc(s.gathered[u], 16)
        turns(pool, G // 2, turn)

    def tensor(pe):
        def broadcast(h, u, w, i):
            if w == 0:
                wait(pe, s.rows_in[u], 16 * (i + 1))
            wait(pe, s.oneT_ready, h)
            pe.matmul(rel_ps, m.pick[0:3, 2 * P:3 * P], b.rows3[u][:, w * HALF:(w + 1) * HALF], start=True, stop=True).then_inc(s.rel_ps, 1)
            wait(pe, s.counted, HS * h)
            pe.matmul(src_ps, m.pick[0:3, 3 * P:4 * P], b.rows3[u][:, w * HALF:(w + 1) * HALF], start=True, stop=True).then_inc(s.src_ps, 1)

        def sums(h, v, u, w, g):
            wait(pe, s.silu_ready, h + 1)
            wait(pe, s.one_ready, h + 1)
            if w == 0:
                wait(pe, s.agg_added, g - 1)
            for j in range(HS):
                pe.matmul(agg_ps[u], b.silu[v][:, j * H:(j + 1) * H], b.one[v][:, j * P:(j + 1) * P],
                          start=(w == 0 and j == 0), stop=(w == 1 and j == HS - 1))
            for j in range(HS):
                upper = b.one[v][:, j * P:(j + 1) * P].bitcast(BF16)[:, 1::2]
                ins = pe.matmul(deg_ps[u], m.ones_bf[:, :], upper, start=(w == 0 and j == 0), stop=(w == 1 and j == HS - 1))
            ins.then_inc(s.agg_ps, 1)

        def turn(i):
            for q in range(4):
                h, u, w, v = 4 * i + q, q // 2, q % 2, q % 2
                if not (isinstance(i, int) and h == NH - 1):
                    broadcast(h + 1, (q + 1) // 2 % 2, 1 - w, i + (q + 1) // 4)
                if w == 0:
                    wait(pe, s.attr_in[u], 16 * (i + 1))
                    wait(pe, s.window_in[u], 16 * (i + 1))
                wait(pe, s.oneT_ready, h + 1)
                wait(pe, s.z_ready, h - 1)
                for j in range(HS):
                    e = (w * HS + j) * P
                    z = z_ps[v][:, j * H:(j + 1) * H]
                    pe.matmul(z, b.attr[u][:, e:e + P], m.w1[:, 2 * H:3 * H], start=True, stop=False)
                    for part in range(3):
                        ins = pe.matmul(z, b.oneT[v][:, j * P:(j + 1) * P], b.window[u][:, part * H:(part + 1) * H], start=False, stop=(part == 2))
                ins.then_inc(s.z_ps, 1)
                if not (isinstance(i, int) and h == 0):
                    sums(h - 1, 1 - v, (q - 1) // 2 % 2, 1 - w, 2 * i + (q - 1) // 2)
        broadcast(0, 0, 0, 0)
        turns(pe, G // 2, turn)
        sums(NH - 1, 1, 1, 1, G - 1)

    def scalar(act):
        def turn(i):
            for q in range(4):
                h, v = 4 * i + q, q % 2
                wait(act, s.z_ready, h + 1)
                wait(act, s.agg_ps, h - 1)
                act.activation(b.silu[v][:, :], b.z[v][:, :], ACT.Silu).then_inc(s.silu_ready, 1)
        turns(act, G // 2, turn)

    def vector(dve):
        def place_indices(g, u):
            dve.tensor_copy(b.idx[u][:, :], cols(m.src_i, g * SUB, SUB)).then_inc(s.idx_ready, 1)

        def add_rows(h, v, u, w, i):
            wait(dve, s.z_ps, h + 1)
            if w == 0:
                wait(dve, s.gathered[u], 16 * SUB * (i + 1))
            wait(dve, s.silu_ready, h - 1)
            dve.tensor_tensor(b.z[v][:, :], z_ps[v], b.gathered[u][:, w * HS * H:(w + 1) * HS * H], ALU.add).then_inc(s.z_ready, 1)

        def add_sums(g, u):
            wait(dve, s.agg_ps, 2 * (g + 1))
            wait(dve, s.agg_added, g)
            wait(dve, s.deg_added, g)
            first = dve.value_load(cols(m.first_row, g, 1), min_val=0, max_val=N)
            dve.tensor_tensor(cols(m.degree, first, P), deg_ps[u], cols(m.degree, first, P), ALU.add).then_inc(s.deg_added, 1)
            wait(dve, s.deg_added, g + 1)
            dve.tensor_tensor(cols(m.aggT, first, P), agg_ps[u], cols(m.aggT, first, P), ALU.add).then_inc(s.agg_added, 1)

        def turn(i):
            for q in range(4):
                h, u, w, v = 4 * i + q, q // 2, q % 2, q % 2
                c = (2 * i + u) * SUB + w * HS
                wait(dve, s.rel_ps, h + 1)
                wait(dve, s.z_ps, h - 1)
                dve.tensor_scalar(b.oneT[v][:, :], rel_ps, m.iota_p[:, :], None, ALU.is_equal).then_inc(s.oneT_ready, 1)
                wait(dve, s.src_ps, h + 1)
                wait(dve, s.counted, HS * h)
                for j in range(HS):
                    dve.scalar_tensor_tensor(b.junk[:, j * P:(j + 1) * P], src_ps[:, j * P:(j + 1) * P], cols(m.src_c, c + j, 1),
                                             m.before[:, :], ALU.is_equal, ALU.mult, accum_out=cols(m.repeats, c + j, 1)).then_inc(s.counted, 1)
                wait(dve, s.agg_ps, h - 1)
                dve.tensor_tensor(tiles(b.one[v][:, :]), wide(cols(m.rel_c, c, HS), [P, HS, P]),
                                  over_tiles(m.iota_n[:, :], [P, HS, P]), ALU.is_equal).then_inc(s.one_ready, 1)
                if not (isinstance(i, int) and h == 0):
                    add_rows(h - 1, 1 - v, (q - 1) // 2 % 2, 1 - w, i + (q - 1) // 4)
                if w == 0 and not (isinstance(i, int) and (h == 0 or h == NH - 2)):
                    place_indices(2 * i + u + 1, 1 - u)
                if w == 1 and not (isinstance(i, int) and h == 1):
                    add_sums(2 * i + u - 1, 1 - u)
        place_indices(0, 0)
        place_indices(1, 1)
        turns(dve, G // 2, turn)
        add_rows(NH - 1, 1, 1, 1, G // 2 - 1)
        add_sums(G - 1, 1)
        again, away = m.rel_c[:, :], m.dst_c[:, :]
        step = Chain(dve, s.rows_chosen)
        dve.wait_ge(s.counted, HS * NH)
        dve.wait_ge(s.one_ready, NH)
        step.did(dve.tensor_scalar(again, m.repeats[:, :], 0.0, None, ALU.is_gt))
        step.then(dve.tensor_scalar(away, m.src_c[:, :], -1.0, m.dump[:, :], ALU.mult, ALU.add))
        step.then(dve.tensor_tensor(away, away, again, ALU.mult))
        step.then(dve.tensor_tensor(again, away, m.src_c[:, :], ALU.add))
        step.then(dve.tensor_copy(m.to_i[:, :], again))
    return sync, gpsimd, tensor, scalar, vector


TAIL = 9


def each_tile(eng, body):
    with eng.Fori(0, G) as g:
        with eng.Fori(0, SUB) as j:
            body(g * SUB + j, g, j)


def combine_indices(dve, m, s, b, own, t, key_c):
    dve.wait_ge(s.key_in, 16 * (t + 1))
    own.then(dve.tensor_copy(b.key_f[:, :], b.key_i[:, :]))
    own.then(dve.tensor_scalar(b.same[:, :], b.key_f[:, :], cols(key_c, t, 1), None, ALU.is_equal))
    own.then(dve.tensor_tensor(b.earlier[:, :], b.same[:, :], m.before[:, :], ALU.mult))
    own.then(dve.tensor_reduce(b.repeat[:, :], b.earlier[:, :], X, ALU.add))
    own.then(dve.tensor_scalar(b.again[:, :], b.repeat[:, :], 0.0, None, ALU.is_gt))
    own.then(dve.tensor_tensor(b.away[:, :], m.dump[:, :], cols(key_c, t, 1), ALU.subtract))
    own.then(dve.tensor_tensor(b.away[:, :], b.away[:, :], b.again[:, :], ALU.mult))
    own.then(dve.tensor_tensor(b.to_f[:, :], b.away[:, :], cols(key_c, t, 1), ALU.add))
    own.then(dve.tensor_copy(b.to_i[:, :], b.to_f[:, :]))


def join_three(dve, own, split, width, out):
    own.then(dve.tensor_tensor(out, split[:, 0:width], split[:, width:2 * width], ALU.add))
    own.then(dve.tensor_tensor(out, out, split[:, 2 * width:3 * width], ALU.add))


def scatter_tile(pool, s, b, t, acc):
    pool.wait_ge(s.sums_moved, t + 1)
    passed(pool, s.passed)
    pool.indirect_dma_start(acc[:, :], bass.IndirectOffsetOnAxis(ap=b.to_i[:, 0:1], axis=0), b.sums[:, :], None,
                            compute_op=ALU.add).then_inc(s.added, 16)
    pool.wait_ge(s.added, 16 * (t + 1))


def general_buffers(nc, ctx, phase):
    return buffers(nc, ctx, phase, src_x=([P, 1], I32), dst_x=([P, 1], I32), key_i=([P, P], I32), key_f=([P, P], F32),
                   same=([P, P], F32), earlier=([P, P], F32), repeat=([P, 1], F32), again=([P, 1], F32), away=([P, 1], F32),
                   to_f=([P, 1], F32), to_i=([P, 1], I32), vals=([P, AW], F32), sums=([P, AW], F32), at_src=([P, 3 * WW], BF16),
                   at_dst=([P, 3 * WW], BF16), p_src=([P, H], F32), src_row=([P, WW], F32), dst_row=([P, WW], F32), attr=([P, P], F32), z=([P, P], F32), score=([P, 1], F32), leaky=([P, 1], F32),
                   node_sums=([P, AW], F32))


GENERAL = "idx_ready rows_in key_in attr_in z_ps z_ready vals_ready own sums_ps sums_moved added node_in node_ps node_moved passed sp_passed"


def edges_one_general(nc, d, m, ps, s, b):
    acc = d.acc[NACC]
    STEPS = TAIL + 5

    def sync(sp):
        def tile(t, g, j):
            sp.dma_start(b.attr[:, :], d.attrT[bass.ds(g, 1), :, bass.ds(j * P, P)].rearrange("o f e -> (o f) e")).then_inc(s.attr_in, 16)
            sp.dma_start(b.key_i[:, :], rows(d.dst, t * P, P).partition_broadcast(P)).then_inc(s.key_in, 16)
            sp.wait_ge(s.added, 16 * (t + 1))
            passed(sp, s.sp_passed)
        each_tile(sp, tile)
        with sp.Fori(0, NT) as t:
            sp.dma_start(b.node_sums[:, :], rows(acc, t * P, P)).then_inc(s.node_in, 16)
            sp.wait_ge(s.node_moved, 2 * (t + 1))
            passed(sp, s.sp_passed)

    def gpsimd(pool):
        def tile(t, g, j):
            pool.tensor_copy(b.src_x[:, :], cols(m.src_i, t, 1)).then_inc(s.idx_ready, 1)
            pool.tensor_copy(b.dst_x[:, :], cols(m.dst_i, t, 1)).then_inc(s.idx_ready, 1)
            pool.wait_ge(s.idx_ready, 2 * (t + 1))
            passed(pool, s.passed)
            pool.indirect_dma_start(b.p_src[:, :], None, d.p_table[:, :], bass.IndirectOffsetOnAxis(ap=b.src_x[:, 0:1], axis=0)).then_inc(s.rows_in, 16)
            pool.indirect_dma_start(b.at_dst[:, 0:3 * H], None, d.q_split[:, :], bass.IndirectOffsetOnAxis(ap=b.dst_x[:, 0:1], axis=0)).then_inc(s.rows_in, 16)
            scatter_tile(pool, s, b, t, acc)
        each_tile(pool, tile)

    def tensor(pe):
        def tile(t, g, j):
            pe.wait_ge(s.attr_in, 16 * (t + 1))
            pe.matmul(ps[:, 0, 0:H], b.attr[:, :], m.w1[:, 2 * H:3 * H], start=True, stop=True).then_inc(s.z_ps, 1)
            pe.wait_ge(s.vals_ready, t + 1)
            pe.wait_ge(s.own, STEPS * (t + 1))
            pe.matmul(ps[:, 1, 0:AW], b.same[:, :], b.vals[:, :], start=True, stop=True).then_inc(s.sums_ps, 1)
            pe.wait_ge(s.added, 16 * (t + 1))
        each_tile(pe, tile)
        with pe.Fori(0, NT) as t:
            pe.wait_ge(s.node_in, 16 * (t + 1))
            pe.transpose(ps[:, 2, 0:P], b.node_sums[:, 0:H], m.ident[:, :])
            pe.transpose(ps[0:1, 3, 0:P], b.node_sums[:, H:AW], m.ident[:, :]).then_inc(s.node_ps, 1)
            pe.wait_ge(s.node_moved, 2 * (t + 1))

    def scalar(act):
        def tile(t, g, j):
            act.wait_ge(s.z_ready, t + 1)
            act.activation(b.vals[:, 0:H], b.z[:, :], ACT.Silu).then_inc(s.vals_ready, 1)
            act.wait_ge(s.added, 16 * (t + 1))
        each_tile(act, tile)

    def vector(dve):
        def tile(t, g, j):
            own = Chain(dve, s.own, STEPS * t)
            own.did(dve.memset(b.vals[:, H:AW], 1.0))
            dve.wait_ge(s.rows_in, 32 * (t + 1))
            join_three(dve, own, b.at_dst[:, :], H, b.z[:, :])
            own.then(dve.tensor_tensor(b.z[:, :], b.z[:, :], b.p_src[:, :], ALU.add))
            dve.wait_ge(s.z_ps, t + 1)
            dve.tensor_tensor(b.z[:, :], b.z[:, :], ps[:, 0, 0:H], ALU.add).then_inc(s.z_ready, 1)
            combine_indices(dve, m, s, b, own, t, m.dst_c)
            own.then(dve.memset(b.away[:, :], 0.0))
            dve.wait_ge(s.sums_ps, t + 1)
            dve.tensor_copy(b.sums[:, :], ps[:, 1, 0:AW]).then_inc(s.sums_moved, 1)
            dve.wait_ge(s.added, 16 * (t + 1))
        each_tile(dve, tile)
        with dve.Fori(0, NT) as t:
            dve.wait_ge(s.node_ps, t + 1)
            dve.tensor_copy(cols(m.aggT, t * P, P), ps[:, 2, 0:P]).then_inc(s.node_moved, 1)
            dve.tensor_copy(cols(m.degree, t * P, P), ps[0:1, 3, 0:P]).then_inc(s.node_moved, 1)
            dve.wait_ge(s.node_moved, 2 * (t + 1))
    return sync, gpsimd, tensor, scalar, vector


def edges_two_general(nc, d, m, ps, s, b):
    acc = d.acc[0]
    STEPS = TAIL + 6

    def sync(sp):
        def tile(t, g, j):
            sp.dma_start(b.key_i[:, :], rows(d.src, t * P, P).partition_broadcast(P)).then_inc(s.key_in, 16)
            sp.wait_ge(s.added, 16 * (t + 1))
            passed(sp, s.sp_passed)
        each_tile(sp, tile)

    def gpsimd(pool):
        def tile(t, g, j):
            pool.tensor_copy(b.src_x[:, :], cols(m.src_i, t, 1)).then_inc(s.idx_ready, 1)
            pool.tensor_copy(b.dst_x[:, :], cols(m.dst_i, t, 1)).then_inc(s.idx_ready, 1)
            pool.wait_ge(s.idx_ready, 2 * (t + 1))
            passed(pool, s.passed)
            pool.indirect_dma_start(b.at_src[:, :], None, d.w_split[:, :], bass.IndirectOffsetOnAxis(ap=b.src_x[:, 0:1], axis=0)).then_inc(s.rows_in, 16)
            pool.indirect_dma_start(b.at_dst[:, :], None, d.w_split[:, :], bass.IndirectOffsetOnAxis(ap=b.dst_x[:, 0:1], axis=0)).then_inc(s.rows_in, 16)
            scatter_tile(pool, s, b, t, acc)
        each_tile(pool, tile)

    def tensor(pe):
        def tile(t, g, j):
            pe.wait_ge(s.z_ready, t + 1)
            pe.matmul(ps[:, 1, 0:AW], b.same[:, :], b.vals[:, :], start=True, stop=True).then_inc(s.sums_ps, 1)
            pe.wait_ge(s.added, 16 * (t + 1))
        each_tile(pe, tile)

    def scalar(act):
        def tile(t, g, j):
            act.wait_ge(s.own, STEPS * t + 6)
            act.activation(b.vals[:, H:AW], b.leaky[:, :], ACT.Exp, scale=-1.0).then_inc(s.vals_ready, 1)
            act.wait_ge(s.added, 16 * (t + 1))
        each_tile(act, tile)

    def vector(dve):
        def tile(t, g, j):
            own = Chain(dve, s.own, STEPS * t)
            dve.wait_ge(s.rows_in, 32 * (t + 1))
            join_three(dve, own, b.at_dst[:, :], WW, b.dst_row[:, :])
            join_three(dve, own, b.at_src[:, :], WW, b.src_row[:, :])
            own.then(dve.tensor_tensor(b.score[:, :], b.dst_row[:, H:H + 1], b.src_row[:, H + 1:H + 2], ALU.add))
            own.then(dve.scalar_tensor_tensor(b.leaky[:, :], b.score[:, :], ALPHA, b.score[:, :], ALU.mult, ALU.max))
            combine_indices(dve, m, s, b, own, t, m.src_c)
            dve.wait_ge(s.vals_ready, t + 1)
            dve.tensor_scalar(b.vals[:, 0:H], b.dst_row[:, 0:H], b.vals[:, H:AW], None, ALU.mult).then_inc(s.z_ready, 1)
            dve.wait_ge(s.sums_ps, t + 1)
            dve.tensor_copy(b.sums[:, :], ps[:, 1, 0:AW]).then_inc(s.sums_moved, 1)
            dve.wait_ge(s.added, 16 * (t + 1))
        each_tile(dve, tile)
    return sync, gpsimd, tensor, scalar, vector


def branch(nc, m, fast, general):
    with nc.Block() as block:
        def both(n):
            def program(eng):
                fits = eng.value_load(m.fits[0:1, 0:1], min_val=0, max_val=1)
                with eng.If(fits == 1):
                    fast[n](eng)
                with eng.Else():
                    general[n](eng)
            return program
        block.sync(both(0))
        block.gpsimd(both(1))
        block.tensor(both(2))
        block.scalar(both(3))
        block.vector(both(4))


def edges_one(nc, d, m, ps):
    with ExitStack() as ctx:
        s = signals(nc, ctx, "e1", "rows_in*2 attr_in*2 window_in*2 idx_ready gathered*2 rel_ps src_ps z_ps agg_ps oneT_ready counted"
                    " one_ready z_ready silu_ready deg_added agg_added rows_chosen passed")
        b = buffers(nc, ctx, "e1", rows3=([3, GROUP], BF16, 2), attr=([P, GROUP], F32, 2), window=([P, 3 * H], BF16, 2),
                    gathered=([P, SUB * H], F32, 2), idx=([P, SUB], I32, 2), oneT=([P, HALF], BF16, 2), one=([P, HALF], F32, 2),
                    z=([P, HALF], F32, 2), silu=([P, HALF], F32, 2), junk=([P, HALF], F32))
        sg = signals(nc, ctx, "e1g", GENERAL)
        bg = general_buffers(nc, ctx, "e1g")
        branch(nc, m, edges_one_fast(nc, d, m, ps, s, b), edges_one_general(nc, d, m, ps, sg, bg))


def node_pass_two(nc, d, m, ps):
    with ExitStack() as ctx:
        s = signals(nc, ctx, "n2", "x_in*2 agg_ps agg_moved pre_ps mid_ready new_ps y_ready normed gammaed biased x1_ready x1_kept shifted relued"
                    " hT_ps hT_moved wh_ps high rest mid low score_kept ws_out*2")
        sa, sb = signals(nc, ctx, "n2a", NORM), signals(nc, ctx, "n2b", NORM)
        na, nb = norm_buffers(nc, ctx, "n2a"), norm_buffers(nc, ctx, "n2b")
        b = buffers(nc, ctx, "n2", x=([P, CW], F32, 2), msg=([P, CW], F32, 2), mid=([P, CW], F32, 2), y=([P, CW], F32, 2),
                    xn=([P, CW], F32, 2), x1=([P, CW], F32, 2), shift=([P, CT], F32, 2), h=([P, CW], F32, 2), hT=([P, CW], F32, 2),
                    rest=([P, CT * WW], F32, 2), ws=([P, 3 * CT * WW], BF16, 2))
        bank2 = [ps[:, 2 * n:2 * n + 2, :].rearrange("p b c -> p (b c)") for n in range(4)]
        one_ps, two_ps = bank2[0:2], bank2[2:4]
        slices = [(0, 512), (512, CW - 512)]
        where = [(t // 3) * 512 + (t % 3) * WW for t in range(CT)]
        spans = [(0, 0, 3), (512, 3, 2)]

        def wh_view(u, bank, n):
            return tiles(two_ps[u][:, bank:bank + n * WW], WW)

        def rest_view(u, t, n):
            return tiles(b.rest[u][:, t * WW:(t + n) * WW], WW)

        def part_view(u, part, t, n):
            return tiles(b.ws[u][:, :], 3 * WW)[:, t:t + n, part * WW:(part + 1) * WW]
        block = ctx.enter_context(nc.Block())

        @block.sync
        def _(sp):
            def load(k, u):
                wait(sp, s.x1_ready, k - 1)
                sp.dma_start(tiles(b.x[u][:, :]), chunk_rows(d.x, k)).then_inc(s.x_in[u], 16)

            def turn(i):
                if not (isinstance(i, int) and i == NC // 2 - 1):
                    for u in range(2):
                        load(2 * i + u + 2, u)
                for u in range(2):
                    k = 2 * i + u
                    wait(sp, s.low, 2 * (k + 1))
                    sp.dma_start(chunk_rows(d.w_split, k), tiles(b.ws[u][:, :], 3 * WW)).then_inc(s.ws_out[u], 16)
            load(0, 0)
            load(1, 1)
            turn_pairs(sp, turn)
            for u in range(2):
                sp.wait_ge(s.ws_out[u], 16 * NC // 2)

        @block.tensor
        def _(pe):
            def turn(i):
                for u in range(2):
                    k = 2 * i + u
                    wait(pe, s.hT_moved, k - 1)
                    for c, n in slices:
                        pe.matmul(one_ps[u][:, c:c + n], m.w2[:, :], cols(m.aggT, k * CW + c, n), start=True, stop=False)
                        ins = pe.matmul(one_ps[u][:, c:c + n], m.b2_row[:, :], cols(m.degree, k * CW + c, n), start=False, stop=True)
                    ins.then_inc(s.agg_ps, 1)
                for u in range(2):
                    k = 2 * i + u
                    wait(pe, s.rest, 2 * (k - 1))
                    wait(pe, s.score_kept, 2 * (k - 1))
                    for c, n in slices:
                        pe.matmul(two_ps[u][:, c:c + n], m.u1[:, 0:H], cols(m.hT, k * CW + c, n), start=True, stop=False)
                        if c == 0:
                            wait(pe, s.agg_moved, k + 1)
                        ins = pe.matmul(two_ps[u][:, c:c + n], m.u1[:, H:2 * H], b.msg[u][:, c:c + n], start=False, stop=True)
                    ins.then_inc(s.pre_ps, 1)
                for u in range(2):
                    k = 2 * i + u
                    wait(pe, s.mid_ready, k + 1)
                    for t in range(CT):
                        out = one_ps[u][:, t * H:(t + 1) * H]
                        pe.matmul(out, b.mid[u][:, t * P:(t + 1) * P], m.u2[:, :], start=True, stop=False)
                        ins = pe.matmul(out, m.ones_row[:, :], m.ub2_row[:, :], start=False, stop=True)
                    ins.then_inc(s.new_ps, 1)
                for u in range(2):
                    k = 2 * i + u
                    wait(pe, s.relued, CT * (k + 1))
                    for t in range(CT):
                        ins = pe.transpose(one_ps[u][:, t * P:(t + 1) * P], b.h[u][:, t * H:(t + 1) * H], m.ident[:, :])
                    ins.then_inc(s.hT_ps, 1)
                for u in range(2):
                    k = 2 * i + u
                    wait(pe, s.hT_moved, k + 1)
                    for t in range(CT):
                        ins = pe.matmul(two_ps[u][:, where[t]:where[t] + WW], b.hT[u][:, t * P:(t + 1) * P], m.l1wx[:, :], start=True, stop=True)
                    ins.then_inc(s.wh_ps, 1)
            turn_pairs(pe, turn)

        @block.scalar
        def _(act):
            def turn(i):
                for u in range(2):
                    k = 2 * i + u
                    wait(act, s.agg_ps, k + 1)
                    wait(act, s.pre_ps, k - 1)
                    act.activation(b.msg[u][:, :], one_ps[u][:, 0:CW], ACT.Copy).then_inc(s.agg_moved, 1)
                for u in range(2):
                    k = 2 * i + u
                    wait(act, s.pre_ps, k + 1)
                    wait(act, s.new_ps, k - 1)
                    act.activation(b.mid[u][:, :], two_ps[u][:, 0:CW], ACT.Silu, bias=m.ub1_col[:, :]).then_inc(s.mid_ready, 1)
                for u in range(2):
                    k = 2 * i + u
                    wait(act, s.shifted, k + 1)
                    wait(act, s.hT_ps, k - 1)
                    for t in range(CT):
                        act.activation(b.h[u][:, t * H:(t + 1) * H], b.x1[u][:, t * H:(t + 1) * H], ACT.Relu,
                                       bias=b.shift[u][:, t:t + 1], scale=nb.inv[u][:, t:t + 1]).then_inc(s.relued, 1)
                for u in range(2):
                    k = 2 * i + u
                    wait(act, s.hT_ps, k + 1)
                    wait(act, s.wh_ps, k - 1)
                    act.activation(b.hT[u][:, :], one_ps[u][:, 0:CW], ACT.Copy).then_inc(s.hT_moved, 1)
                for u in range(2):
                    k = 2 * i + u
                    wait(act, s.wh_ps, k + 1)
                    wait(act, s.ws_out[u], 16 * i)
                    for bank, t, n in spans:
                        act.activation(part_view(u, 0, t, n), wh_view(u, bank, n), ACT.Copy).then_inc(s.high, 1)
                for u in range(2):
                    k = 2 * i + u
                    for n, (bank, t, count) in enumerate(spans):
                        wait(act, s.rest, 2 * k + n + 1)
                        act.activation(part_view(u, 1, t, count), rest_view(u, t, count), ACT.Copy).then_inc(s.mid, 1)
            turn_pairs(act, turn)

        @block.gpsimd
        def _(pool):
            def turn(i):
                for u in range(2):
                    k = 2 * i + u
                    wait(pool, s.x_in[u], 16 * (i + 1))
                    wait(pool, s.x1_ready, k - 1)
                    pool.tensor_tensor(tiles(b.x[u][:, :]), tiles(b.x[u][:, :]), over_tiles(m.beta_all[:, :], [P, CT, H]), ALU.add).then_inc(s.biased, 1)
                for u in range(2):
                    norm_root(pool, m, sa, na, 2 * i + u, u)
                for u in range(2):
                    norm_root(pool, m, sb, nb, 2 * i + u, u)
                for u in range(2):
                    k = 2 * i + u
                    wait(pool, s.agg_ps, k + 1)
                    wait(pool, s.x1_ready, k + 1)
                    pool.tensor_copy(cols(m.aggT, k * CW, CW), b.x1[u][:, :]).then_inc(s.x1_kept, 1)
            turn_pairs(pool, turn)

        @block.vector
        def _(dve):
            def turn(i):
                for u in range(2):
                    k = 2 * i + u
                    wait(dve, s.new_ps, k + 1)
                    wait(dve, s.normed, CT * (k - 1))
                    dve.tensor_tensor(b.y[u][:, :], one_ps[u][:, 0:CW], cols(m.h, k * CW, CW), ALU.add).then_inc(s.y_ready, 1)
                    wait(dve, s.y_ready, k + 1)
                    norm_measure(dve, sa, na, k, u, b.y[u][:, :])
                for u in range(2):
                    k = 2 * i + u
                    wait(dve, s.x1_ready, k - 1)
                    norm_apply(dve, sa, na, k, u, b.y[u][:, :], b.xn[u][:, :], s.normed)
                    wait(dve, s.normed, CT * (k + 1))
                    xn = b.xn[u][:, :]
                    dve.tensor_tensor(tiles(xn), tiles(xn), over_tiles(m.gamma_all[:, :], [P, CT, H]), ALU.mult).then_inc(s.gammaed, 1)
                    wait(dve, s.gammaed, k + 1)
                    wait(dve, s.biased, k + 1)
                    wait(dve, s.x1_kept, k - 1)
                    wait(dve, s.relued, CT * (k - 1))
                    dve.tensor_tensor(b.x1[u][:, :], xn, b.x[u][:, :], ALU.add).then_inc(s.x1_ready, 1)
                    wait(dve, s.x1_ready, k + 1)
                    norm_measure(dve, sb, nb, k, u, b.x1[u][:, :])
                for u in range(2):
                    k = 2 * i + u
                    wait(dve, sb.rooted, k + 1)
                    dve.scalar_tensor_tensor(b.shift[u][:, :], tiles(nb.mv[u][:, :], 2)[:, :, 0], -1.0, nb.inv[u][:, :],
                                             ALU.mult, ALU.mult).then_inc(s.shifted, 1)
                for u in range(2):
                    k = 2 * i + u
                    wait(dve, s.low, 2 * (k - 1))
                    for n, (bank, t, count) in enumerate(spans):
                        wait(dve, s.high, 2 * k + 2)
                        dve.tensor_tensor(rest_view(u, t, count), wh_view(u, bank, count), part_view(u, 0, t, count), ALU.subtract).then_inc(s.rest, 1)
                        dve.tensor_copy(cols(m.s_src, k * CT + t, count), wh_view(u, bank, count)[:, :, WW - 1]).then_inc(s.score_kept, 1)
                for u in range(2):
                    k = 2 * i + u
                    for n, (bank, t, count) in enumerate(spans):
                        wait(dve, s.mid, 2 * k + n + 1)
                        dve.tensor_tensor(part_view(u, 2, t, count), rest_view(u, t, count), part_view(u, 1, t, count), ALU.subtract).then_inc(s.low, 1)
            turn_pairs(dve, turn)


def edges_two_fast(nc, d, m, ps, s, b):
    rel_ps, lo_ps, src_ps, score_ps = ps[:, 0, :], ps[:, 1, :], ps[:, 2, :], ps[:, 3, 0:HS * NT]
    s_dst_ps = ps[:, 3, HS * NT:HS * NT + HS * 3]
    wh_ps = [ps[:, 4, :], ps[:, 5, :]]
    sums_ps = ps[:, 6:8, 0:2 * AW]

    def sync(sp):
        def turn(i):
            for u in range(2):
                g = 2 * i + u
                wait(sp, s.wh_ps, 2 * (g - 1))
                wait(sp, s.src_ps, 2 * (g - 1))
                sp.dma_start(b.rows3[u][:, :], rows(d.edge_rows, g, 1).rearrange("o r e -> (o r) e")).then_inc(s.rows_in[u], 16)
                first = sp.value_load(cols(m.first_row, g, 1), min_val=0, max_val=N)
                sp.dma_start(b.window[u][:, :], rows(d.w_split, first, P)).then_inc(s.window_in[u], 16)
        turns(sp, G // 2, turn)

    def gpsimd(pool):
        def turn(i):
            for u in range(2):
                g = 2 * i + u
                pool.wait_ge(s.idx_ready, g + 1)
                for j in range(SUB):
                    w, a = j // HS, j % HS
                    h = 2 * g + w
                    if a == 0:
                        pool.wait_ge(s.sums_moved, h + 1)
                    wait(pool, s.added[a], 16 * h)
                    passed(pool, s.passed)
                    pool.indirect_dma_start(d.acc[a][:, :], bass.IndirectOffsetOnAxis(ap=b.idx[u][:, j:j + 1], axis=0),
                                            b.sums[w][:, a * AW:(a + 1) * AW], None, compute_op=ALU.add).then_inc(s.added[a], 16)
        turns(pool, G // 2, turn)
        for a in range(NACC):
            pool.wait_ge(s.added[a], 16 * NH)

    def tensor(pe):
        def broadcast(h, u, w, i):
            if w == 0:
                wait(pe, s.rows_in[u], 16 * (i + 1))
            half = b.rows3[u][:, w * HALF:(w + 1) * HALF]
            wait(pe, s.oneT_ready, h)
            pe.matmul(rel_ps, m.pick[0:3, 2 * P:3 * P], half, start=True, stop=True).then_inc(s.rel_ps, 1)
            wait(pe, s.loT_ready, h)
            pe.matmul(lo_ps, m.pick[0:3, P:2 * P], half, start=True, stop=True).then_inc(s.lo_ps, 1)
            wait(pe, s.same_ready, h)
            pe.matmul(src_ps, m.pick[0:3, 3 * P:4 * P], half, start=True, stop=True).then_inc(s.src_ps, 1)

        def combine(h, v):
            wait(pe, s.same_ready, h + 1)
            wait(pe, s.vals_ready, h + 1)
            wait(pe, s.sums_moved, h)
            for j in range(HS):
                ins = pe.matmul(sums_ps[:, j // 2, (j % 2) * AW:(j % 2 + 1) * AW], b.same[v][:, j * P:(j + 1) * P],
                                b.vals[v][:, j * AW:(j + 1) * AW], start=True, stop=True)
            ins.then_inc(s.sums_ps, 1)

        def turn(i):
            for q in range(4):
                h, u, w, v = 4 * i + q, q // 2, q % 2, q % 2
                if not (isinstance(i, int) and h == NH - 1):
                    broadcast(h + 1, (q + 1) // 2 % 2, 1 - w, i + (q + 1) // 4)
                if w == 0:
                    wait(pe, s.window_in[u], 16 * (i + 1))
                wait(pe, s.oneT_ready, h + 1)
                wait(pe, s.loT_ready, h + 1)
                wait(pe, s.scored, 2 * h)
                for j in range(HS):
                    for part in range(3):
                        pe.matmul(score_ps[:, j * NT:(j + 1) * NT], b.loT[v][:, j * P:(j + 1) * P],
                                  b.s_src[:, part * NT:(part + 1) * NT], start=(part == 0), stop=(part == 2))
                s_dst = tiles(b.window[u][:, :], WW)[:, :, H]
                for j in range(HS):
                    ins = pe.matmul(s_dst_ps[:, j * 3:(j + 1) * 3], b.oneT[v][:, j * P:(j + 1) * P], s_dst, start=True, stop=True)
                ins.then_inc(s.score_ps, 1)
                wait(pe, s.vals_ready, h - 1)
                for j in range(HS):
                    for part in range(3):
                        ins = pe.matmul(wh_ps[v][:, j * H:(j + 1) * H], b.oneT[v][:, j * P:(j + 1) * P],
                                        b.window[u][:, part * WW:part * WW + H], start=(part == 0), stop=(part == 2))
                ins.then_inc(s.wh_ps, 1)
                if not (isinstance(i, int) and h == 0):
                    combine(h - 1, 1 - v)
        broadcast(0, 0, 0, 0)
        wait(pe, s.table_split, 5)
        turns(pe, G // 2, turn)
        combine(NH - 1, 1)

    def scalar(act):
        def place_indices(g, u):
            act.activation(b.idx[u][:, :], cols(m.to_i, g * SUB, SUB), ACT.Copy).then_inc(s.idx_ready, 1)

        def move_sums(h, v):
            wait(act, s.sums_ps, h + 1)
            for a in range(NACC):
                wait(act, s.added[a], 16 * (h - 1))
            act.activation(b.sums[v][:, :].rearrange("p (b c) -> p b c", b=2), sums_ps, ACT.Copy).then_inc(s.sums_moved, 1)

        def turn(i):
            for q in range(4):
                h, v = 4 * i + q, q % 2
                wait(act, s.scored, 2 * (h + 1))
                wait(act, s.vals_ready, h - 1)
                act.activation(b.weight[v][:, :], b.leaky[v][:, :], ACT.Exp, scale=-1.0).then_inc(s.weighed, 1)
                wait(act, s.weighed, h + 1)
                wait(act, s.wh_ps, h + 1)
                wait(act, s.sums_ps, h - 1)
                for j in range(HS):
                    act.activation(b.vals[v][:, j * AW:j * AW + H], wh_ps[v][:, j * H:(j + 1) * H], ACT.Copy,
                                   scale=b.weight[v][:, j:j + 1]).then_inc(s.val_parts, 1)
                act.activation(tiles(b.vals[v][:, :], AW)[:, :, H], b.weight[v][:, :], ACT.Copy).then_inc(s.val_parts, 1)
                wait(act, s.val_parts, (HS + 1) * (h + 1))
                act.nop().then_inc(s.vals_ready, 1)
                if not (isinstance(i, int) and h == 0):
                    move_sums(h - 1, 1 - v)
                if q % 2 == 0 and not (isinstance(i, int) and h < 4):
                    place_indices(2 * i + q // 2, q // 2)
        place_indices(0, 0)
        place_indices(1, 1)
        turns(act, G // 2, turn)
        move_sums(NH - 1, 1)

    def vector(dve):
        def one_hots(h, v):
            wait(dve, s.rel_ps, h + 1)
            wait(dve, s.wh_ps, h - 1)
            dve.tensor_scalar(b.oneT[v][:, :], rel_ps, m.iota_p[:, :], None, ALU.is_equal).then_inc(s.oneT_ready, 1)
            wait(dve, s.lo_ps, h + 1)
            dve.tensor_scalar(b.loT[v][:, :], lo_ps, m.iota_p[:, :], None, ALU.is_equal).then_inc(s.loT_ready, 1)

        def find_same(h, v, c):
            wait(dve, s.src_ps, h + 1)
            wait(dve, s.sums_ps, h - 1)
            dve.tensor_tensor(tiles(b.same[v][:, :]), tiles(src_ps), wide(cols(m.src_c, c, HS), [P, HS, P]),
                              ALU.is_equal).then_inc(s.same_ready, 1)

        def pick_scores(h, v, c):
            wait(dve, s.score_ps, h + 1)
            wait(dve, s.picked, (HS + 1) * h)
            wait(dve, s.scored, 2 * h)
            dve.tensor_reduce(b.s_dst[:, :], tiles(s_dst_ps, 3), X, ALU.add).then_inc(s.picked, 1)
            for j in range(HS):
                dve.scalar_tensor_tensor(b.junk[:, j * NT:(j + 1) * NT], m.iota_n[:, 0:NT], cols(m.hi_c, c + j, 1),
                                         score_ps[:, j * NT:(j + 1) * NT], ALU.is_equal, ALU.mult,
                                         accum_out=b.score[v][:, j:j + 1]).then_inc(s.picked, 1)
            wait(dve, s.picked, (HS + 1) * (h + 1))
            dve.tensor_tensor(b.score[v][:, :], b.score[v][:, :], b.s_dst[:, :], ALU.add).then_inc(s.scored, 1)
            wait(dve, s.scored, 2 * h + 1)
            wait(dve, s.weighed, h - 1)
            dve.scalar_tensor_tensor(b.leaky[v][:, :], b.score[v][:, :], ALPHA, b.score[v][:, :], ALU.mult, ALU.max).then_inc(s.scored, 1)

        def turn(i):
            for q in range(4):
                h, v = 4 * i + q, q % 2
                last = isinstance(i, int) and h == NH - 1
                if not last:
                    one_hots(h + 1, 1 - v)
                pick_scores(h, v, h * HS)
                if not last:
                    find_same(h + 1, 1 - v, (h + 1) * HS)
        split = Chain(dve, s.table_split)
        split.then(dve.tensor_copy(b.s_src[:, 0:NT], m.s_src[:, :]))
        split.then(dve.tensor_tensor(b.rest[:, :], m.s_src[:, :], b.s_src[:, 0:NT], ALU.subtract))
        split.then(dve.tensor_copy(b.s_src[:, NT:2 * NT], b.rest[:, :]))
        split.then(dve.tensor_tensor(b.rest[:, :], b.rest[:, :], b.s_src[:, NT:2 * NT], ALU.subtract))
        split.did(dve.tensor_copy(b.s_src[:, 2 * NT:], b.rest[:, :]))
        one_hots(0, 0)
        find_same(0, 0, 0)
        turns(dve, G // 2, turn)
    return sync, gpsimd, tensor, scalar, vector


def edges_two(nc, d, m, ps):
    with ExitStack() as ctx:
        s = signals(nc, ctx, "e2", "rows_in*2 window_in*2 idx_ready added*4 rel_ps lo_ps src_ps score_ps wh_ps sums_ps oneT_ready loT_ready"
                    " same_ready picked scored weighed val_parts vals_ready sums_moved table_split passed")
        b = buffers(nc, ctx, "e2", rows3=([3, GROUP], BF16, 2), window=([P, 3 * WW], BF16, 2), idx=([P, SUB], I32, 2),
                    oneT=([P, HALF], BF16, 2), loT=([P, HALF], BF16, 2), s_src=([P, 3 * NT], BF16), rest=([P, NT], F32), s_dst=([P, HS], F32), same=([P, HALF], F32, 2), junk=([P, HS * NT], F32),
                    score=([P, HS], F32, 2), leaky=([P, HS], F32, 2), weight=([P, HS], F32, 2), vals=([P, HS * AW], F32, 2),
                    sums=([P, HS * AW], F32, 2))
        sg = signals(nc, ctx, "e2g", GENERAL)
        bg = general_buffers(nc, ctx, "e2g")
        branch(nc, m, edges_two_fast(nc, d, m, ps, s, b), edges_two_general(nc, d, m, ps, sg, bg))


def node_pass_three(nc, d, m):
    with ExitStack() as ctx:
        s = signals(nc, ctx, "n3", "acc_in*2 added01 added23 summed totalled inverted divided below powered above elued out_ready out_done*2")
        b = buffers(nc, ctx, "n3", acc=([P, NACC * CT * AW], F32, 2), one=([P, CT * AW], F32, 2), two=([P, CT * AW], F32, 2),
                    sums=([P, CT * AW], F32, 2), inv=([P, CT], F32, 2), total=([P, CT], F32, 2), mean=([P, CW], F32, 2), below=([P, CW], F32, 2),
                    power=([P, CW], F32, 2), out=([P, CW], F32, 2))
        block = ctx.enter_context(nc.Block())
        W = CT * AW

        @block.sync
        def _(sp):
            def turn(i):
                for u in range(2):
                    k = 2 * i + u
                    wait(sp, s.added01, k - 1)
                    wait(sp, s.added23, k - 1)
                    for a in range(NACC):
                        sp.dma_start(tiles(b.acc[u][:, a * W:(a + 1) * W], AW), chunk_rows(d.acc[a], k)).then_inc(s.acc_in[u], 16)
                for u in range(2):
                    k = 2 * i + u
                    wait(sp, s.out_ready, k + 1)
                    if isinstance(i, int) and k == NC - 1:
                        full, left = divmod(N - k * CW, P)
                        sp.dma_start(d.out[k * CW:k * CW + full * P].rearrange("(t p) f -> p t f", p=P),
                                     tiles(b.out[u][:, 0:full * H])).then_inc(s.out_done[u], 16)
                        sp.dma_start(d.out[k * CW + full * P:N], b.out[u][0:left, full * H:(full + 1) * H]).then_inc(s.out_done[u], 16)
                    else:
                        sp.dma_start(chunk_rows(d.out, k), tiles(b.out[u][:, :])).then_inc(s.out_done[u], 16)
            turn_pairs(sp, turn)
            sp.wait_ge(s.out_done[0], 16 * (NC // 2))
            sp.wait_ge(s.out_done[1], 16 * (NC // 2 + 1))

        @block.gpsimd
        def _(pool):
            def turn(i):
                for u in range(2):
                    k = 2 * i + u
                    wait(pool, s.acc_in[u], 16 * NACC * (i + 1))
                    wait(pool, s.summed, k - 1)
                    pool.tensor_tensor(b.two[u][:, :], b.acc[u][:, 2 * W:3 * W], b.acc[u][:, 3 * W:], ALU.add).then_inc(s.added23, 1)
            turn_pairs(pool, turn)

        @block.vector
        def _(dve):
            def turn(i):
                for u in range(2):
                    k = 2 * i + u
                    wait(dve, s.acc_in[u], 16 * NACC * (i + 1))
                    wait(dve, s.summed, k - 1)
                    dve.tensor_tensor(b.one[u][:, :], b.acc[u][:, 0:W], b.acc[u][:, W:2 * W], ALU.add).then_inc(s.added01, 1)
                    wait(dve, s.added01, k + 1)
                    wait(dve, s.added23, k + 1)
                    wait(dve, s.divided, k - 1)
                    dve.tensor_tensor(b.sums[u][:, :], b.one[u][:, :], b.two[u][:, :], ALU.add).then_inc(s.summed, 1)
                    wait(dve, s.summed, k + 1)
                    wait(dve, s.inverted, k - 1)
                    dve.tensor_tensor(b.total[u][:, :], tiles(b.sums[u][:, :], AW)[:, :, H], cols(m.no_node, k * CT, CT), ALU.add).then_inc(s.totalled, 1)
                    wait(dve, s.totalled, k + 1)
                    dve.reciprocal(b.inv[u][:, :], b.total[u][:, :]).then_inc(s.inverted, 1)
                    wait(dve, s.inverted, k + 1)
                    wait(dve, s.above, k - 1)
                    dve.tensor_tensor(tiles(b.mean[u][:, :]), tiles(b.sums[u][:, :], AW)[:, :, 0:H],
                                      wide(b.inv[u][:, :], [P, CT, H]), ALU.mult).then_inc(s.divided, 1)
                    wait(dve, s.divided, k + 1)
                    wait(dve, s.powered, k - 1)
                    dve.tensor_scalar(b.below[u][:, :], b.mean[u][:, :], 0.0, None, ALU.min).then_inc(s.below, 1)
                for u in range(2):
                    k = 2 * i + u
                    wait(dve, s.powered, k + 1)
                    wait(dve, s.out_done[u], 16 * i)
                    dve.scalar_tensor_tensor(b.out[u][:, :], b.mean[u][:, :], 0.0, b.power[u][:, :], ALU.max, ALU.add).then_inc(s.above, 1)
                    wait(dve, s.above, k + 1)
                    dve.scalar_tensor_tensor(b.out[u][:, :], b.out[u][:, :], -1.0, cols(m.aggT, k * CW, CW), ALU.add, ALU.add).then_inc(s.out_ready, 1)
            turn_pairs(dve, turn)

        @block.scalar
        def _(act):
            def turn(i):
                for u in range(2):
                    k = 2 * i + u
                    wait(act, s.below, k + 1)
                    wait(act, s.above, k - 1)
                    act.activation(b.power[u][:, :], b.below[u][:, :], ACT.Exp).then_inc(s.powered, 1)
            turn_pairs(act, turn)


def program(nc, given):
    tables = {}
    for name, shape, dtype in (("p_table", [ROWS, H], F32), ("q_split", [ROWS, 3 * H], BF16),
                               ("w_split", [ROWS, 3 * WW], BF16), ("edge_rows", [G, 3, GROUP], BF16)):
        tables[name] = nc.dram_tensor(name, shape, dtype, kind="Internal").ap()
    tables["acc"] = [nc.dram_tensor(f"acc{a}", [ROWS, AW], F32, kind="Internal").ap() for a in range(NACC + 1)]
    d = named("Dram", {**given, **tables})
    with ExitStack() as ctx:
        ps = ctx.enter_context(nc.psum_tensor("ps", [P, 8, 512], F32))
        m = buffers(nc, ctx, "all", h=([P, ROWS], F32), hT=([P, ROWS], F32), aggT=([P, ROWS], F32), degree=([1, ROWS], F32),
                    w1=([P, 3 * H], F32), w2=([P, H], F32), u1=([P, 2 * H], F32), u2=([P, H], F32), l1wx=([P, WW], F32),
                    b1_row=([1, H], F32), minus_half=([P, CT], F32), gamma_all=([P, H], F32), beta_all=([P, H], F32), ub1_col=([P, 1], F32),
                    b2_row=([1, H], F32), ub2_row=([1, H], F32), ones_row=([1, P], F32), ones_bf=([P, 1], BF16),
                    iota_n=([P, P], F32), iota_p=([P, 1], F32), before=([P, P], F32), ident=([P, P], F32), dump=([P, 1], F32),
                    pick=([3, 4 * P], BF16), first_row=([1, G], I32), fits=([1, 1], I32), src_c=([P, G * SUB], F32),
                    hi_c=([P, G * SUB], F32), dst_c=([P, G * SUB], F32), rel_c=([P, G * SUB], F32), src_i=([P, G * SUB], I32),
                    dst_i=([P, G * SUB], I32), repeats=([P, G * SUB], F32), to_i=([P, G * SUB], I32), s_src=([P, NT], F32), no_node=([P, NT], F32))
        prepare(nc, d, m, ps)
        node_pass_one(nc, d, m, ps)
        edges_one(nc, d, m, ps)
        node_pass_two(nc, d, m, ps)
        edges_two(nc, d, m, ps)
        node_pass_three(nc, d, m)


def kernel(**inputs):
    import numpy as np
    import concourse.bacc as bacc
    from concourse.bass_utils import run_bass_kernel_spmd

    x = np.zeros((ROWS, H), np.float32)
    x[:N] = inputs["x"]
    attr = np.zeros((G * GROUP, H), np.float32)
    attr[:E] = inputs["edge_attr_128"]
    ends = {}
    for name in ("src", "dst"):
        ends[name] = np.full(G * GROUP, N, np.int32)
        ends[name][:E] = inputs[name]
    arrays = {
        "x": x, "src": ends["src"], "dst": ends["dst"],
        "attrT": np.ascontiguousarray(attr.reshape(G, GROUP, H).transpose(0, 2, 1)),
        "w1": inputs["L0_gnn_msg_W1"], "b1": inputs["L0_gnn_msg_b1"], "w2": inputs["L0_gnn_msg_W2"], "b2": inputs["L0_gnn_msg_b2"],
        "u1": inputs["L0_gnn_upd_W1"], "ub1": inputs["L0_gnn_upd_b1"], "u2": inputs["L0_gnn_upd_W2"], "ub2": inputs["L0_gnn_upd_b2"],
        "gamma": inputs["L0_gnn_ln_gamma"], "beta": inputs["L0_gnn_ln_beta"], "l1w": inputs["L1_gnn_W"], "a": inputs["L1_gnn_a"],
    }
    arrays = {name: np.ascontiguousarray(a) for name, a in arrays.items()}
    nc = bacc.Bacc("TRN2", target_bir_lowering=False, num_devices=1)
    d = {name: nc.dram_tensor(f"in_{name}", a.shape, mybir.dt.from_np(a.dtype), kind="ExternalInput").ap()
         for name, a in arrays.items()}
    d["out"] = nc.dram_tensor("out", (N, H), F32, kind="ExternalOutput").ap()
    program(nc, d)
    return run_bass_kernel_spmd(nc, [{f"in_{name}": a for name, a in arrays.items()}], core_ids=[0]).results[0]["out"]
```

```python
import concourse.bass as bass
from concourse import mybir
from concourse.alu_op_type import AluOpType as ALU
from contextlib import ExitStack
from collections import namedtuple

N, E, H = 6250, 106250, 128
P = 128
GROUP = 1024
G = -(-E // GROUP)
SUB = GROUP // P
HALF = GROUP // 2
HS = SUB // 2
NH = 2 * G
NT = 50
ROWS = NT * P
CT = 5
CW = CT * P
NC = NT // CT
DUMP = N + 1
NACC = 4
AW = H + 1
WW = H + 2
EPS = 1e-5
ALPHA = 0.2

F32, BF16, I32 = mybir.dt.float32, mybir.dt.bfloat16, mybir.dt.int32
ACT = mybir.ActivationFunctionType
X = mybir.AxisListType.X


def wait(eng, sem, value):
    if isinstance(value, int) and value <= 0:
        return
    eng.wait_ge(sem, value)


def passed(eng, sem):
    eng.sem_inc(sem, 1)


def cols(tensor, start, size):
    if isinstance(start, int):
        return tensor[:, start:start + size]
    return tensor[:, bass.ds(start, size)]


def rows(table, start, size):
    if isinstance(start, int):
        return table[start:start + size]
    return table[bass.ds(start, size)]


def wide(column, shape):
    return column.unsqueeze(2).broadcast_to(shape)


def over_tiles(row, shape):
    return row.unsqueeze(1).broadcast_to(shape)


class Chain:

    def __init__(self, eng, sem, start=0):
        self.eng, self.sem, self.start, self.n = eng, sem, start, 0

    def did(self, instruction):
        self.n += 1
        instruction.then_inc(self.sem, 1)
        return self.n

    def after(self, n=None):
        wait(self.eng, self.sem, self.start + (self.n if n is None else n))

    def then(self, instruction):
        self.did(instruction)
        self.after()


def turns(eng, count, body):
    body(0)
    with eng.Fori(1, count - 1) as i:
        body(i)
    body(count - 1)


def named(kind, things):
    return namedtuple(kind, list(things))(**things)


def signals(nc, ctx, phase, names):
    found, free = {}, []

    def clear(*_):
        nc.clear_and_free_semaphores(free)
        nc.all_engine_barrier(sem_only=True)
    ctx.callback(clear)
    for name in names.split():
        name, _, n = name.partition("*")
        if n:
            found[name] = [nc.alloc_semaphore(f"{phase}_{name}{k}") for k in range(int(n))]
        else:
            found[name] = nc.alloc_semaphore(f"{phase}_{name}")
        free += found[name] if n else [found[name]]
    return named("Signals", found)


def buffers(nc, ctx, phase, **shapes):
    found = {}
    for name, (shape, dtype, *n) in shapes.items():
        made = [ctx.enter_context(nc.sbuf_tensor(f"{phase}_{name}{k}", shape, dtype)) for k in range(n[0] if n else 1)]
        found[name] = made if n else made[0]
    return named("Buffers", found)


def tiles(ap, width=H):
    return ap.rearrange("p (t f) -> p t f", f=width)


def prepare(nc, d, m, ps):
    with ExitStack() as ctx:
        s = signals(nc, ctx, "prep", "ids_in weights_in vectors_in iotas consts own rows_ready rows_out tr_ps tr_evac bc_ps bc_used"
                    " span_ps flag_ready zeros_ready sums_zeroed acc_zeroed l1wT_ps l1wT wa_ps")
        b = buffers(nc, ctx, "prep", dst_g=([G, GROUP], I32), src_g=([G, GROUP], I32), hi_i=([G, GROUP], I32),
                    lo_i=([G, GROUP], I32), dst_f=([G, GROUP], F32), src_f=([G, GROUP], F32), hi_f=([G, GROUP], F32),
                    rel_f=([G, GROUP], F32), rows3=([G, 3 * GROUP], BF16), first=([G, 1], F32), last=([G, 1], F32),
                    span=([G, 1], F32), iota_n_i=([P, P], I32), iota_p_i=([P, 1], I32), iota_node=([P, NT], I32), node_f=([P, NT], F32), span_row=([1, G], F32),
                    vec=([1, 8 * H], F32), l1w=([P, H], F32), l1wT=([P, H], F32), w2T=([P, H], F32), acol=([P, 2], F32), b2_col=([P, 1], F32), w2=([P, H], F32),
                    b1=([3, H], F32), b1_high=([3, H], BF16), b1_mid=([3, H], BF16), b1_rest=([3, H], F32), widest=([1, 1], F32))
        VEC = ["b1", "b2", "ub1", "ub2", "gamma", "beta"]
        block = ctx.enter_context(nc.Block())

        @block.sync
        def _(sp):
            sp.dma_start(b.dst_g[:, :], d.dst.rearrange("(g e) -> g e", e=GROUP)).then_inc(s.ids_in, 16)
            sp.dma_start(b.src_g[:, :], d.src.rearrange("(g e) -> g e", e=GROUP)).then_inc(s.ids_in, 16)
            for t in range(3):
                sp.dma_start(m.w1[:, t * H:(t + 1) * H], d.w1[t * H:(t + 1) * H, :]).then_inc(s.weights_in, 16)
            for t in range(2):
                sp.dma_start(m.u1[:, t * H:(t + 1) * H], d.u1[t * H:(t + 1) * H, :]).then_inc(s.weights_in, 16)
            sp.dma_start(b.w2[:, :], d.w2).then_inc(s.weights_in, 16)
            sp.dma_start(m.u2[:, :], d.u2).then_inc(s.weights_in, 16)
            sp.dma_start(b.l1w[:, :], d.l1w).then_inc(s.weights_in, 16)
            for n, name in enumerate(VEC):
                v = {"b1": d.b1, "b2": d.b2, "ub1": d.ub1, "ub2": d.ub2, "gamma": d.gamma, "beta": d.beta}[name]
                sp.dma_start(b.vec[:, n * H:(n + 1) * H], v.rearrange("(o f) -> o f", o=1)).then_inc(s.vectors_in, 16)
            sp.dma_start(b.vec[:, 6 * H:8 * H], d.a).then_inc(s.vectors_in, 16)
            sp.wait_ge(s.zeros_ready, 1)
            sp.dma_start(d.acc[NACC].rearrange("(p r) c -> p r c", p=P), over_tiles(m.zeros[:, :], [P, NT, AW])).then_inc(s.acc_zeroed, 16)
            sp.wait_ge(s.rows_ready, 3)
            sp.dma_start(d.edge_rows.rearrange("g r e -> g (r e)"), b.rows3[:, :]).then_inc(s.rows_out, 16)
            sp.wait_ge(s.rows_out, 16)
            sp.wait_ge(s.weights_in, 16 * 8)
            sp.wait_ge(s.acc_zeroed, 16)

        @block.gpsimd
        def _(pool):
            pool.iota(b.iota_n_i[:, :], [[1, P]], base=0, channel_multiplier=0).then_inc(s.iotas, 1)
            pool.iota(b.iota_p_i[:, :], [[0, 1]], base=0, channel_multiplier=1).then_inc(s.iotas, 1)
            pool.iota(b.iota_node[:, :], [[P, NT]], base=0, channel_multiplier=1).then_inc(s.iotas, 1)
            pool.memset(m.zeros[:, :], 0.0).then_inc(s.zeros_ready, 1)
            pool.memset(m.aggT[:, :], 0.0).then_inc(s.sums_zeroed, 1)
            pool.memset(m.degree[:, :], 0.0).then_inc(s.sums_zeroed, 1)
            pool.wait_ge(s.sums_zeroed, 2)

        @block.vector
        def _(dve):
            own = Chain(dve, s.own)
            own.did(dve.memset(m.ones_row[:, :], 1.0))
            own.did(dve.memset(m.ones_bf[:, :], 1.0))
            own.did(dve.memset(m.ones_three[:, :], 1.0))
            own.did(dve.memset(m.minus_half[:, :], -0.5))
            dve.wait_ge(s.iotas, 3)
            own.then(dve.tensor_copy(b.node_f[:, :], b.iota_node[:, :]))
            own.did(dve.tensor_scalar(m.no_node[:, :], b.node_f[:, :], float(N), None, ALU.is_ge))
            own.then(dve.tensor_copy(m.iota_n[:, :], b.iota_n_i[:, :]))
            own.then(dve.tensor_copy(m.iota_p[:, :], b.iota_p_i[:, :]))
            own.did(dve.tensor_scalar(m.before[:, :], m.iota_n[:, :], m.iota_p[:, :], None, ALU.is_lt))
            own.did(dve.tensor_scalar(m.ident[:, :], m.iota_n[:, :], m.iota_p[:, :], None, ALU.is_equal))
            for n in range(3):
                own.did(dve.tensor_scalar(m.pick[0:3, n * P:(n + 1) * P], m.iota_p[0:3, :].broadcast_to([3, P]), float(n), None, ALU.is_equal))
            own.after()
            own.then(dve.scalar_tensor_tensor(m.pick[0:3, 3 * P:4 * P], m.pick[0:3, 0:P], float(P), m.pick[0:3, P:2 * P], ALU.mult, ALU.add))
            dve.tensor_scalar(m.dump[:, :], m.iota_p[:, :], float(DUMP), None, ALU.add).then_inc(s.consts, 1)
            dve.wait_ge(s.ids_in, 32)
            own.did(dve.tensor_copy(b.dst_f[:, :], b.dst_g[:, :]))
            own.did(dve.tensor_copy(b.src_f[:, :], b.src_g[:, :]))
            own.did(dve.tensor_single_scalar(b.hi_i[:, :], b.src_g[:, :], 7, ALU.logical_shift_right))
            own.then(dve.tensor_single_scalar(b.lo_i[:, :], b.src_g[:, :], P - 1, ALU.bitwise_and))
            own.did(dve.tensor_copy(b.hi_f[:, :], b.hi_i[:, :]))
            own.did(dve.tensor_reduce(b.first[:, :], b.dst_f[:, :], X, ALU.min))
            own.then(dve.tensor_reduce(b.last[:, :], b.dst_f[:, :], X, ALU.max))
            own.did(dve.tensor_tensor(b.span[:, :], b.last[:, :], b.first[:, :], ALU.subtract))
            own.then(dve.tensor_scalar(b.rel_f[:, :], b.dst_f[:, :], b.first[:, :], None, ALU.subtract))
            dve.tensor_copy(b.rows3[:, 0:GROUP], b.hi_i[:, :]).then_inc(s.rows_ready, 1)
            dve.tensor_copy(b.rows3[:, GROUP:2 * GROUP], b.lo_i[:, :]).then_inc(s.rows_ready, 1)
            dve.tensor_copy(b.rows3[:, 2 * GROUP:], b.rel_f[:, :]).then_inc(s.rows_ready, 1)
            for q, col in enumerate((m.src_c, m.hi_c, m.dst_c, m.rel_c)):
                dve.wait_ge(s.tr_ps, 2 * q + 2)
                for half in range(2):
                    got = ps[:, 2 * q + half, 0:HS * G].rearrange("p (j g) -> p j g", g=G)
                    ins = dve.tensor_copy(col[:, :].rearrange("p (g j) -> p j g", j=SUB)[:, half * HS:(half + 1) * HS, :], got)
                    ins.then_inc(s.tr_evac, 1)
            dve.wait_ge(s.tr_evac, 8)
            own.did(dve.tensor_copy(m.src_i[:, :], m.src_c[:, :]))
            own.did(dve.tensor_copy(m.dst_i[:, :], m.dst_c[:, :]))
            dve.wait_ge(s.bc_ps, 1)
            own.did(dve.tensor_copy(b.b1[:, :], ps[0:3, 7, 0:H]))
            own.did(dve.tensor_copy(m.gamma_all[:, :], ps[:, 0, H:2 * H]))
            own.did(dve.tensor_copy(m.beta_all[:, :], ps[:, 0, 2 * H:3 * H]))
            own.did(dve.tensor_copy(m.ub1_col[:, :], ps[:, 1, 0:1]))
            own.did(dve.tensor_copy(b.acol[:, :], ps[:, 1, 1:3]))
            own.did(dve.tensor_copy(b.b2_col[:, :], ps[:, 1, 3:4]))
            own.did(dve.tensor_copy(m.ub2_all[:, :], ps[:, 0, 3 * H:4 * H]))
            own.did(dve.tensor_copy(b.w2T[:, :], ps[:, 2, H:2 * H]))
            own.did(dve.tensor_copy(b.l1wT[:, :], ps[:, 2, 0:H]))
            own.did(dve.tensor_copy(m.first_row[:, :], ps[0:1, 3, 0:G]))
            own.after()
            dve.tensor_copy(b.span_row[:, :], ps[0:1, 3, G:2 * G]).then_inc(s.bc_used, 1)
            dve.wait_ge(s.bc_used, 1)
            own.then(dve.tensor_reduce(b.widest[:, :], b.span_row[:, :], X, ALU.max))
            own.did(dve.tensor_scalar(m.fits[:, :], b.widest[:, :], float(P), None, ALU.is_lt))
            own.did(dve.tensor_copy(m.l1wx[:, 0:H], b.l1w[:, :]))
            own.then(dve.tensor_copy(b.b1_high[:, :], b.b1[:, :]))
            own.then(dve.tensor_tensor(b.b1_rest[:, :], b.b1[:, :], b.b1_high[:, :], ALU.subtract))
            own.then(dve.tensor_copy(b.b1_mid[:, :], b.b1_rest[:, :]))
            own.then(dve.tensor_tensor(b.b1_rest[:, :], b.b1_rest[:, :], b.b1_mid[:, :], ALU.subtract))
            own.then(dve.tensor_scalar(b.b1[:, :], b.b1_high[:, :], m.ident[0:3, 0:1], None, ALU.mult))
            own.then(dve.scalar_tensor_tensor(b.b1[:, :], b.b1_mid[:, :], m.ident[0:3, 1:2], b.b1[:, :], ALU.mult, ALU.add))
            own.then(dve.scalar_tensor_tensor(m.b1_parts[:, :], b.b1_rest[:, :], m.ident[0:3, 2:3], b.b1[:, :], ALU.mult, ALU.add))
            dve.wait_ge(s.wa_ps, 1)
            own.did(dve.tensor_copy(m.l1wx[:, H:H + 1], ps[:, 4, 1:2]))
            own.did(dve.tensor_copy(m.l1wx[:, H + 1:H + 2], ps[:, 4, 0:1]))
            own.did(dve.tensor_copy(m.w2u[:, :], ps[:, 5, 0:H]))
            own.did(dve.tensor_copy(m.b2u_row[:, :], ps[0:1, 6, 0:H]))
            own.after()

        @block.tensor
        def _(pe):
            pe.wait_ge(s.consts, 1)
            pe.wait_ge(s.rows_ready, 3)
            for q, f in enumerate((b.src_f, b.hi_f, b.dst_f, b.rel_f)):
                for j in range(SUB):
                    out = ps[:, 2 * q + j // HS, (j % HS) * G:(j % HS + 1) * G]
                    ins = pe.transpose(out, f[:, j * P:(j + 1) * P], m.ident[0:G, 0:G])
                    if j % HS == HS - 1:
                        ins.then_inc(s.tr_ps, 1)
            pe.wait_ge(s.tr_evac, 8)
            pe.wait_ge(s.vectors_in, 16 * 7)
            pe.wait_ge(s.weights_in, 16 * 8)
            for n, v in ((1, 4), (2, 5), (3, 3)):
                pe.matmul(ps[:, 0, n * H:(n + 1) * H], m.ones_row[:, :], b.vec[:, v * H:(v + 1) * H], start=True, stop=True)
            pe.matmul(ps[0:3, 7, 0:H], m.ones_row[:, 0:3], b.vec[:, 0:H], start=True, stop=True)
            for n, v in enumerate((2, 6, 7, 1)):
                pe.matmul(ps[:, 1, n:n + 1], b.vec[:, v * H:(v + 1) * H], m.ones_row[:, 0:1], start=True, stop=True)
            pe.transpose(ps[:, 2, 0:H], b.l1w[:, :], m.ident[:, :])
            pe.transpose(ps[:, 2, H:2 * H], b.w2[:, :], m.ident[:, :])
            pe.transpose(ps[0:1, 3, 0:G], b.first[:, :], m.ident[0:G, 0:G])
            pe.transpose(ps[0:1, 3, G:2 * G], b.span[:, :], m.ident[0:G, 0:G]).then_inc(s.bc_ps, 1)
            pe.wait_ge(s.bc_used, 1)
            pe.matmul(ps[:, 4, 0:2], b.l1wT[:, :], b.acol[:, :], start=True, stop=True)
            pe.matmul(ps[:, 5, 0:H], b.w2T[:, :], m.u1[:, H:2 * H], start=True, stop=True)
            pe.matmul(ps[0:1, 6, 0:H], b.b2_col[:, :], m.u1[:, H:2 * H], start=True, stop=True).then_inc(s.wa_ps, 1)


NORM = "normable measured aggregated spread rooted"


def norm_buffers(nc, ctx, phase):
    return buffers(nc, ctx, phase, stats=([P, CT * 6], F32, 2), mv=([P, CT * 2], F32, 2), var=([P, CT], F32, 2), inv=([P, CT], F32, 2))


def norm_measure(dve, s, b, k, u, x):
    for t in range(CT):
        dve.bn_stats(b.stats[u][:, t * 6:(t + 1) * 6], x[:, t * H:(t + 1) * H]).then_inc(s.measured, 1)
    wait(dve, s.measured, CT * (k + 1))
    passed(dve, s.normable)
    for t in range(CT):
        dve.bn_aggr(b.mv[u][:, t * 2:(t + 1) * 2], b.stats[u][:, t * 6:(t + 1) * 6]).then_inc(s.aggregated, 1)
    wait(dve, s.aggregated, CT * (k + 1))
    dve.tensor_scalar(b.var[u][:, :], tiles(b.mv[u][:, :], 2)[:, :, 1], EPS, None, ALU.add).then_inc(s.spread, 1)


def norm_root(pool, m, s, b, k, u):
    wait(pool, s.spread, k + 1)
    pool.tensor_tensor(b.inv[u][:, :], b.var[u][:, :], m.minus_half[:, :], ALU.pow).then_inc(s.rooted, 1)


def norm_apply(dve, s, b, k, u, x, out, done):
    wait(dve, s.rooted, k + 1)
    for t in range(CT):
        dve.tensor_scalar(out[:, t * H:(t + 1) * H], x[:, t * H:(t + 1) * H], b.mv[u][:, 2 * t:2 * t + 1], b.inv[u][:, t:t + 1],
                          ALU.subtract, ALU.mult).then_inc(done, 1)


def chunk_rows(table, k):
    return rows(table, k * CW, CW).rearrange("(t p) f -> p t f", p=P)


def turn_pairs(eng, body):
    turns(eng, NC // 2, body)


def node_pass_one(nc, d, m, ps):
    with ExitStack() as ctx:
        s = signals(nc, ctx, "n1", NORM + " x_in*2 normed relued h_kept hT_ps hT_moved hT_kept pq_ps p_moved high rest mid low p_out*2 qs_out*2")
        nb = norm_buffers(nc, ctx, "n1")
        b = buffers(nc, ctx, "n1", x=([P, CW], F32, 2), xn=([P, CW], F32, 2), h=([P, CW], F32, 2), hT=([P, CW], F32, 2),
                    p=([P, CW], F32, 2), rest=([P, CW], F32, 2), qs=([P, 3 * CW], BF16, 2))
        hT_ps = ps[:, 0:2, :].rearrange("p b c -> p (b c)")
        pq_ps = [ps[:, n:n + 3, :].rearrange("p b c -> p (b c)") for n in (2, 5)]
        q_ps = [tiles(pq[:, 0:2 * CW], 2 * H)[:, :, H:] for pq in pq_ps]
        parts = [[tiles(b.qs[u][:, :], 3 * H)[:, :, n * H:(n + 1) * H] for n in range(3)] for u in range(2)]
        block = ctx.enter_context(nc.Block())

        @block.sync
        def _(sp):
            def load(k, u):
                wait(sp, s.normed, CT * (k - 1))
                sp.dma_start(tiles(b.x[u][:, :]), chunk_rows(d.x, k)).then_inc(s.x_in[u], 16)

            def turn(i):
                if not (isinstance(i, int) and i == NC // 2 - 1):
                    for u in range(2):
                        load(2 * i + u + 2, u)
            load(0, 0)
            load(1, 1)
            turn_pairs(sp, turn)
            for u in range(2):
                sp.wait_ge(s.p_out[u], 16 * NC // 2)
                sp.wait_ge(s.qs_out[u], 16 * NC // 2)

        @block.vector
        def _(dve):
            def measure(k, u, i):
                wait(dve, s.x_in[u], 16 * (i + 1))
                norm_measure(dve, s, nb, k, u, b.x[u][:, :])

            def apply(k, u):
                wait(dve, s.relued, k - 1)
                norm_apply(dve, s, nb, k, u, b.x[u][:, :], b.xn[u][:, :], s.normed)

            def turn(i):
                if not (isinstance(i, int) and i == NC // 2 - 1):
                    for u in range(2):
                        measure(2 * i + u + 2, u, i + 1)
                    for u in range(2):
                        apply(2 * i + u + 2, u)
                for u in range(2):
                    k = 2 * i + u
                    wait(dve, s.high, k + 1)
                    wait(dve, s.low, k - 1)
                    dve.tensor_tensor(tiles(b.rest[u][:, :]), q_ps[u], parts[u][0], ALU.subtract).then_inc(s.rest, 1)
                for u in range(2):
                    k = 2 * i + u
                    wait(dve, s.mid, k + 1)
                    dve.tensor_tensor(parts[u][2], tiles(b.rest[u][:, :]), parts[u][1], ALU.subtract).then_inc(s.low, 1)
            for u in range(2):
                measure(u, u, 0)
            for u in range(2):
                apply(u, u)
            turn_pairs(dve, turn)

        @block.scalar
        def _(act):
            def positive(k, u):
                wait(act, s.normed, CT * (k + 1))
                wait(act, s.hT_ps, k - 1)
                wait(act, s.h_kept, k - 1)
                act.activation(b.h[u][:, :], b.xn[u][:, :], ACT.Relu).then_inc(s.relued, 1)

            def move(k, u):
                wait(act, s.hT_ps, k + 1)
                wait(act, s.pq_ps, k - 1)
                wait(act, s.hT_kept, k - 1)
                act.activation(b.hT[u][:, :], hT_ps[:, 0:CW], ACT.Copy).then_inc(s.hT_moved, 1)

            def p_and_high(k, u, i):
                wait(act, s.pq_ps, k + 1)
                wait(act, s.p_out[u], 16 * i)
                act.activation(tiles(b.p[u][:, :]), tiles(pq_ps[u][:, 0:2 * CW], 2 * H)[:, :, 0:H], ACT.Copy).then_inc(s.p_moved, 1)
                wait(act, s.qs_out[u], 16 * i)
                act.activation(parts[u][0], q_ps[u], ACT.Copy).then_inc(s.high, 1)
                wait(act, s.p_moved, k + 1)
                act.dma_start(chunk_rows(d.p_table, k), tiles(b.p[u][:, :])).then_inc(s.p_out[u], 16)

            def store_parts(k, u):
                wait(act, s.low, k + 1)
                act.dma_start(chunk_rows(d.q_split, k), tiles(b.qs[u][:, :], 3 * H)).then_inc(s.qs_out[u], 16)

            def turn(i):
                k = 2 * i
                last = isinstance(i, int) and i == NC // 2 - 1
                if not (isinstance(i, int) and i == 0):
                    store_parts(k - 2, 0)
                    store_parts(k - 1, 1)
                for u in range(2):
                    p_and_high(k + u, u, i)
                    if not last:
                        positive(k + u + 2, u)
                if not last:
                    move(k + 2, 0)
                for u in range(2):
                    wait(act, s.rest, k + u + 1)
                    act.activation(parts[u][1], tiles(b.rest[u][:, :]), ACT.Copy).then_inc(s.mid, 1)
                if not last:
                    move(k + 3, 1)
            for u in range(2):
                positive(u, u)
            for u in range(2):
                move(u, u)
            turn_pairs(act, turn)
            store_parts(NC - 2, 0)
            store_parts(NC - 1, 1)

        @block.gpsimd
        def _(pool):
            def keep(k):
                for u in range(2):
                    wait(pool, s.relued, k + u + 1)
                    pool.tensor_tensor(tiles(cols(m.h, (k + u) * CW, CW)), tiles(b.h[u][:, :]),
                                       over_tiles(m.ub2_all[:, :], [P, CT, H]), ALU.add).then_inc(s.h_kept, 1)
                for u in range(2):
                    wait(pool, s.hT_moved, k + u + 1)
                    pool.tensor_copy(cols(m.hT, (k + u) * CW, CW), b.hT[u][:, :]).then_inc(s.hT_kept, 1)

            def turn(i):
                if not (isinstance(i, int) and i == NC // 2 - 1):
                    for u in range(2):
                        norm_root(pool, m, s, nb, 2 * i + u + 2, u)
                    keep(2 * i + 2)
            norm_root(pool, m, s, nb, 0, 0)
            norm_root(pool, m, s, nb, 1, 1)
            keep(0)
            turn_pairs(pool, turn)

        @block.tensor
        def _(pe):
            def transposes(k, u):
                wait(pe, s.relued, k + 1)
                wait(pe, s.hT_moved, k)
                for t in range(CT):
                    ins = pe.transpose(hT_ps[:, t * P:(t + 1) * P], b.h[u][:, t * H:(t + 1) * H], m.ident[:, :])
                ins.then_inc(s.hT_ps, 1)

            def turn(i):
                for u in range(2):
                    k = 2 * i + u
                    wait(pe, s.hT_moved, k + 1)
                    wait(pe, s.p_moved, k - 1)
                    wait(pe, s.rest, k - 1)
                    for t in range(CT):
                        out = pq_ps[u][:, t * 2 * H:(t + 1) * 2 * H]
                        pe.matmul(out, b.hT[u][:, t * P:(t + 1) * P], m.w1[:, 0:2 * H], start=True, stop=False)
                        ins = pe.matmul(out[:, H:], m.ones_three[:, :], m.b1_parts[:, :], start=False, stop=True)
                    ins.then_inc(s.pq_ps, 1)
                if not (isinstance(i, int) and i == NC // 2 - 1):
                    for u in range(2):
                        transposes(2 * i + u + 2, u)
            for u in range(2):
                transposes(u, u)
            turn_pairs(pe, turn)


def edges_one_fast(nc, d, m, ps, s, b):
    rel_ps = ps[:, 0, :]
    z_ps = [ps[:, 2, :], ps[:, 3, :]]
    src_ps = ps[:, 4, :]
    agg_ps = [ps[:, 5, 0:P], ps[:, 6, 0:P]]
    deg_ps = [ps[0:1, 1, 0:P], ps[0:1, 7, 0:P]]

    def sync(sp):
        def turn(i):
            for u in range(2):
                g = 2 * i + u
                wait(sp, s.z_ps, 2 * (g - 1))
                wait(sp, s.src_ps, 2 * (g - 1))
                sp.dma_start(b.rows3[u][:, :], rows(d.edge_rows, g, 1).rearrange("o r e -> (o r) e")).then_inc(s.rows_in[u], 16)
                sp.dma_start(b.attr[u][:, :], rows(d.attrT, g, 1).rearrange("o f e -> (o f) e")).then_inc(s.attr_in[u], 16)
                first = sp.value_load(cols(m.first_row, g, 1), min_val=0, max_val=N)
                sp.dma_start(b.window[u][:, :], rows(d.q_split, first, P)).then_inc(s.window_in[u], 16)
        turns(sp, G // 2, turn)

    def gpsimd(pool):
        def turn(i):
            for u in range(2):
                g = 2 * i + u
                pool.wait_ge(s.idx_ready, g + 1)
                wait(pool, s.z_ready, 2 * (g - 1))
                passed(pool, s.passed)
                for j in range(SUB):
                    pool.indirect_dma_start(b.gathered[u][:, j * H:(j + 1) * H], None, d.p_table[:, :],
                                            bass.IndirectOffsetOnAxis(ap=b.idx[u][:, j:j + 1], axis=0)).then_inc(s.gathered[u], 16)
        turns(pool, G // 2, turn)

    def tensor(pe):
        def broadcast(h, u, w, i):
            if w == 0:
                wait(pe, s.rows_in[u], 16 * (i + 1))
            wait(pe, s.oneT_ready, h)
            pe.matmul(rel_ps, m.pick[0:3, 2 * P:3 * P], b.rows3[u][:, w * HALF:(w + 1) * HALF], start=True, stop=True).then_inc(s.rel_ps, 1)
            wait(pe, s.counted, HS * h)
            pe.matmul(src_ps, m.pick[0:3, 3 * P:4 * P], b.rows3[u][:, w * HALF:(w + 1) * HALF], start=True, stop=True).then_inc(s.src_ps, 1)

        def sums(h, v, u, w, g):
            wait(pe, s.silu_ready, h + 1)
            wait(pe, s.one_ready, h + 1)
            if w == 0:
                wait(pe, s.agg_added, g - 1)
            for j in range(HS):
                pe.matmul(agg_ps[u], b.silu[v][:, j * H:(j + 1) * H], b.one[v][:, j * P:(j + 1) * P],
                          start=(w == 0 and j == 0), stop=(w == 1 and j == HS - 1))
            for j in range(HS):
                upper = b.one[v][:, j * P:(j + 1) * P].bitcast(BF16)[:, 1::2]
                ins = pe.matmul(deg_ps[u], m.ones_bf[:, :], upper, start=(w == 0 and j == 0), stop=(w == 1 and j == HS - 1))
            ins.then_inc(s.agg_ps, 1)

        def turn(i):
            for q in range(4):
                h, u, w, v = 4 * i + q, q // 2, q % 2, q % 2
                if not (isinstance(i, int) and h == NH - 1):
                    broadcast(h + 1, (q + 1) // 2 % 2, 1 - w, i + (q + 1) // 4)
                if w == 0:
                    wait(pe, s.attr_in[u], 16 * (i + 1))
                    wait(pe, s.window_in[u], 16 * (i + 1))
                wait(pe, s.oneT_ready, h + 1)
                wait(pe, s.z_ready, h - 1)
                for j in range(HS):
                    e = (w * HS + j) * P
                    z = z_ps[v][:, j * H:(j + 1) * H]
                    pe.matmul(z, b.attr[u][:, e:e + P], m.w1[:, 2 * H:3 * H], start=True, stop=False)
                    for part in range(3):
                        ins = pe.matmul(z, b.oneT[v][:, j * P:(j + 1) * P], b.window[u][:, part * H:(part + 1) * H], start=False, stop=(part == 2))
                ins.then_inc(s.z_ps, 1)
                if not (isinstance(i, int) and h == 0):
                    sums(h - 1, 1 - v, (q - 1) // 2 % 2, 1 - w, 2 * i + (q - 1) // 2)
        broadcast(0, 0, 0, 0)
        turns(pe, G // 2, turn)
        sums(NH - 1, 1, 1, 1, G - 1)

    def scalar(act):
        def turn(i):
            for q in range(4):
                h, v = 4 * i + q, q % 2
                wait(act, s.z_ready, h + 1)
                wait(act, s.agg_ps, h - 1)
                act.activation(b.silu[v][:, :], b.z[v][:, :], ACT.Silu).then_inc(s.silu_ready, 1)
        turns(act, G // 2, turn)

    def vector(dve):
        def place_indices(g, u):
            dve.tensor_copy(b.idx[u][:, :], cols(m.src_i, g * SUB, SUB)).then_inc(s.idx_ready, 1)

        def add_rows(h, v, u, w, i):
            wait(dve, s.z_ps, h + 1)
            if w == 0:
                wait(dve, s.gathered[u], 16 * SUB * (i + 1))
            wait(dve, s.silu_ready, h - 1)
            dve.tensor_tensor(b.z[v][:, :], z_ps[v], b.gathered[u][:, w * HS * H:(w + 1) * HS * H], ALU.add).then_inc(s.z_ready, 1)

        def add_sums(g, u):
            wait(dve, s.agg_ps, 2 * (g + 1))
            wait(dve, s.agg_added, g)
            wait(dve, s.deg_added, g)
            first = dve.value_load(cols(m.first_row, g, 1), min_val=0, max_val=N)
            dve.tensor_tensor(cols(m.degree, first, P), deg_ps[u], cols(m.degree, first, P), ALU.add).then_inc(s.deg_added, 1)
            wait(dve, s.deg_added, g + 1)
            dve.tensor_tensor(cols(m.aggT, first, P), agg_ps[u], cols(m.aggT, first, P), ALU.add).then_inc(s.agg_added, 1)

        def turn(i):
            for q in range(4):
                h, u, w, v = 4 * i + q, q // 2, q % 2, q % 2
                c = (2 * i + u) * SUB + w * HS
                wait(dve, s.rel_ps, h + 1)
                wait(dve, s.z_ps, h - 1)
                dve.tensor_scalar(b.oneT[v][:, :], rel_ps, m.iota_p[:, :], None, ALU.is_equal).then_inc(s.oneT_ready, 1)
                wait(dve, s.src_ps, h + 1)
                wait(dve, s.counted, HS * h)
                for j in range(HS):
                    dve.scalar_tensor_tensor(b.junk[:, j * P:(j + 1) * P], src_ps[:, j * P:(j + 1) * P], cols(m.src_c, c + j, 1),
                                             m.before[:, :], ALU.is_equal, ALU.mult, accum_out=cols(m.repeats, c + j, 1)).then_inc(s.counted, 1)
                wait(dve, s.agg_ps, h - 1)
                dve.tensor_tensor(tiles(b.one[v][:, :]), wide(cols(m.rel_c, c, HS), [P, HS, P]),
                                  over_tiles(m.iota_n[:, :], [P, HS, P]), ALU.is_equal).then_inc(s.one_ready, 1)
                if not (isinstance(i, int) and h == 0):
                    add_rows(h - 1, 1 - v, (q - 1) // 2 % 2, 1 - w, i + (q - 1) // 4)
                if w == 0 and not (isinstance(i, int) and (h == 0 or h == NH - 2)):
                    place_indices(2 * i + u + 1, 1 - u)
                if w == 1 and not (isinstance(i, int) and h == 1):
                    add_sums(2 * i + u - 1, 1 - u)
        place_indices(0, 0)
        place_indices(1, 1)
        turns(dve, G // 2, turn)
        add_rows(NH - 1, 1, 1, 1, G // 2 - 1)
        add_sums(G - 1, 1)
        again, away = m.rel_c[:, :], m.dst_c[:, :]
        step = Chain(dve, s.rows_chosen)
        dve.wait_ge(s.counted, HS * NH)
        dve.wait_ge(s.one_ready, NH)
        step.did(dve.tensor_scalar(again, m.repeats[:, :], 0.0, None, ALU.is_gt))
        step.then(dve.tensor_scalar(away, m.src_c[:, :], -1.0, m.dump[:, :], ALU.mult, ALU.add))
        step.then(dve.tensor_tensor(away, away, again, ALU.mult))
        step.then(dve.tensor_tensor(again, away, m.src_c[:, :], ALU.add))
        step.then(dve.tensor_copy(m.to_i[:, :], again))
    return sync, gpsimd, tensor, scalar, vector


TAIL = 9


def each_tile(eng, body):
    with eng.Fori(0, G) as g:
        with eng.Fori(0, SUB) as j:
            body(g * SUB + j, g, j)


def combine_indices(dve, m, s, b, own, t, key_c):
    dve.wait_ge(s.key_in, 16 * (t + 1))
    own.then(dve.tensor_copy(b.key_f[:, :], b.key_i[:, :]))
    own.then(dve.tensor_scalar(b.same[:, :], b.key_f[:, :], cols(key_c, t, 1), None, ALU.is_equal))
    own.then(dve.tensor_tensor(b.earlier[:, :], b.same[:, :], m.before[:, :], ALU.mult))
    own.then(dve.tensor_reduce(b.repeat[:, :], b.earlier[:, :], X, ALU.add))
    own.then(dve.tensor_scalar(b.again[:, :], b.repeat[:, :], 0.0, None, ALU.is_gt))
    own.then(dve.tensor_tensor(b.away[:, :], m.dump[:, :], cols(key_c, t, 1), ALU.subtract))
    own.then(dve.tensor_tensor(b.away[:, :], b.away[:, :], b.again[:, :], ALU.mult))
    own.then(dve.tensor_tensor(b.to_f[:, :], b.away[:, :], cols(key_c, t, 1), ALU.add))
    own.then(dve.tensor_copy(b.to_i[:, :], b.to_f[:, :]))


def join_three(dve, own, split, width, out):
    own.then(dve.tensor_tensor(out, split[:, 0:width], split[:, width:2 * width], ALU.add))
    own.then(dve.tensor_tensor(out, out, split[:, 2 * width:3 * width], ALU.add))


def scatter_tile(pool, s, b, t, acc):
    pool.wait_ge(s.sums_moved, t + 1)
    passed(pool, s.passed)
    pool.indirect_dma_start(acc[:, :], bass.IndirectOffsetOnAxis(ap=b.to_i[:, 0:1], axis=0), b.sums[:, :], None,
                            compute_op=ALU.add).then_inc(s.added, 16)
    pool.wait_ge(s.added, 16 * (t + 1))


def general_buffers(nc, ctx, phase):
    return buffers(nc, ctx, phase, src_x=([P, 1], I32), dst_x=([P, 1], I32), key_i=([P, P], I32), key_f=([P, P], F32),
                   same=([P, P], F32), earlier=([P, P], F32), repeat=([P, 1], F32), again=([P, 1], F32), away=([P, 1], F32),
                   to_f=([P, 1], F32), to_i=([P, 1], I32), vals=([P, AW], F32), sums=([P, AW], F32), at_src=([P, 3 * WW], BF16),
                   at_dst=([P, 3 * WW], BF16), p_src=([P, H], F32), src_row=([P, WW], F32), dst_row=([P, WW], F32), attr=([P, P], F32), z=([P, P], F32), score=([P, 1], F32), leaky=([P, 1], F32),
                   node_sums=([P, AW], F32))


GENERAL = "idx_ready rows_in key_in attr_in z_ps z_ready vals_ready own sums_ps sums_moved added node_in node_ps node_moved passed sp_passed"


def edges_one_general(nc, d, m, ps, s, b):
    acc = d.acc[NACC]
    STEPS = TAIL + 5

    def sync(sp):
        def tile(t, g, j):
            sp.dma_start(b.attr[:, :], d.attrT[bass.ds(g, 1), :, bass.ds(j * P, P)].rearrange("o f e -> (o f) e")).then_inc(s.attr_in, 16)
            sp.dma_start(b.key_i[:, :], rows(d.dst, t * P, P).partition_broadcast(P)).then_inc(s.key_in, 16)
            sp.wait_ge(s.added, 16 * (t + 1))
            passed(sp, s.sp_passed)
        each_tile(sp, tile)
        with sp.Fori(0, NT) as t:
            sp.dma_start(b.node_sums[:, :], rows(acc, t * P, P)).then_inc(s.node_in, 16)
            sp.wait_ge(s.node_moved, 2 * (t + 1))
            passed(sp, s.sp_passed)

    def gpsimd(pool):
        def tile(t, g, j):
            pool.tensor_copy(b.src_x[:, :], cols(m.src_i, t, 1)).then_inc(s.idx_ready, 1)
            pool.tensor_copy(b.dst_x[:, :], cols(m.dst_i, t, 1)).then_inc(s.idx_ready, 1)
            pool.wait_ge(s.idx_ready, 2 * (t + 1))
            passed(pool, s.passed)
            pool.indirect_dma_start(b.p_src[:, :], None, d.p_table[:, :], bass.IndirectOffsetOnAxis(ap=b.src_x[:, 0:1], axis=0)).then_inc(s.rows_in, 16)
            pool.indirect_dma_start(b.at_dst[:, 0:3 * H], None, d.q_split[:, :], bass.IndirectOffsetOnAxis(ap=b.dst_x[:, 0:1], axis=0)).then_inc(s.rows_in, 16)
            scatter_tile(pool, s, b, t, acc)
        each_tile(pool, tile)

    def tensor(pe):
        def tile(t, g, j):
            pe.wait_ge(s.attr_in, 16 * (t + 1))
            pe.matmul(ps[:, 0, 0:H], b.attr[:, :], m.w1[:, 2 * H:3 * H], start=True, stop=True).then_inc(s.z_ps, 1)
            pe.wait_ge(s.vals_ready, t + 1)
            pe.wait_ge(s.own, STEPS * (t + 1))
            pe.matmul(ps[:, 1, 0:AW], b.same[:, :], b.vals[:, :], start=True, stop=True).then_inc(s.sums_ps, 1)
            pe.wait_ge(s.added, 16 * (t + 1))
        each_tile(pe, tile)
        with pe.Fori(0, NT) as t:
            pe.wait_ge(s.node_in, 16 * (t + 1))
            pe.transpose(ps[:, 2, 0:P], b.node_sums[:, 0:H], m.ident[:, :])
            pe.transpose(ps[0:1, 3, 0:P], b.node_sums[:, H:AW], m.ident[:, :]).then_inc(s.node_ps, 1)
            pe.wait_ge(s.node_moved, 2 * (t + 1))

    def scalar(act):
        def tile(t, g, j):
            act.wait_ge(s.z_ready, t + 1)
            act.activation(b.vals[:, 0:H], b.z[:, :], ACT.Silu).then_inc(s.vals_ready, 1)
            act.wait_ge(s.added, 16 * (t + 1))
        each_tile(act, tile)

    def vector(dve):
        def tile(t, g, j):
            own = Chain(dve, s.own, STEPS * t)
            own.did(dve.memset(b.vals[:, H:AW], 1.0))
            dve.wait_ge(s.rows_in, 32 * (t + 1))
            join_three(dve, own, b.at_dst[:, :], H, b.z[:, :])
            own.then(dve.tensor_tensor(b.z[:, :], b.z[:, :], b.p_src[:, :], ALU.add))
            dve.wait_ge(s.z_ps, t + 1)
            dve.tensor_tensor(b.z[:, :], b.z[:, :], ps[:, 0, 0:H], ALU.add).then_inc(s.z_ready, 1)
            combine_indices(dve, m, s, b, own, t, m.dst_c)
            own.then(dve.memset(b.away[:, :], 0.0))
            dve.wait_ge(s.sums_ps, t + 1)
            dve.tensor_copy(b.sums[:, :], ps[:, 1, 0:AW]).then_inc(s.sums_moved, 1)
            dve.wait_ge(s.added, 16 * (t + 1))
        each_tile(dve, tile)
        with dve.Fori(0, NT) as t:
            dve.wait_ge(s.node_ps, t + 1)
            dve.tensor_copy(cols(m.aggT, t * P, P), ps[:, 2, 0:P]).then_inc(s.node_moved, 1)
            dve.tensor_copy(cols(m.degree, t * P, P), ps[0:1, 3, 0:P]).then_inc(s.node_moved, 1)
            dve.wait_ge(s.node_moved, 2 * (t + 1))
    return sync, gpsimd, tensor, scalar, vector


def edges_two_general(nc, d, m, ps, s, b):
    acc = d.acc[0]
    STEPS = TAIL + 6

    def sync(sp):
        def tile(t, g, j):
            sp.dma_start(b.key_i[:, :], rows(d.src, t * P, P).partition_broadcast(P)).then_inc(s.key_in, 16)
            sp.wait_ge(s.added, 16 * (t + 1))
            passed(sp, s.sp_passed)
        each_tile(sp, tile)

    def gpsimd(pool):
        def tile(t, g, j):
            pool.tensor_copy(b.src_x[:, :], cols(m.src_i, t, 1)).then_inc(s.idx_ready, 1)
            pool.tensor_copy(b.dst_x[:, :], cols(m.dst_i, t, 1)).then_inc(s.idx_ready, 1)
            pool.wait_ge(s.idx_ready, 2 * (t + 1))
            passed(pool, s.passed)
            pool.indirect_dma_start(b.at_src[:, :], None, d.w_split[:, :], bass.IndirectOffsetOnAxis(ap=b.src_x[:, 0:1], axis=0)).then_inc(s.rows_in, 16)
            pool.indirect_dma_start(b.at_dst[:, :], None, d.w_split[:, :], bass.IndirectOffsetOnAxis(ap=b.dst_x[:, 0:1], axis=0)).then_inc(s.rows_in, 16)
            scatter_tile(pool, s, b, t, acc)
        each_tile(pool, tile)

    def tensor(pe):
        def tile(t, g, j):
            pe.wait_ge(s.z_ready, t + 1)
            pe.matmul(ps[:, 1, 0:AW], b.same[:, :], b.vals[:, :], start=True, stop=True).then_inc(s.sums_ps, 1)
            pe.wait_ge(s.added, 16 * (t + 1))
        each_tile(pe, tile)

    def scalar(act):
        def tile(t, g, j):
            act.wait_ge(s.own, STEPS * t + 6)
            act.activation(b.vals[:, H:AW], b.leaky[:, :], ACT.Exp, scale=-1.0).then_inc(s.vals_ready, 1)
            act.wait_ge(s.added, 16 * (t + 1))
        each_tile(act, tile)

    def vector(dve):
        def tile(t, g, j):
            own = Chain(dve, s.own, STEPS * t)
            dve.wait_ge(s.rows_in, 32 * (t + 1))
            join_three(dve, own, b.at_dst[:, :], WW, b.dst_row[:, :])
            join_three(dve, own, b.at_src[:, :], WW, b.src_row[:, :])
            own.then(dve.tensor_tensor(b.score[:, :], b.dst_row[:, H:H + 1], b.src_row[:, H + 1:H + 2], ALU.add))
            own.then(dve.scalar_tensor_tensor(b.leaky[:, :], b.score[:, :], ALPHA, b.score[:, :], ALU.mult, ALU.max))
            combine_indices(dve, m, s, b, own, t, m.src_c)
            dve.wait_ge(s.vals_ready, t + 1)
            dve.tensor_scalar(b.vals[:, 0:H], b.dst_row[:, 0:H], b.vals[:, H:AW], None, ALU.mult).then_inc(s.z_ready, 1)
            dve.wait_ge(s.sums_ps, t + 1)
            dve.tensor_copy(b.sums[:, :], ps[:, 1, 0:AW]).then_inc(s.sums_moved, 1)
            dve.wait_ge(s.added, 16 * (t + 1))
        each_tile(dve, tile)
    return sync, gpsimd, tensor, scalar, vector


def branch(nc, m, fast, general):
    with nc.Block() as block:
        def both(n):
            def program(eng):
                fits = eng.value_load(m.fits[0:1, 0:1], min_val=0, max_val=1)
                with eng.If(fits == 1):
                    fast[n](eng)
                with eng.Else():
                    general[n](eng)
            return program
        block.sync(both(0))
        block.gpsimd(both(1))
        block.tensor(both(2))
        block.scalar(both(3))
        block.vector(both(4))


def edges_one(nc, d, m, ps):
    with ExitStack() as ctx:
        s = signals(nc, ctx, "e1", "rows_in*2 attr_in*2 window_in*2 idx_ready gathered*2 rel_ps src_ps z_ps agg_ps oneT_ready counted"
                    " one_ready z_ready silu_ready deg_added agg_added rows_chosen passed")
        b = buffers(nc, ctx, "e1", rows3=([3, GROUP], BF16, 2), attr=([P, GROUP], F32, 2), window=([P, 3 * H], BF16, 2),
                    gathered=([P, SUB * H], F32, 2), idx=([P, SUB], I32, 2), oneT=([P, HALF], BF16, 2), one=([P, HALF], F32, 2),
                    z=([P, HALF], F32, 2), silu=([P, HALF], F32, 2), junk=([P, HALF], F32))
        sg = signals(nc, ctx, "e1g", GENERAL)
        bg = general_buffers(nc, ctx, "e1g")
        branch(nc, m, edges_one_fast(nc, d, m, ps, s, b), edges_one_general(nc, d, m, ps, sg, bg))


def node_pass_two(nc, d, m, ps):
    with ExitStack() as ctx:
        s = signals(nc, ctx, "n2", "x_in*2 pre_ps mid_ready new_ps y_ready normed gammaed biased x1_ready x1_kept shifted relued"
                    " hT_ps hT_moved wh_ps high rest mid low score_kept ws_out*2 acc_zeroed")
        sa, sb = signals(nc, ctx, "n2a", NORM), signals(nc, ctx, "n2b", NORM)
        na, nb = norm_buffers(nc, ctx, "n2a"), norm_buffers(nc, ctx, "n2b")
        b = buffers(nc, ctx, "n2", x=([P, CW], F32, 2), mid=([P, CW], F32, 2), y=([P, CW], F32, 2),
                    xn=([P, CW], F32, 2), x1=([P, CW], F32, 2), shift=([P, CT], F32, 2), h=([P, CW], F32, 2), hT=([P, CW], F32, 2),
                    rest=([P, CT * WW], F32, 2), ws=([P, 3 * CT * WW], BF16, 2))
        bank2 = [ps[:, 2 * n:2 * n + 2, :].rearrange("p b c -> p (b c)") for n in range(4)]
        one_ps, two_ps = bank2[0:2], bank2[2:4]
        slices = [(512, CW - 512), (0, 512)]
        where = [(t // 3) * 512 + (t % 3) * WW for t in range(CT)]
        spans = [(0, 0, 3), (512, 3, 2)]

        def wh_view(u, bank, n):
            return tiles(one_ps[u][:, bank:bank + n * WW], WW)

        def rest_view(u, t, n):
            return tiles(b.rest[u][:, t * WW:(t + n) * WW], WW)

        def part_view(u, part, t, n):
            return tiles(b.ws[u][:, :], 3 * WW)[:, t:t + n, part * WW:(part + 1) * WW]
        block = ctx.enter_context(nc.Block())

        def from_chunk(k, first, steps):
            if not (isinstance(k, int) and k < first):
                steps()

        @block.sync
        def _(sp):
            def load(k, u):
                wait(sp, s.x1_ready, k - 1)
                sp.dma_start(tiles(b.x[u][:, :]), chunk_rows(d.x, k)).then_inc(s.x_in[u], 16)

            def store(k, u):
                wait(sp, s.low, 2 * (k + 1))
                sp.dma_start(chunk_rows(d.w_split, k), tiles(b.ws[u][:, :], 3 * WW)).then_inc(s.ws_out[u], 16)

            def turn(i):
                for acc in d.acc[:NACC]:
                    sp.dma_start(rows(acc, 2 * i * CW, 2 * CW).rearrange("(p r) c -> p r c", p=P),
                                 over_tiles(m.zeros[:, :], [P, 2 * CT, AW])).then_inc(s.acc_zeroed, 16)
                for u in range(2):
                    k = 2 * i + u
                    from_chunk(k, 2, lambda: store(k - 2, u))
                    if not (isinstance(i, int) and i == NC // 2 - 1):
                        load(k + 2, u)
            load(0, 0)
            load(1, 1)
            turn_pairs(sp, turn)
            store(NC - 2, 0)
            store(NC - 1, 1)
            sp.wait_ge(s.ws_out[0], 16 * (NC // 2))
            sp.wait_ge(s.ws_out[1], 16 * (NC // 2 + 1))
            sp.wait_ge(s.acc_zeroed, 16 * NACC * NC // 2)

        @block.tensor
        def _(pe):
            def hidden(k, u, part):
                c, n = slices[part]
                wait(pe, s.mid_ready, 2 * (k - 1))
                out = two_ps[u][:, c:c + n]
                pe.matmul(out, m.u1[:, 0:H], cols(m.hT, k * CW + c, n), start=True, stop=False)
                pe.matmul(out, m.w2u[:, :], cols(m.aggT, k * CW + c, n), start=False, stop=False)
                pe.matmul(out, m.b2u_row[:, :], cols(m.degree, k * CW + c, n), start=False, stop=True).then_inc(s.pre_ps, 1)

            def update(k, u):
                wait(pe, s.mid_ready, 2 * (k + 1))
                wait(pe, s.rest, 2 * (k - 1))
                wait(pe, s.score_kept, 2 * (k - 1))
                for t in range(CT):
                    ins = pe.matmul(one_ps[u][:, t * H:(t + 1) * H], b.mid[u][:, t * P:(t + 1) * P], m.u2[:, :], start=True, stop=True)
                ins.then_inc(s.new_ps, 1)

            def transposes(k, u):
                wait(pe, s.relued, CT * (k + 1))
                for t in range(CT):
                    ins = pe.transpose(one_ps[u][:, t * P:(t + 1) * P], b.h[u][:, t * H:(t + 1) * H], m.ident[:, :])
                ins.then_inc(s.hT_ps, 1)

            def project(k, u):
                wait(pe, s.hT_moved, k + 1)
                for t in range(CT):
                    ins = pe.matmul(one_ps[u][:, where[t]:where[t] + WW], b.hT[u][:, t * P:(t + 1) * P], m.l1wx[:, :], start=True, stop=True)
                ins.then_inc(s.wh_ps, 1)

            def turn(i):
                for u in range(2):
                    k = 2 * i + u
                    last = isinstance(k, int) and k == NC - 1
                    update(k, u)
                    from_chunk(k, 1, lambda: transposes(k - 1, 1 - u))
                    if not last:
                        hidden(k + 1, 1 - u, 0)
                    from_chunk(k, 1, lambda: project(k - 1, 1 - u))
                    if not last:
                        hidden(k + 1, 1 - u, 1)
            hidden(0, 0, 0)
            hidden(0, 0, 1)
            turn_pairs(pe, turn)
            transposes(NC - 1, 1)
            project(NC - 1, 1)

        @block.scalar
        def _(act):
            def hidden(k, u, part):
                c, n = slices[part]
                wait(act, s.pre_ps, 2 * k + part + 1)
                wait(act, s.new_ps, k - 1)
                act.activation(b.mid[u][:, c:c + n], two_ps[u][:, c:c + n], ACT.Silu, bias=m.ub1_col[:, :]).then_inc(s.mid_ready, 1)

            def move(k, u):
                wait(act, s.hT_ps, k + 1)
                wait(act, s.wh_ps, k)
                act.activation(b.hT[u][:, :], one_ps[u][:, 0:CW], ACT.Copy).then_inc(s.hT_moved, 1)

            def high(k, u):
                wait(act, s.wh_ps, k + 1)
                for bank, t, n in spans:
                    act.activation(part_view(u, 0, t, n), wh_view(u, bank, n), ACT.Copy).then_inc(s.high, 1)

            def middle(k, u):
                for n, (bank, t, count) in enumerate(spans):
                    wait(act, s.rest, 2 * k + n + 1)
                    act.activation(part_view(u, 1, t, count), rest_view(u, t, count), ACT.Copy).then_inc(s.mid, 1)

            def norm(k, u):
                wait(act, s.shifted, k + 1)
                wait(act, s.hT_ps, k - 1)
                for t in range(CT):
                    act.activation(b.h[u][:, t * H:(t + 1) * H], b.x1[u][:, t * H:(t + 1) * H], ACT.Relu,
                                   bias=b.shift[u][:, t:t + 1], scale=nb.inv[u][:, t:t + 1]).then_inc(s.relued, 1)

            def turn(i):
                for u in range(2):
                    k = 2 * i + u
                    last = isinstance(k, int) and k == NC - 1
                    from_chunk(k, 1, lambda: move(k - 1, 1 - u))
                    if not last:
                        hidden(k + 1, 1 - u, 0)
                    wait(act, s.ws_out[1 - u], 16 * i)
                    from_chunk(k, 1, lambda: high(k - 1, 1 - u))
                    if not last:
                        hidden(k + 1, 1 - u, 1)
                    from_chunk(k, 1, lambda: middle(k - 1, 1 - u))
                    norm(k, u)
            hidden(0, 0, 0)
            hidden(0, 0, 1)
            act.sem_inc(s.ws_out[1], 16)
            turn_pairs(act, turn)
            act.wait_ge(s.ws_out[1], 16 * (NC // 2))
            move(NC - 1, 1)
            high(NC - 1, 1)
            middle(NC - 1, 1)

        @block.gpsimd
        def _(pool):
            def bias(k, u, i):
                wait(pool, s.x_in[u], 16 * (i + 1))
                wait(pool, s.x1_ready, k - 1)
                pool.tensor_tensor(tiles(b.x[u][:, :]), tiles(b.x[u][:, :]), over_tiles(m.beta_all[:, :], [P, CT, H]), ALU.add).then_inc(s.biased, 1)

            def keep(k, u):
                wait(pool, s.pre_ps, 2 * (k + 1))
                wait(pool, s.x1_ready, k + 1)
                pool.tensor_copy(cols(m.aggT, k * CW, CW), b.x1[u][:, :]).then_inc(s.x1_kept, 1)

            def turn(i):
                for u in range(2):
                    k = 2 * i + u
                    norm_root(pool, m, sa, na, k, u)
                    from_chunk(k, 1, lambda: keep(k - 1, 1 - u))
                    norm_root(pool, m, sb, nb, k, u)
                    if not (isinstance(k, int) and k == NC - 1):
                        bias(k + 1, 1 - u, i + u)
            bias(0, 0, 0)
            turn_pairs(pool, turn)
            keep(NC - 1, 1)

        @block.vector
        def _(dve):
            def low(k, u):
                for n, (bank, t, count) in enumerate(spans):
                    wait(dve, s.mid, 2 * k + n + 1)
                    dve.tensor_tensor(part_view(u, 2, t, count), rest_view(u, t, count), part_view(u, 1, t, count), ALU.subtract).then_inc(s.low, 1)

            def rest(k, u):
                wait(dve, s.low, 2 * k)
                wait(dve, s.high, 2 * k + 2)
                for n, (bank, t, count) in enumerate(spans):
                    dve.tensor_tensor(rest_view(u, t, count), wh_view(u, bank, count), part_view(u, 0, t, count), ALU.subtract).then_inc(s.rest, 1)
                    dve.tensor_copy(cols(m.s_src, k * CT + t, count), wh_view(u, bank, count)[:, :, WW - 1]).then_inc(s.score_kept, 1)

            def turn(i):
                for u in range(2):
                    k = 2 * i + u
                    wait(dve, s.new_ps, k + 1)
                    wait(dve, s.normed, CT * (k - 1))
                    dve.tensor_tensor(b.y[u][:, :], one_ps[u][:, 0:CW], cols(m.h, k * CW, CW), ALU.add).then_inc(s.y_ready, 1)
                    wait(dve, s.y_ready, k + 1)
                    norm_measure(dve, sa, na, k, u, b.y[u][:, :])
                    wait(dve, s.x1_ready, k - 1)
                    norm_apply(dve, sa, na, k, u, b.y[u][:, :], b.xn[u][:, :], s.normed)
                    wait(dve, s.normed, CT * (k + 1))
                    xn = b.xn[u][:, :]
                    dve.tensor_tensor(tiles(xn), tiles(xn), over_tiles(m.gamma_all[:, :], [P, CT, H]), ALU.mult).then_inc(s.gammaed, 1)
                    wait(dve, s.gammaed, k + 1)
                    wait(dve, s.biased, k + 1)
                    wait(dve, s.x1_kept, k - 1)
                    wait(dve, s.relued, CT * (k - 1))
                    dve.tensor_tensor(b.x1[u][:, :], xn, b.x[u][:, :], ALU.add).then_inc(s.x1_ready, 1)
                    from_chunk(k, 1, lambda: rest(k - 1, 1 - u))
                    wait(dve, s.x1_ready, k + 1)
                    norm_measure(dve, sb, nb, k, u, b.x1[u][:, :])
                    from_chunk(k, 1, lambda: low(k - 1, 1 - u))
                    wait(dve, sb.rooted, k + 1)
                    dve.scalar_tensor_tensor(b.shift[u][:, :], tiles(nb.mv[u][:, :], 2)[:, :, 0], -1.0, nb.inv[u][:, :],
                                             ALU.mult, ALU.mult).then_inc(s.shifted, 1)
            turn_pairs(dve, turn)
            rest(NC - 1, 1)
            low(NC - 1, 1)


def edges_two_fast(nc, d, m, ps, s, b):
    rel_ps, lo_ps, src_ps, score_ps = ps[:, 0, :], ps[:, 1, :], ps[:, 2, :], ps[:, 3, 0:HS * NT]
    s_dst_ps = ps[:, 3, HS * NT:HS * NT + HS * 3]
    wh_ps = [ps[:, 4, :], ps[:, 5, :]]
    sums_ps = ps[:, 6:8, 0:2 * AW]

    def sync(sp):
        def turn(i):
            for u in range(2):
                g = 2 * i + u
                wait(sp, s.wh_ps, 2 * (g - 1))
                wait(sp, s.src_ps, 2 * (g - 1))
                sp.dma_start(b.rows3[u][:, :], rows(d.edge_rows, g, 1).rearrange("o r e -> (o r) e")).then_inc(s.rows_in[u], 16)
                first = sp.value_load(cols(m.first_row, g, 1), min_val=0, max_val=N)
                sp.dma_start(b.window[u][:, :], rows(d.w_split, first, P)).then_inc(s.window_in[u], 16)
        turns(sp, G // 2, turn)

    def gpsimd(pool):
        def turn(i):
            for u in range(2):
                g = 2 * i + u
                pool.wait_ge(s.idx_ready, g + 1)
                for j in range(SUB):
                    w, a = j // HS, j % HS
                    h = 2 * g + w
                    if a == 0:
                        pool.wait_ge(s.sums_moved, h + 1)
                    wait(pool, s.added[a], 16 * h)
                    passed(pool, s.passed)
                    pool.indirect_dma_start(d.acc[a][:, :], bass.IndirectOffsetOnAxis(ap=b.idx[u][:, j:j + 1], axis=0),
                                            b.sums[w][:, a * AW:(a + 1) * AW], None, compute_op=ALU.add).then_inc(s.added[a], 16)
        turns(pool, G // 2, turn)
        for a in range(NACC):
            pool.wait_ge(s.added[a], 16 * NH)

    def tensor(pe):
        def broadcast(h, u, w, i):
            if w == 0:
                wait(pe, s.rows_in[u], 16 * (i + 1))
            half = b.rows3[u][:, w * HALF:(w + 1) * HALF]
            wait(pe, s.oneT_ready, h)
            pe.matmul(rel_ps, m.pick[0:3, 2 * P:3 * P], half, start=True, stop=True).then_inc(s.rel_ps, 1)
            wait(pe, s.loT_ready, h)
            pe.matmul(lo_ps, m.pick[0:3, P:2 * P], half, start=True, stop=True).then_inc(s.lo_ps, 1)
            wait(pe, s.same_ready, h)
            pe.matmul(src_ps, m.pick[0:3, 3 * P:4 * P], half, start=True, stop=True).then_inc(s.src_ps, 1)

        def combine(h, v):
            wait(pe, s.same_ready, h + 1)
            wait(pe, s.vals_ready, h + 1)
            wait(pe, s.sums_moved, h)
            for j in range(HS):
                ins = pe.matmul(sums_ps[:, j // 2, (j % 2) * AW:(j % 2 + 1) * AW], b.same[v][:, j * P:(j + 1) * P],
                                b.vals[v][:, j * AW:(j + 1) * AW], start=True, stop=True)
            ins.then_inc(s.sums_ps, 1)

        def turn(i):
            for q in range(4):
                h, u, w, v = 4 * i + q, q // 2, q % 2, q % 2
                if not (isinstance(i, int) and h == NH - 1):
                    broadcast(h + 1, (q + 1) // 2 % 2, 1 - w, i + (q + 1) // 4)
                if w == 0:
                    wait(pe, s.window_in[u], 16 * (i + 1))
                wait(pe, s.oneT_ready, h + 1)
                wait(pe, s.loT_ready, h + 1)
                wait(pe, s.scored, 2 * h)
                for j in range(HS):
                    for part in range(3):
                        pe.matmul(score_ps[:, j * NT:(j + 1) * NT], b.loT[v][:, j * P:(j + 1) * P],
                                  b.s_src[:, part * NT:(part + 1) * NT], start=(part == 0), stop=(part == 2))
                s_dst = tiles(b.window[u][:, :], WW)[:, :, H]
                for j in range(HS):
                    ins = pe.matmul(s_dst_ps[:, j * 3:(j + 1) * 3], b.oneT[v][:, j * P:(j + 1) * P], s_dst, start=True, stop=True)
                ins.then_inc(s.score_ps, 1)
                wait(pe, s.vals_ready, h - 1)
                for j in range(HS):
                    for part in range(3):
                        ins = pe.matmul(wh_ps[v][:, j * H:(j + 1) * H], b.oneT[v][:, j * P:(j + 1) * P],
                                        b.window[u][:, part * WW:part * WW + H], start=(part == 0), stop=(part == 2))
                ins.then_inc(s.wh_ps, 1)
                if not (isinstance(i, int) and h == 0):
                    combine(h - 1, 1 - v)
        broadcast(0, 0, 0, 0)
        wait(pe, s.table_split, 5)
        turns(pe, G // 2, turn)
        combine(NH - 1, 1)

    def scalar(act):
        def place_indices(g, u):
            act.activation(b.idx[u][:, :], cols(m.to_i, g * SUB, SUB), ACT.Copy).then_inc(s.idx_ready, 1)

        def move_sums(h, v):
            wait(act, s.sums_ps, h + 1)
            for a in range(NACC):
                wait(act, s.added[a], 16 * (h - 1))
            act.activation(b.sums[v][:, :].rearrange("p (b c) -> p b c", b=2), sums_ps, ACT.Copy).then_inc(s.sums_moved, 1)

        def turn(i):
            for q in range(4):
                h, v = 4 * i + q, q % 2
                wait(act, s.scored, 2 * (h + 1))
                wait(act, s.vals_ready, h - 1)
                act.activation(b.weight[v][:, :], b.leaky[v][:, :], ACT.Exp, scale=-1.0).then_inc(s.weighed, 1)
                wait(act, s.weighed, h + 1)
                wait(act, s.wh_ps, h + 1)
                wait(act, s.sums_ps, h - 1)
                for j in range(HS):
                    act.activation(b.vals[v][:, j * AW:j * AW + H], wh_ps[v][:, j * H:(j + 1) * H], ACT.Copy,
                                   scale=b.weight[v][:, j:j + 1]).then_inc(s.val_parts, 1)
                act.activation(tiles(b.vals[v][:, :], AW)[:, :, H], b.weight[v][:, :], ACT.Copy).then_inc(s.val_parts, 1)
                wait(act, s.val_parts, (HS + 1) * (h + 1))
                act.nop().then_inc(s.vals_ready, 1)
                if not (isinstance(i, int) and h == 0):
                    move_sums(h - 1, 1 - v)
                if q % 2 == 0 and not (isinstance(i, int) and h < 4):
                    place_indices(2 * i + q // 2, q // 2)
        place_indices(0, 0)
        place_indices(1, 1)
        turns(act, G // 2, turn)
        move_sums(NH - 1, 1)

    def vector(dve):
        def one_hots(h, v):
            wait(dve, s.rel_ps, h + 1)
            wait(dve, s.wh_ps, h - 1)
            dve.tensor_scalar(b.oneT[v][:, :], rel_ps, m.iota_p[:, :], None, ALU.is_equal).then_inc(s.oneT_ready, 1)
            wait(dve, s.lo_ps, h + 1)
            dve.tensor_scalar(b.loT[v][:, :], lo_ps, m.iota_p[:, :], None, ALU.is_equal).then_inc(s.loT_ready, 1)

        def find_same(h, v, c):
            wait(dve, s.src_ps, h + 1)
            wait(dve, s.sums_ps, h - 1)
            dve.tensor_tensor(tiles(b.same[v][:, :]), tiles(src_ps), wide(cols(m.src_c, c, HS), [P, HS, P]),
                              ALU.is_equal).then_inc(s.same_ready, 1)

        def pick_scores(h, v, c):
            wait(dve, s.score_ps, h + 1)
            wait(dve, s.picked, (HS + 1) * h)
            wait(dve, s.scored, 2 * h)
            dve.tensor_reduce(b.s_dst[:, :], tiles(s_dst_ps, 3), X, ALU.add).then_inc(s.picked, 1)
            for j in range(HS):
                dve.scalar_tensor_tensor(b.junk[:, j * NT:(j + 1) * NT], m.iota_n[:, 0:NT], cols(m.hi_c, c + j, 1),
                                         score_ps[:, j * NT:(j + 1) * NT], ALU.is_equal, ALU.mult,
                                         accum_out=b.score[v][:, j:j + 1]).then_inc(s.picked, 1)
            wait(dve, s.picked, (HS + 1) * (h + 1))
            dve.tensor_tensor(b.score[v][:, :], b.score[v][:, :], b.s_dst[:, :], ALU.add).then_inc(s.scored, 1)
            wait(dve, s.scored, 2 * h + 1)
            wait(dve, s.weighed, h - 1)
            dve.scalar_tensor_tensor(b.leaky[v][:, :], b.score[v][:, :], ALPHA, b.score[v][:, :], ALU.mult, ALU.max).then_inc(s.scored, 1)

        def turn(i):
            for q in range(4):
                h, v = 4 * i + q, q % 2
                last = isinstance(i, int) and h == NH - 1
                if not last:
                    one_hots(h + 1, 1 - v)
                pick_scores(h, v, h * HS)
                if not last:
                    find_same(h + 1, 1 - v, (h + 1) * HS)
        split = Chain(dve, s.table_split)
        split.then(dve.tensor_copy(b.s_src[:, 0:NT], m.s_src[:, :]))
        split.then(dve.tensor_tensor(b.rest[:, :], m.s_src[:, :], b.s_src[:, 0:NT], ALU.subtract))
        split.then(dve.tensor_copy(b.s_src[:, NT:2 * NT], b.rest[:, :]))
        split.then(dve.tensor_tensor(b.rest[:, :], b.rest[:, :], b.s_src[:, NT:2 * NT], ALU.subtract))
        split.did(dve.tensor_copy(b.s_src[:, 2 * NT:], b.rest[:, :]))
        one_hots(0, 0)
        find_same(0, 0, 0)
        turns(dve, G // 2, turn)
    return sync, gpsimd, tensor, scalar, vector


def edges_two(nc, d, m, ps):
    with ExitStack() as ctx:
        s = signals(nc, ctx, "e2", "rows_in*2 window_in*2 idx_ready added*4 rel_ps lo_ps src_ps score_ps wh_ps sums_ps oneT_ready loT_ready"
                    " same_ready picked scored weighed val_parts vals_ready sums_moved table_split passed")
        b = buffers(nc, ctx, "e2", rows3=([3, GROUP], BF16, 2), window=([P, 3 * WW], BF16, 2), idx=([P, SUB], I32, 2),
                    oneT=([P, HALF], BF16, 2), loT=([P, HALF], BF16, 2), s_src=([P, 3 * NT], BF16), rest=([P, NT], F32), s_dst=([P, HS], F32), same=([P, HALF], F32, 2), junk=([P, HS * NT], F32),
                    score=([P, HS], F32, 2), leaky=([P, HS], F32, 2), weight=([P, HS], F32, 2), vals=([P, HS * AW], F32, 2),
                    sums=([P, HS * AW], F32, 2))
        sg = signals(nc, ctx, "e2g", GENERAL)
        bg = general_buffers(nc, ctx, "e2g")
        branch(nc, m, edges_two_fast(nc, d, m, ps, s, b), edges_two_general(nc, d, m, ps, sg, bg))


def node_pass_three(nc, d, m):
    with ExitStack() as ctx:
        s = signals(nc, ctx, "n3", "acc_in*2 added01 added23 summed totalled inverted divided below powered above out_ready out_done*2")
        b = buffers(nc, ctx, "n3", acc=([P, NACC * CT * AW], F32, 2), one=([P, CT * AW], F32, 2), two=([P, CT * AW], F32, 2),
                    sums=([P, CT * AW], F32, 2), inv=([P, CT], F32, 2), total=([P, CT], F32, 2), mean=([P, CW], F32, 2), below=([P, CW], F32, 2),
                    power=([P, CW], F32, 2), out=([P, CW], F32, 2))
        block = ctx.enter_context(nc.Block())
        W = CT * AW

        @block.sync
        def _(sp):
            def load(k, u):
                wait(sp, s.added01, k - 1)
                wait(sp, s.added23, k - 1)
                for a in range(NACC):
                    sp.dma_start(tiles(b.acc[u][:, a * W:(a + 1) * W], AW), chunk_rows(d.acc[a], k)).then_inc(s.acc_in[u], 16)

            def turn(i):
                for u in range(2):
                    k = 2 * i + u
                    if not (isinstance(i, int) and i == NC // 2 - 1):
                        load(k + 2, u)
                    if not (isinstance(i, int) and k == 0):
                        store(k - 1, 1 - u)

            def store(k, u):
                wait(sp, s.out_ready, k + 1)
                sp.dma_start(chunk_rows(d.out, k), tiles(b.out[u][:, :])).then_inc(s.out_done[u], 16)
            load(0, 0)
            load(1, 1)
            turn_pairs(sp, turn)
            k, u = NC - 1, 1
            full, left = divmod(N - k * CW, P)
            sp.wait_ge(s.out_ready, NC)
            sp.dma_start(d.out[k * CW:k * CW + full * P].rearrange("(t p) f -> p t f", p=P),
                         tiles(b.out[u][:, 0:full * H])).then_inc(s.out_done[u], 16)
            sp.dma_start(d.out[k * CW + full * P:N], b.out[u][0:left, full * H:(full + 1) * H]).then_inc(s.out_done[u], 16)
            sp.wait_ge(s.out_done[0], 16 * (NC // 2))
            sp.wait_ge(s.out_done[1], 16 * (NC // 2 + 2))

        @block.gpsimd
        def _(pool):
            def turn(i):
                for u in range(2):
                    k = 2 * i + u
                    wait(pool, s.acc_in[u], 16 * NACC * (i + 1))
                    wait(pool, s.summed, k - 1)
                    pool.tensor_tensor(b.two[u][:, :], b.acc[u][:, 2 * W:3 * W], b.acc[u][:, 3 * W:], ALU.add).then_inc(s.added23, 1)
            turn_pairs(pool, turn)

        @block.vector
        def _(dve):
            def divide(k, u, i):
                wait(dve, s.acc_in[u], 16 * NACC * (i + 1))
                wait(dve, s.summed, k - 1)
                dve.tensor_tensor(b.one[u][:, :], b.acc[u][:, 0:W], b.acc[u][:, W:2 * W], ALU.add).then_inc(s.added01, 1)
                wait(dve, s.added01, k + 1)
                wait(dve, s.added23, k + 1)
                wait(dve, s.divided, k - 1)
                dve.tensor_tensor(b.sums[u][:, :], b.one[u][:, :], b.two[u][:, :], ALU.add).then_inc(s.summed, 1)
                wait(dve, s.summed, k + 1)
                wait(dve, s.inverted, k - 1)
                dve.tensor_tensor(b.total[u][:, :], tiles(b.sums[u][:, :], AW)[:, :, H], cols(m.no_node, k * CT, CT), ALU.add).then_inc(s.totalled, 1)
                wait(dve, s.totalled, k + 1)
                dve.reciprocal(b.inv[u][:, :], b.total[u][:, :]).then_inc(s.inverted, 1)
                wait(dve, s.inverted, k + 1)
                wait(dve, s.above, k - 1)
                wait(dve, s.below, k - 1)
                dve.tensor_tensor(tiles(b.mean[u][:, :]), tiles(b.sums[u][:, :], AW)[:, :, 0:H],
                                  wide(b.inv[u][:, :], [P, CT, H]), ALU.mult).then_inc(s.divided, 1)

            def finish(k, u, stores):
                wait(dve, s.powered, k + 1)
                wait(dve, s.out_done[u], 16 * stores)
                dve.scalar_tensor_tensor(b.out[u][:, :], b.mean[u][:, :], 0.0, b.power[u][:, :], ALU.max, ALU.add).then_inc(s.above, 1)
                wait(dve, s.above, k + 1)
                dve.scalar_tensor_tensor(b.out[u][:, :], b.out[u][:, :], -1.0, cols(m.aggT, k * CW, CW), ALU.add, ALU.add).then_inc(s.out_ready, 1)

            def turn(i):
                divide(2 * i, 0, i)
                if not (isinstance(i, int) and i == 0):
                    finish(2 * i - 1, 1, i)
                divide(2 * i + 1, 1, i)
                finish(2 * i, 0, i)
            dve.sem_inc(s.out_done[1], 16)
            turn_pairs(dve, turn)
            finish(NC - 1, 1, NC // 2)

        @block.scalar
        def _(act):
            def turn(i):
                for u in range(2):
                    k = 2 * i + u
                    wait(act, s.divided, k + 1)
                    wait(act, s.powered, k - 1)
                    act.activation(b.below[u][:, :], b.mean[u][:, :], ACT.Relu, scale=-1.0).then_inc(s.below, 1)
                    wait(act, s.below, k + 1)
                    wait(act, s.above, k - 1)
                    act.activation(b.power[u][:, :], b.below[u][:, :], ACT.Exp, scale=-1.0).then_inc(s.powered, 1)
            turn_pairs(act, turn)


def program(nc, given):
    tables = {}
    for name, shape, dtype in (("p_table", [ROWS, H], F32), ("q_split", [ROWS, 3 * H], BF16),
                               ("w_split", [ROWS, 3 * WW], BF16), ("edge_rows", [G, 3, GROUP], BF16)):
        tables[name] = nc.dram_tensor(name, shape, dtype, kind="Internal").ap()
    tables["acc"] = [nc.dram_tensor(f"acc{a}", [ROWS, AW], F32, kind="Internal").ap() for a in range(NACC + 1)]
    d = named("Dram", {**given, **tables})
    with ExitStack() as ctx:
        ps = ctx.enter_context(nc.psum_tensor("ps", [P, 8, 512], F32))
        m = buffers(nc, ctx, "all", h=([P, ROWS], F32), hT=([P, ROWS], F32), aggT=([P, ROWS], F32), degree=([1, ROWS], F32),
                    w1=([P, 3 * H], F32), w2u=([P, H], F32), u1=([P, 2 * H], F32), u2=([P, H], F32), l1wx=([P, WW], F32),
                    b1_parts=([3, H], BF16), ones_three=([3, P], BF16), minus_half=([P, CT], F32), gamma_all=([P, H], F32), beta_all=([P, H], F32), ub1_col=([P, 1], F32),
                    b2u_row=([1, H], F32), ub2_all=([P, H], F32), ones_row=([1, P], F32), ones_bf=([P, 1], BF16), zeros=([P, AW], F32),
                    iota_n=([P, P], F32), iota_p=([P, 1], F32), before=([P, P], F32), ident=([P, P], F32), dump=([P, 1], F32),
                    pick=([3, 4 * P], BF16), first_row=([1, G], I32), fits=([1, 1], I32), src_c=([P, G * SUB], F32),
                    hi_c=([P, G * SUB], F32), dst_c=([P, G * SUB], F32), rel_c=([P, G * SUB], F32), src_i=([P, G * SUB], I32),
                    dst_i=([P, G * SUB], I32), repeats=([P, G * SUB], F32), to_i=([P, G * SUB], I32), s_src=([P, NT], F32), no_node=([P, NT], F32))
        prepare(nc, d, m, ps)
        node_pass_one(nc, d, m, ps)
        edges_one(nc, d, m, ps)
        node_pass_two(nc, d, m, ps)
        edges_two(nc, d, m, ps)
        node_pass_three(nc, d, m)


def kernel(**inputs):
    import numpy as np
    import concourse.bacc as bacc
    from concourse.bass_utils import run_bass_kernel_spmd

    x = np.zeros((ROWS, H), np.float32)
    x[:N] = inputs["x"]
    attr = np.zeros((G * GROUP, H), np.float32)
    attr[:E] = inputs["edge_attr_128"]
    ends = {}
    for name in ("src", "dst"):
        ends[name] = np.full(G * GROUP, N, np.int32)
        ends[name][:E] = inputs[name]
    arrays = {
        "x": x, "src": ends["src"], "dst": ends["dst"],
        "attrT": np.ascontiguousarray(attr.reshape(G, GROUP, H).transpose(0, 2, 1)),
        "w1": inputs["L0_gnn_msg_W1"], "b1": inputs["L0_gnn_msg_b1"], "w2": inputs["L0_gnn_msg_W2"], "b2": inputs["L0_gnn_msg_b2"],
        "u1": inputs["L0_gnn_upd_W1"], "ub1": inputs["L0_gnn_upd_b1"], "u2": inputs["L0_gnn_upd_W2"], "ub2": inputs["L0_gnn_upd_b2"],
        "gamma": inputs["L0_gnn_ln_gamma"], "beta": inputs["L0_gnn_ln_beta"], "l1w": inputs["L1_gnn_W"], "a": inputs["L1_gnn_a"],
    }
    arrays = {name: np.ascontiguousarray(a) for name, a in arrays.items()}
    nc = bacc.Bacc("TRN2", target_bir_lowering=False, num_devices=1)
    d = {name: nc.dram_tensor(f"in_{name}", a.shape, mybir.dt.from_np(a.dtype), kind="ExternalInput").ap()
         for name, a in arrays.items()}
    d["out"] = nc.dram_tensor("out", (N, H), F32, kind="ExternalOutput").ap()
    program(nc, d)
    return run_bass_kernel_spmd(nc, [{f"in_{name}": a for name, a in arrays.items()}], core_ids=[0]).results[0]["out"]
```
